# Optimizing a Trainium2 kernel written in Bass

```python
import numpy as np
import jax
import jax.numpy as jnp

def _softmax(x, axis=-1):
    return jax.nn.softmax(x, axis=axis)

def _gelu(x):
    return jax.nn.gelu(x, approximate=True)

def _silu(x):
    return jax.nn.silu(x)

def _sigmoid(x):
    return jax.nn.sigmoid(x)

def _layernorm(x, axis=-1, eps=1e-05):
    m = jnp.mean(x, axis=axis, keepdims=True)
    v = jnp.var(x, axis=axis, keepdims=True)
    return (x - m) / jnp.sqrt(v + eps)

def _scatter_add(tgt, idx, src, axis=0):
    return tgt.at[idx].add(src)

def _segment_sum(src, seg, n):
    return jax.ops.segment_sum(src, seg, n)
kernel_name = 'mk_gnn_resnorm_d2_gnn_r32_54d490'

def setup_inputs(seed: int=0):
    np.random.seed(seed)
    _w = jnp.asarray

    def _rec_inputs():
        import jax
        import jax.numpy as jnp
        _gk = jax.random.key(seed)
        x = -0.0005121 + 1.001 * jax.random.normal(jax.random.fold_in(_gk, 1), (50000, 160), jnp.float32)
        src = jax.random.randint(jax.random.fold_in(_gk, 2), (25000,), 0, 50000, jnp.int32)
        dst = jnp.minimum((50000 * jax.random.uniform(jax.random.fold_in(_gk, 3), (25000,)) ** 2.0).astype(jnp.int32), 49999)
        _o = jnp.argsort(dst, stable=True)
        src = src[_o]
        dst = dst[_o]
        edge_attr_16 = jax.random.uniform(jax.random.fold_in(_gk, 11), (25000, 16), jnp.float32, 0.0, 1)
        edge_attr_4 = 0.000898722 + 1.00012 * jax.random.normal(jax.random.fold_in(_gk, 12), (25000, 4), jnp.float32)
        edge_attr_8 = jax.random.uniform(jax.random.fold_in(_gk, 13), (25000, 8), jnp.float32, 0.0, 1)
        return (x, src, dst, edge_attr_16, edge_attr_4, edge_attr_8)
    x, src, dst, edge_attr_16, edge_attr_4, edge_attr_8 = _rec_inputs()

    def _L0_gnn_setup():
        import jax, jax.numpy as jnp
        import numpy as np
        N, E = (625, 10000)
        CS, CV = (64, 32)
        AS_, AV, H = (16, 8, 4)
        NB = 16
        SQRT3 = 1.7320508075688772
        SQRT2 = 1.4142135623730951
        EPS = 1e-05

        def _cg_tp(s, v, y0, y1, w_ss, w_sv, w_vs, w_vv0, w_vv1):
            out_s = jnp.concatenate([w_ss * s * y0[:, None], w_vv0 * (jnp.einsum('eci,ei->ec', v, y1) / SQRT3)], axis=-1)
            out_v = jnp.concatenate([(w_sv * s)[:, :, None] * y1[:, None, :], (w_vs * jnp.ones_like(v[..., 0]))[..., None] * v * y0[:, None, None], (w_vv1 * jnp.ones_like(v[..., 0]))[..., None] * (jnp.cross(v, y1[:, None, :]) / SQRT2)], axis=1)
            return (out_s, out_v)

        def _equiv_layernorm(s, v, gamma_s, beta_s, gamma_v):
            mu = jnp.mean(s, axis=-1, keepdims=True)
            var = jnp.var(s, axis=-1, keepdims=True)
            s_n = (s - mu) * jax.lax.rsqrt(var + EPS) * gamma_s + beta_s
            rms = jnp.sqrt(jnp.mean(jnp.sum(v * v, axis=-1), axis=-1, keepdims=True) + EPS)
            v_n = v / rms[..., None] * gamma_v[None, :, None]
            return (s_n, v_n)
        key = jax.random.key(seed)
        ks = jax.random.split(key, 26)

        def rn(k, shape, fan):
            return jax.random.normal(k, shape, jnp.float32) / np.sqrt(fan)
        D1S, D1V = (CS + CV, CS + 2 * CV)
        WN = 2 * CS + 3 * CV
        inp = {'node': jax.random.normal(ks[0], (N, CS + 3 * CV), jnp.float32), 'edge_index': jax.random.randint(ks[1], (2, E), 0, N, jnp.int64 if jax.config.jax_enable_x64 else jnp.int32), 'rbf': jax.random.uniform(ks[2], (E, NB), jnp.float32), 'rsh': jax.random.normal(ks[3], (E, 4), jnp.float32), 'gamma_s': jnp.ones((CS,), jnp.float32), 'beta_s': jnp.zeros((CS,), jnp.float32), 'gamma_v': jnp.ones((CV,), jnp.float32), 'Ws_src': rn(ks[4], (CS, CS), CS), 'Wv_src': rn(ks[5], (CV, CV), CV), 'Ws_dst': rn(ks[6], (CS, CS), CS), 'Wv_dst': rn(ks[7], (CV, CV), CV), 'W_rbf': rn(ks[8], (NB, WN), NB), 'W_alpha': rn(ks[9], (D1S, H * AS_), D1S), 'alpha_dot': rn(ks[10], (1, H, AS_), AS_), 'Ws_val': rn(ks[11], (D1S, CS), D1S), 'Wv_val': rn(ks[12], (D1V, CV), D1V), 'Wg': rn(ks[13], (CS, CV), CS), 'w2_ss': rn(ks[14], (CS,), 1), 'w2_sv': rn(ks[15], (CS,), 1), 'w2_vs': rn(ks[16], (CV,), 1), 'w2_vv0': rn(ks[17], (CV,), 1), 'w2_vv1': rn(ks[18], (CV,), 1), 'Ws_vlin': rn(ks[19], (D1S, H * AS_), D1S), 'Wv_vlin': rn(ks[20], (D1V, H * AV), D1V), 'Wps': rn(ks[21], (H * AS_, CS), H * AS_), 'Wpv': rn(ks[22], (H * AV, CV), H * AV)}
        return inp
    _L0_gnn_all = _L0_gnn_setup()
    _L0_gnn_in = {k: v for k, v in _L0_gnn_all.items() if k in ('gamma_s', 'beta_s', 'gamma_v', 'Ws_src', 'Wv_src', 'Ws_dst', 'Wv_dst', 'W_rbf', 'W_alpha', 'alpha_dot', 'Ws_val', 'Wv_val', 'Wg', 'w2_ss', 'w2_sv', 'w2_vs', 'w2_vv0', 'w2_vv1', 'Ws_vlin', 'Wv_vlin', 'Wps', 'Wpv')}
    del _L0_gnn_all

    def _L1_gnn_setup():
        import jax, jax.numpy as jnp
        import numpy as np
        N = 50000
        E = 25000
        MUL0 = 64
        MUL1 = 32
        NB = 8
        HID = 64
        WNUM = MUL0 + MUL0 + MUL1 + MUL1
        D_IN = MUL0 + 3 * MUL1
        AVG_DEG = E / N
        key = jax.random.key(seed)
        ks = jax.random.split(key, 16)
        p = lambda i, s: jax.random.normal(ks[i], s, jnp.float32)
        return {'node_features': p(0, (N, D_IN)), 'edge_sh': p(1, (E, 4)), 'edge_embed': jax.random.uniform(ks[2], (E, NB), jnp.float32), 'W1_s': p(3, (MUL0, MUL0)), 'W1_v': p(4, (MUL1, MUL1)), 'fc_w1': p(5, (NB, HID)), 'fc_b1': jnp.zeros((HID,), jnp.float32), 'fc_w2': p(6, (HID, WNUM)) * 0.1, 'fc_b2': jnp.zeros((WNUM,), jnp.float32), 'W2_s': p(7, (96, 96)), 'W2_v': p(8, (96, MUL1)), 'Wsc_s': p(9, (MUL0, 96)), 'Wsc_v': p(10, (MUL1, MUL1)), 'edge_index': jax.random.randint(ks[11], (2, E), 0, N)}
    _L1_gnn_all = _L1_gnn_setup()
    _L1_gnn_in = {k: v for k, v in _L1_gnn_all.items() if k in ('W1_s', 'W1_v', 'fc_w1', 'fc_b1', 'fc_w2', 'fc_b2', 'W2_s', 'W2_v', 'Wsc_s', 'Wsc_v')}
    del _L1_gnn_all
    return {'x': x, 'src': src, 'dst': dst, 'edge_attr_16': edge_attr_16, 'edge_attr_4': edge_attr_4, 'edge_attr_8': edge_attr_8, 'L0_gnn_gamma_s': _L0_gnn_in['gamma_s'], 'L0_gnn_beta_s': _L0_gnn_in['beta_s'], 'L0_gnn_gamma_v': _L0_gnn_in['gamma_v'], 'L0_gnn_Ws_src': _L0_gnn_in['Ws_src'], 'L0_gnn_Wv_src': _L0_gnn_in['Wv_src'], 'L0_gnn_Ws_dst': _L0_gnn_in['Ws_dst'], 'L0_gnn_Wv_dst': _L0_gnn_in['Wv_dst'], 'L0_gnn_W_rbf': _L0_gnn_in['W_rbf'], 'L0_gnn_W_alpha': _L0_gnn_in['W_alpha'], 'L0_gnn_alpha_dot': _L0_gnn_in['alpha_dot'], 'L0_gnn_Ws_val': _L0_gnn_in['Ws_val'], 'L0_gnn_Wv_val': _L0_gnn_in['Wv_val'], 'L0_gnn_Wg': _L0_gnn_in['Wg'], 'L0_gnn_w2_ss': _L0_gnn_in['w2_ss'], 'L0_gnn_w2_sv': _L0_gnn_in['w2_sv'], 'L0_gnn_w2_vs': _L0_gnn_in['w2_vs'], 'L0_gnn_w2_vv0': _L0_gnn_in['w2_vv0'], 'L0_gnn_w2_vv1': _L0_gnn_in['w2_vv1'], 'L0_gnn_Ws_vlin': _L0_gnn_in['Ws_vlin'], 'L0_gnn_Wv_vlin': _L0_gnn_in['Wv_vlin'], 'L0_gnn_Wps': _L0_gnn_in['Wps'], 'L0_gnn_Wpv': _L0_gnn_in['Wpv'], 'L1_gnn_W1_s': _L1_gnn_in['W1_s'], 'L1_gnn_W1_v': _L1_gnn_in['W1_v'], 'L1_gnn_fc_w1': _L1_gnn_in['fc_w1'], 'L1_gnn_fc_b1': _L1_gnn_in['fc_b1'], 'L1_gnn_fc_w2': _L1_gnn_in['fc_w2'], 'L1_gnn_fc_b2': _L1_gnn_in['fc_b2'], 'L1_gnn_W2_s': _L1_gnn_in['W2_s'], 'L1_gnn_W2_v': _L1_gnn_in['W2_v'], 'L1_gnn_Wsc_s': _L1_gnn_in['Wsc_s'], 'L1_gnn_Wsc_v': _L1_gnn_in['Wsc_v']}

def reference(x, src, dst, edge_attr_16, edge_attr_4, edge_attr_8, L0_gnn_gamma_s, L0_gnn_beta_s, L0_gnn_gamma_v, L0_gnn_Ws_src, L0_gnn_Wv_src, L0_gnn_Ws_dst, L0_gnn_Wv_dst, L0_gnn_W_rbf, L0_gnn_W_alpha, L0_gnn_alpha_dot, L0_gnn_Ws_val, L0_gnn_Wv_val, L0_gnn_Wg, L0_gnn_w2_ss, L0_gnn_w2_sv, L0_gnn_w2_vs, L0_gnn_w2_vv0, L0_gnn_w2_vv1, L0_gnn_Ws_vlin, L0_gnn_Wv_vlin, L0_gnn_Wps, L0_gnn_Wpv, L1_gnn_W1_s, L1_gnn_W1_v, L1_gnn_fc_w1, L1_gnn_fc_b1, L1_gnn_fc_w2, L1_gnn_fc_b2, L1_gnn_W2_s, L1_gnn_W2_v, L1_gnn_Wsc_s, L1_gnn_Wsc_v):
    import jax
    import jax.numpy as jnp

    def _L0_gnn_ref(node, rbf, rsh, gamma_s, beta_s, gamma_v, Ws_src, Wv_src, Ws_dst, Wv_dst, W_rbf, W_alpha, alpha_dot, Ws_val, Wv_val, Wg, w2_ss, w2_sv, w2_vs, w2_vv0, w2_vv1, Ws_vlin, Wv_vlin, Wps, Wpv, edge_index):
        import jax, jax.numpy as jnp
        import numpy as np
        N, E = (625, 10000)
        CS, CV = (64, 32)
        AS_, AV, H = (16, 8, 4)
        NB = 16
        SQRT3 = 1.7320508075688772
        SQRT2 = 1.4142135623730951
        EPS = 1e-05

        def _cg_tp(s, v, y0, y1, w_ss, w_sv, w_vs, w_vv0, w_vv1):
            out_s = jnp.concatenate([w_ss * s * y0[:, None], w_vv0 * (jnp.einsum('eci,ei->ec', v, y1) / SQRT3)], axis=-1)
            out_v = jnp.concatenate([(w_sv * s)[:, :, None] * y1[:, None, :], (w_vs * jnp.ones_like(v[..., 0]))[..., None] * v * y0[:, None, None], (w_vv1 * jnp.ones_like(v[..., 0]))[..., None] * (jnp.cross(v, y1[:, None, :]) / SQRT2)], axis=1)
            return (out_s, out_v)

        def _equiv_layernorm(s, v, gamma_s, beta_s, gamma_v):
            mu = jnp.mean(s, axis=-1, keepdims=True)
            var = jnp.var(s, axis=-1, keepdims=True)
            s_n = (s - mu) * jax.lax.rsqrt(var + EPS) * gamma_s + beta_s
            rms = jnp.sqrt(jnp.mean(jnp.sum(v * v, axis=-1), axis=-1, keepdims=True) + EPS)
            v_n = v / rms[..., None] * gamma_v[None, :, None]
            return (s_n, v_n)
        n = node.shape[0]
        e = rsh.shape[0]
        s = node[:, :CS]
        v = node[:, CS:].reshape(n, CV, 3)
        s_n, v_n = _equiv_layernorm(s, v, gamma_s, beta_s, gamma_v)
        src, dst = (edge_index[0], edge_index[1])
        msg_s = (s_n @ Ws_src)[src] + (s_n @ Ws_dst)[dst]
        msg_v = jnp.einsum('ncx,cd->ndx', v_n, Wv_src)[src] + jnp.einsum('ncx,cd->ndx', v_n, Wv_dst)[dst]
        y0, y1 = (rsh[:, 0], rsh[:, 1:4])
        w1 = rbf @ W_rbf
        m1_s, m1_v = _cg_tp(msg_s, msg_v, y0, y1, w1[:, :CS], w1[:, CS:2 * CS], w1[:, 2 * CS:2 * CS + CV], w1[:, 2 * CS + CV:2 * CS + 2 * CV], w1[:, 2 * CS + 2 * CV:])
        a = (m1_s @ W_alpha).reshape(e, H, AS_)
        a = jnp.where(a > 0, a, 0.2 * a)
        a = jnp.sum(a * alpha_dot, axis=-1, keepdims=True)
        amax = jax.ops.segment_max(a, dst, num_segments=n)
        amax = jnp.where(jnp.isfinite(amax), amax, 0.0)
        ex = jnp.exp(a - amax[dst])
        den = jax.ops.segment_sum(ex, dst, num_segments=n)
        alpha = ex / (den[dst] + 1e-16)
        val_s = m1_s @ Ws_val
        val_v = jnp.einsum('ecx,cd->edx', m1_v, Wv_val)
        val_v = val_v * jax.nn.sigmoid(val_s @ Wg)[..., None]
        val_s = jax.nn.sigmoid(val_s)
        m2_s, m2_v = _cg_tp(val_s, val_v, y0, y1, w2_ss, w2_sv, w2_vs, w2_vv0, w2_vv1)
        hs = (m2_s @ Ws_vlin).reshape(e, H, AS_)
        hv = jnp.einsum('ecx,cd->edx', m2_v, Wv_vlin).reshape(e, H, AV, 3)
        h = jnp.concatenate([hs, hv.reshape(e, H, AV * 3)], axis=-1)
        agg = jax.ops.segment_sum(alpha * h, dst, num_segments=n)
        agg_s = agg[:, :, :AS_].reshape(n, H * AS_)
        agg_v = agg[:, :, AS_:].reshape(n, H * AV, 3)
        out = node + jnp.concatenate([agg_s @ Wps, jnp.einsum('ncx,cd->ndx', agg_v, Wpv).reshape(n, CV * 3)], axis=-1)
        return out

    def _L1_gnn_ref(node_features, edge_sh, edge_embed, W1_s, W1_v, fc_w1, fc_b1, fc_w2, fc_b2, W2_s, W2_v, Wsc_s, Wsc_v, edge_index):
        import jax, jax.numpy as jnp
        import numpy as np
        N = 50000
        E = 25000
        MUL0 = 64
        MUL1 = 32
        NB = 8
        HID = 64
        WNUM = MUL0 + MUL0 + MUL1 + MUL1
        D_IN = MUL0 + 3 * MUL1
        AVG_DEG = E / N
        n = node_features.shape[0]
        s = node_features[:, :MUL0]
        v = node_features[:, MUL0:].reshape(n, MUL1, 3)
        xs = s @ W1_s / np.sqrt(MUL0)
        xv = jnp.einsum('nmc,mk->nkc', v, W1_v) / np.sqrt(MUL1)
        src, dst = (edge_index[0], edge_index[1])
        sh0 = edge_sh[:, 0]
        sh1 = edge_sh[:, 1:4]
        w = jax.nn.silu(edge_embed @ fc_w1 + fc_b1) @ fc_w2 + fc_b2
        w_ss = w[:, :MUL0]
        w_sv = w[:, MUL0:2 * MUL0]
        w_vs = w[:, 2 * MUL0:2 * MUL0 + MUL1]
        w_vv = w[:, 2 * MUL0 + MUL1:]
        xs_e = xs[src]
        xv_e = xv[src]
        m0_a = w_ss * xs_e * sh0[:, None]
        m1_a = (w_sv * xs_e)[:, :, None] * sh1[:, None, :]
        m1_b = w_vs[:, :, None] * xv_e * sh0[:, None, None]
        m0_b = w_vv * jnp.einsum('emc,ec->em', xv_e, sh1) / np.sqrt(3.0)
        msg = jnp.concatenate([m0_a, m0_b, m1_a.reshape(-1, MUL0 * 3), m1_b.reshape(-1, MUL1 * 3)], axis=1)
        agg = jax.ops.segment_sum(msg, dst, num_segments=n) / np.sqrt(AVG_DEG)
        agg_s = agg[:, :96]
        agg_v = agg[:, 96:].reshape(n, 96, 3)
        out_s = agg_s @ W2_s / np.sqrt(96.0)
        out_v = jnp.einsum('nmc,mk->nkc', agg_v, W2_v) / np.sqrt(96.0)
        out_s = out_s + s @ Wsc_s / np.sqrt(MUL0)
        out_v = out_v + jnp.einsum('nmc,mk->nkc', v, Wsc_v) / np.sqrt(MUL1)
        scalars = jax.nn.silu(out_s[:, :MUL0])
        gates = jax.nn.silu(out_s[:, MUL0:MUL0 + MUL1])
        gated = out_v * gates[:, :, None]
        feats = jnp.concatenate([scalars, gated.reshape(n, MUL1 * 3)], axis=1)
        return node_features + feats
    edge_index = jnp.stack([src, dst])
    x = _layernorm(x + _L0_gnn_ref(x, edge_attr_16, edge_attr_4, L0_gnn_gamma_s, L0_gnn_beta_s, L0_gnn_gamma_v, L0_gnn_Ws_src, L0_gnn_Wv_src, L0_gnn_Ws_dst, L0_gnn_Wv_dst, L0_gnn_W_rbf, L0_gnn_W_alpha, L0_gnn_alpha_dot, L0_gnn_Ws_val, L0_gnn_Wv_val, L0_gnn_Wg, L0_gnn_w2_ss, L0_gnn_w2_sv, L0_gnn_w2_vs, L0_gnn_w2_vv0, L0_gnn_w2_vv1, L0_gnn_Ws_vlin, L0_gnn_Wv_vlin, L0_gnn_Wps, L0_gnn_Wpv, edge_index), axis=-1)
    x = _layernorm(x + _L1_gnn_ref(x, edge_attr_4, edge_attr_8, L1_gnn_W1_s, L1_gnn_W1_v, L1_gnn_fc_w1, L1_gnn_fc_b1, L1_gnn_fc_w2, L1_gnn_fc_b2, L1_gnn_W2_s, L1_gnn_W2_v, L1_gnn_Wsc_s, L1_gnn_Wsc_v, edge_index), axis=-1)
    return x

_drawn_inputs = setup_inputs


def setup_inputs(seed=0):
    import zlib

    import numpy as np

    out = dict(_drawn_inputs(seed))
    spreads = {'L0_gnn_gamma_s': (1.0, 0.6),
     'L0_gnn_beta_s': (0.0, 0.8),
     'L0_gnn_gamma_v': (1.0, 0.6),
     'L1_gnn_fc_b1': (0.0, 0.334),
     'L1_gnn_fc_b2': (0.0, 0.1)}
    factors = {'L0_gnn_W_alpha': 3.763, 'L0_gnn_alpha_dot': 3.642, 'L0_gnn_w2_vv1': 2.709}
    for name, (base, spread) in spreads.items():
        noise = np.random.default_rng([zlib.crc32(name.encode()), seed]).standard_normal(out[name].shape)
        drawn = base * np.exp(spread * noise) if base else spread * noise
        out[name] = jnp.asarray(drawn.astype(out[name].dtype))
    for name, factor in factors.items():
        out[name] = (out[name] * factor).astype(out[name].dtype)
    return out
```

```python
from contextlib import ExitStack

import concourse.bass as bass
from concourse import mybir

F32 = mybir.dt.float32
I32 = mybir.dt.int32
ALU = mybir.AluOpType
ACT = mybir.ActivationFunctionType

P = 128
NODES, EDGES = 50000, 25000
CS, CV, HEADS = 64, 32, 4
CV3 = 3 * CV
D = CS + CV3
TG = 4
GROUP = TG * P
ITERS = 25
CHUNK = 2 * GROUP
EP = ITERS * CHUNK
GROUPS = 2 * ITERS
NODE_ITERS = 49
NP = NODE_ITERS * CHUNK
EPS = 1e-5
BIG = 1e30
SKIP = 1 << 20
SEG = HEADS * ITERS
AGG = D + HEADS
MSG = 96 + CV3

BLOCKS = [
    ("msg_s", 128, 128), ("msg_v_src", 96, 96), ("msg_v_dst", 96, 96),
    ("rbf_s", 80, 128), ("rbf_vv0", 80, 96), ("rbf_vs", 80, 96), ("rbf_vv1_next", 80, 96), ("rbf_vv1_prev", 80, 96),
    ("alpha_s", 128, 64), ("alpha_dotv", 96, 64), ("val_s", 128, 128), ("val_dotv", 96, 128),
    ("gate", 128, 96), ("val_v_sv", 128, 96), ("val_v_vs", 96, 96), ("val_v_next", 96, 96), ("val_v_prev", 96, 96),
    ("alpha_dot", 64, 4),
    ("out_s01", 128, 96), ("out_s23", 128, 64), ("out_dotv", 96, 64), ("out_vs", 96, 96),
    ("out_next", 96, 96), ("out_prev", 96, 96), ("proj_s", 64, 64), ("proj_v", 96, 96),
    ("l1_xs", 64, 128), ("l1_xv", 96, 96), ("fc1", 8, 64), ("fc2_s01", 64, 128), ("fc2_s23", 64, 128),
    ("fc2_vs", 64, 96), ("fc2_vv", 64, 96),
    ("l1_s01", 128, 128), ("l1_s23", 128, 64), ("l1_vs", 96, 96), ("l1_vv", 96, 96),
    ("self_s", 64, 96), ("self_v", 96, 96),
]
COL, at = {}, 0
for _name, _rows, _cols in BLOCKS:
    COL[_name] = (at, _rows, _cols)
    at += _cols
WCOLS = at
VECS = ["gamma_s2", "beta_s2", "gamma_v3", "w2_s01", "w2_s23", "w2_vv0", "w2_vs", "w2_vv1",
        "b_s01", "b_s23", "b_vs", "b_vv", "b_fc1", "last_row"]
VCOL = {n: i for i, n in enumerate(VECS)}
ONE, Y0, YX, RBF, EMB = 0, 1, 2, 7, 23
EROWS = 31


def build(nc, x, src_idx, dst_idx, dst_cols, dst_next, dst_line, edge_rows, weights, vectors, ident, head_mask, out):
    h_rows = nc.dram_tensor("h_rows", [GROUPS, P, TG * D], F32).ap()
    x1 = nc.dram_tensor("x1", [NP, D], F32).ap()
    x1_dst = nc.dram_tensor("x1_dst", [GROUPS, P, TG * D], F32).ap()

    with ExitStack() as top:
        def sem_in(ctx):
            made = []

            def new_sem(name):
                made.append(ctx.enter_context(nc.semaphore(name)))
                return made[-1]

            def clear():
                with nc.Block() as block:
                    @block.gpsimd
                    def _(pool):
                        for s in made:
                            pool.sem_clear(s)

            ctx.callback(clear) if ctx is not top else None
            return new_sem

        def sb_in(ctx):
            return lambda name, shape, dt=F32: ctx.enter_context(nc.sbuf_tensor(name, shape, dt))

        sb, sem = sb_in(top), sem_in(top)
        top_sem = sem
        w_sb = sb("w_sb", [P, WCOLS])
        v_sb = sb("v_sb", [P, len(VECS)])
        id_sb = sb("id_sb", [P, P])
        go = sem("go")
        half = sb("half", [P, 2 * TG * 2])
        msg_bias = sb("msg_bias", [P, 1])
        a_edge = sb("a_edge", [P, 2 * TG, HEADS, ITERS])
        ex_edge = sb("ex_edge", [P, 2 * TG, HEADS, ITERS])

        def W(name, rows=None):
            c, r, n = COL[name]
            return w_sb[0:rows or r, c:c + n]

        def V(name, rows):
            return v_sb[0:rows, VCOL[name]:VCOL[name] + 1]

        psum = [top.enter_context(nc.psum_tensor(f"bank{b}", [P, 512], F32)) for b in range(8)]

        const_in, scaled, bias_ps, bias_ok = sem("const_in"), sem("scaled"), sem("bias_ps"), sem("bias_ok")
        with nc.Block() as block:
            @block.sync
            def _(sp):
                sp.dma_start(w_sb[:], weights).then_inc(const_in, 16)
                sp.dma_start(v_sb[:], vectors).then_inc(const_in, 16)
                sp.dma_start(id_sb[:], ident).then_inc(const_in, 16)

            @block.tensor
            def _(pe):
                pe.wait_ge(const_in, 48)
                pe.matmul(psum[0][:, 0:1], W("msg_s"), V("beta_s2", 128), start=True, stop=True).then_inc(bias_ps, 1)

            @block.vector
            def _(dve):
                dve.memset(half[:], -0.5)
                dve.wait_ge(bias_ps, 1)
                dve.tensor_copy(msg_bias[:], psum[0][:, 0:1]).then_inc(bias_ok, 1)
                dve.wait_ge(const_in, 48)
                r3, r2 = 3 ** -0.5, 2 ** -0.5
                for name, vec, scale in (
                        ("msg_s", "gamma_s2", 1.0), ("msg_v_src", "gamma_v3", 1.0), ("msg_v_dst", "gamma_v3", 1.0),
                        ("out_s01", "w2_s01", 1.0), ("out_s23", "w2_s23", 1.0), ("out_dotv", "w2_vv0", r3),
                        ("out_vs", "w2_vs", 1.0), ("out_next", "w2_vv1", r2), ("out_prev", "w2_vv1", -r2)):
                    m = W(name)
                    dve.tensor_scalar(m, m, V(vec, m.shape[0]), scale, ALU.mult, ALU.mult)
                agg = 48 ** -0.5
                for name, scale in (
                        ("alpha_dotv", r3), ("val_dotv", r3), ("val_v_next", r2), ("val_v_prev", -r2),
                        ("l1_xs", 1 / 8), ("l1_xv", 32 ** -0.5), ("l1_s01", agg), ("l1_s23", agg), ("l1_vs", agg),
                        ("l1_vv", agg * r3), ("self_s", 1 / 8), ("self_v", 32 ** -0.5)):
                    last = dve.tensor_scalar_mul(W(name), W(name), scale)
                last.then_inc(scaled, 1)

        with ExitStack() as ctx:
            sem = sem_in(ctx)
            stages0 = ["z_ready", "zT_s", "zT_vs", "zT_vd", "zs_sb", "zvs_sb", "zvd_sb", "msgs_ps", "msgv_ps", "msgs_sb",
                       "msgv_sb", "w_s", "w_vs", "w_next", "w_prev", "w_vv0", "p_s", "p_vs", "p_next", "p_prev", "p_vv0",
                       "alpha_ps", "vals_ps", "fifth_sb", "leaky_sb", "vals_sb", "sig_sb", "svy_ps", "valv_ps", "gate_ps", "gate_sb",
                       "svy_sb", "valv_sum", "valv_sb", "a_ps", "a_sb", "prod_sb", "h_ps0", "h_ps1", "h_sb0", "h_sb1",
                       "stats_ready", "mv_ready", "sq_ready", "q_ready", "rstd_ready", "r_ready", "attn_used"]
            s0 = {n: sem("e0_" + n) for n in stages0}
            x_in = [top_sem(f"x_in{u}") for u in range(2)]
            idx_in = [sem(f"idx_in{u}") for u in range(2)]
            rbf_in = [sem(f"rbf_in{u}") for u in range(2)]
            y_in = [sem(f"y_in{u}") for u in range(2)]
            h_out = [sem(f"h_out{u}") for u in range(2)]
            primed = sem("primed")

            def prime(sp, sems):
                for s in sems:
                    sp.sem_inc(s, 1)

            with nc.Block() as block:
                sb = sb_in(ctx)
                two = lambda name, shape, dt=F32: [sb(f"{name}{u}", shape, dt) for u in range(2)]
                sidx, didx = two("sidx", [P, TG], I32), two("didx", [P, TG], I32)
                xg = two("xg", [P, 2 * TG, D])
                z = two("z", [P, TG, 2 * D])
                stats, mv = two("stats", [P, 4 * TG, 6]), two("mv", [P, 4 * TG, 2])
                msq, q, rstd = two("msq", [P, 2 * TG]), two("q", [P, 4 * TG]), two("rstd", [P, 4 * TG])
                rbf_rep, y_rep, r80 = two("rbf_rep", [80, GROUP]), two("y_rep", [80, GROUP]), two("r80", [80, GROUP])
                ybc = two("ybc", [P, 6, GROUP])
                zs, zvs, zvd = two("zs", [P, GROUP]), two("zvs", [96, GROUP]), two("zvd", [96, GROUP])
                msgs, msgv = two("msgs", [P, GROUP]), two("msgv", [96, GROUP])
                p_s, p_vs, p_next, p_prev, p_vv0 = (two(n, [128 if n == "p_s" else 96, GROUP])
                                                    for n in ("p_s", "p_vs", "p_next", "p_prev", "p_vv0"))
                leaky, vals, sig, gate = (two("leaky", [64, GROUP]), two("vals", [P, GROUP]), two("sig", [P, GROUP]),
                                          two("gate", [96, GROUP]))
                valv = two("valv", [96, GROUP])
                m_s01, m_s23, m_vs, m_dot, m_next, m_prev = (two("m_" + n, [128 if n[0] == "s" else 96, GROUP])
                                                             for n in ("s01", "s23", "vs", "dot", "next", "prev"))
                h_sb = two("h_sb", [P, TG * D])

                @block.sync
                def _(sp):
                    prime(sp, s0.values())
                    sp.sem_inc(primed, 1)
                    for u in range(2):
                        sp.dma_start(h_sb[u][0:16, 0:D], x[0:16, :]).then_inc(h_out[u], 16)
                    with sp.Fori(0, ITERS) as i:
                        for u in range(2):
                            sp.wait_ge(s0["z_ready"], 2 * i + 1)
                            sp.dma_start(sidx[u][:], src_idx[bass.ds(2 * i + u, 1)].rearrange("a p t -> (a p) t")).then_inc(idx_in[u], 16)
                            sp.dma_start(didx[u][:], dst_idx[bass.ds(2 * i + u, 1)].rearrange("a p t -> (a p) t")).then_inc(idx_in[u], 16)
                        for u in range(2):
                            cols = bass.ds(i * CHUNK + u * GROUP, GROUP)
                            sp.wait_ge(s0["r_ready"], 2 * i + 1)
                            sp.dma_start(rbf_rep[u][:], edge_rows[RBF:RBF + 16, cols].unsqueeze(1).broadcast_to([16, 5, GROUP])).then_inc(rbf_in[u], 16)
                            sp.dma_start(y_rep[u][:], edge_rows[ONE:ONE + 5, cols].unsqueeze(0).broadcast_to([16, 5, GROUP])).then_inc(rbf_in[u], 16)
                        for u in range(2):
                            cols = bass.ds(i * CHUNK + u * GROUP, GROUP)
                            sp.wait_ge(s0["prod_sb"], 2 * i + 1)
                            for k, (row, n, rep) in enumerate(((Y0, 2, 64), (YX + 1, 2, 64), (Y0, 1, 96), (YX, 3, 32),
                                                               (YX + 1, 3, 32), (YX + 2, 3, 32))):
                                sp.dma_start(ybc[u][0:n * rep, k, :],
                                             edge_rows[row:row + n, cols].unsqueeze(0).broadcast_to([rep, n, GROUP])
                                             ).then_inc(y_in[u], 16)

                @block.gpsimd
                def _(pool):
                    pool.wait_ge(primed, 1)
                    with pool.Fori(0, ITERS) as i:
                        for u in range(2):
                            pool.wait_ge(s0["z_ready"], 2 * i + 1)
                            pool.wait_ge(idx_in[u], 32 * i + 32)
                            pool.sem_inc(go, 1)
                            for side, idx in enumerate((sidx[u], didx[u])):
                                for t in range(TG):
                                    pool.indirect_dma_start(
                                        out=xg[u][:, side * TG + t, :], out_offset=None, in_=x,
                                        in_offset=bass.IndirectOffsetOnAxis(ap=idx[:, t:t + 1], axis=0)).then_inc(x_in[u], 16)
                        for u in range(2):
                            pool.wait_ge(s0["q_ready"], 2 * i + u + 2)
                            pool.tensor_tensor(rstd[u][:], q[u][:], half[:], ALU.pow).then_inc(s0["rstd_ready"], 1)

                @block.tensor
                def _(pe):
                    pe.wait_ge(primed, 1)
                    with pe.Fori(0, ITERS) as i:
                        B = lambda u, b: psum[4 * u + b]
                        new = lambda u: 2 * i + u + 2
                        old = 2 * i + 1

                        def job(u, bank, width, waits, mms, done):
                            for name, value in waits:
                                pe.wait_ge(s0[name], value)
                            for n, (w, rhs) in enumerate(mms):
                                last = pe.matmul(B(u, bank)[0:w.shape[1], 0:GROUP], w, rhs, start=(n == 0), stop=(n == len(mms) - 1))
                            last.then_inc(s0[done], 1)

                        for u in range(2):
                            pe.wait_ge(s0["z_ready"], new(u))
                            for bank, c, n, freed, done in ((0, 0, 128, "h_sb0", "zT_s"), (1, 128, 96, "h_sb1", "zT_vs"),
                                                            (2, 224, 96, "gate_sb", "zT_vd")):
                                pe.wait_ge(s0[freed], old)
                                pe.sem_inc(go, 1)
                                for t in range(TG):
                                    last = pe.transpose(B(u, bank)[0:n, t * P:(t + 1) * P], z[u][:, t, c:c + n], id_sb[:])
                                last.then_inc(s0[done], 1)
                        for u in range(2):
                            job(u, 3, 128, [("zs_sb", new(u)), ("a_sb", old)], [(W("msg_s"), zs[u][:])], "msgs_ps")
                        for u in range(2):
                            job(u, 0, 96, [("zvs_sb", new(u)), ("zvd_sb", new(u))],
                                [(W("msg_v_src"), zvs[u][:]), (W("msg_v_dst"), zvd[u][:])], "msgv_ps")
                        for u in range(2):
                            job(u, 1, 128, [("r_ready", new(u))], [(W("rbf_s"), r80[u][:])], "w_s")
                        for u in range(2):
                            job(u, 2, 96, [], [(W("rbf_vs"), r80[u][:])], "w_vs")
                        for u in range(2):
                            job(u, 3, 96, [("msgs_sb", new(u))], [(W("rbf_vv1_next"), r80[u][:])], "w_next")
                        for u in range(2):
                            job(u, 0, 96, [("msgv_sb", new(u))], [(W("rbf_vv1_prev"), r80[u][:])], "w_prev")
                        for u in range(2):
                            job(u, 1, 96, [("p_s", new(u))], [(W("rbf_vv0"), r80[u][:])], "w_vv0")
                        for u in range(2):
                            job(u, 3, 128, [("p_next", new(u)), ("p_vv0", new(u))],
                                [(W("val_s"), p_s[u][:]), (W("val_dotv"), p_vv0[u][:])], "vals_ps")
                        for u in range(2):
                            job(u, 2, 64, [("p_vs", new(u))], [(W("alpha_s"), p_s[u][:]), (W("alpha_dotv"), p_vv0[u][:])],
                                "alpha_ps")
                        for u in range(2):
                            job(u, 0, 96, [("p_prev", new(u))], [(W("val_v_sv"), p_s[u][:])], "svy_ps")
                        for u in range(2):
                            job(u, 1, 96, [], [(W("val_v_vs"), p_vs[u][:]), (W("val_v_next"), p_next[u][:]),
                                               (W("val_v_prev"), p_prev[u][:])], "valv_ps")
                        for u in range(2):
                            job(u, 2, 96, [("vals_sb", new(u)), ("leaky_sb", new(u))], [(W("gate"), vals[u][:])], "gate_ps")
                        for u in range(2):
                            pe.wait_ge(s0["sig_sb"], new(u))
                            for t in range(TG):
                                last = pe.matmul(B(u, 3)[:, t * HEADS:(t + 1) * HEADS], leaky[u][:, t * P:(t + 1) * P],
                                                 W("alpha_dot"), start=True, stop=True)
                            last.then_inc(s0["a_ps"], 1)
                        for u in range(2):
                            pe.wait_ge(s0["prod_sb"], new(u))
                            for t in range(TG):
                                if t == 0:
                                    pe.wait_ge(s0["svy_sb"], new(u))
                                if t == 3:
                                    pe.wait_ge(s0["valv_sum"], new(u))
                                o = B(u, t // 3)[:, (t % 3) * D:(t % 3 + 1) * D]
                                e = slice(t * P, (t + 1) * P)
                                pe.matmul(o[:, 0:96], m_s01[u][:, e], W("out_s01"), start=True, stop=False, skip_group_check=True)
                                pe.matmul(o[:, 96:160], m_s23[u][:, e], W("out_s23"), start=False, stop=False, skip_group_check=True)
                                pe.matmul(o[:, 0:64], m_dot[u][:, e], W("out_dotv"), start=False, stop=False, skip_group_check=True)
                                for m, w in ((m_vs, "out_vs"), (m_next, "out_next"), (m_prev, "out_prev")):
                                    last = pe.matmul(o[:, 64:160], m[u][:, e], W(w), start=False, stop=(w == "out_prev"),
                                                     skip_group_check=True)
                                if t == 2:
                                    last.then_inc(s0["h_ps0"], 1)
                            last.then_inc(s0["h_ps1"], 1)

                @block.scalar
                def _(act):
                    act.wait_ge(primed, 1)
                    with act.Fori(0, ITERS) as i:
                        B = lambda u, b: psum[4 * u + b]
                        new = lambda u: 2 * i + u + 2
                        old = 2 * i + 1
                        for u in range(2):
                            for bank, n, src, dst, done, freed in ((0, 128, "zT_s", zs, "zs_sb", "msgs_ps"),
                                                                   (1, 96, "zT_vs", zvs, "zvs_sb", "msgv_ps"),
                                                                   (2, 96, "zT_vd", zvd, "zvd_sb", "msgv_ps")):
                                act.wait_ge(s0[src], new(u))
                                act.wait_ge(s0[freed], old)
                                nc.scalar.activation(dst[u][:], B(u, bank)[0:n, :], ACT.Copy).then_inc(s0[done], 1)
                        for u in range(2):
                            act.wait_ge(s0["msgs_ps"], new(u))
                            act.wait_ge(s0["p_s"], old)
                            nc.scalar.activation(msgs[u][:], B(u, 3)[:, :], ACT.Identity, bias=msg_bias[:, 0:1]).then_inc(s0["msgs_sb"], 1)
                        for u in range(2):
                            act.wait_ge(s0["msgv_ps"], new(u))
                            act.wait_ge(s0["p_vv0"], old)
                            nc.scalar.activation(msgv[u][:], B(u, 0)[0:96, :], ACT.Copy).then_inc(s0["msgv_sb"], 1)
                        for u in range(2):
                            act.wait_ge(s0["vals_ps"], new(u))
                            act.wait_ge(s0["gate_ps"], old)
                            nc.scalar.activation(vals[u][:], B(u, 3)[:, :], ACT.Copy).then_inc(s0["vals_sb"], 1)
                            act.wait_ge(s0["prod_sb"], old)
                            nc.scalar.activation(sig[u][:], B(u, 3)[:, :], ACT.Sigmoid).then_inc(s0["sig_sb"], 1)
                        for u in range(2):
                            act.wait_ge(s0["alpha_ps"], new(u))
                            act.wait_ge(s0["a_ps"], old)
                            nc.scalar.activation(leaky[u][:], B(u, 2)[0:64, :], ACT.Copy, scale=0.2).then_inc(s0["fifth_sb"], 1)
                        for u in range(2):
                            act.wait_ge(s0["gate_ps"], new(u))
                            act.wait_ge(s0["valv_sb"], old)
                            nc.scalar.activation(gate[u][:], B(u, 2)[0:96, :], ACT.Sigmoid).then_inc(s0["gate_sb"], 1)
                        for u in range(2):
                            act.wait_ge(s0["h_ps0"], new(u))
                            act.wait_ge(h_out[u], 16 * i + 16)
                            nc.scalar.activation(h_sb[u][:, 0:3 * D], B(u, 0)[:, 0:3 * D], ACT.Copy).then_inc(s0["h_sb0"], 1)
                            act.wait_ge(s0["h_ps1"], new(u))
                            nc.scalar.activation(h_sb[u][:, 3 * D:4 * D], B(u, 1)[:, 0:D], ACT.Copy).then_inc(s0["h_sb1"], 1)
                            act.wait_ge(s0["h_sb0"], new(u))
                            act.wait_ge(s0["h_sb1"], new(u))
                            act.dma_start(h_rows[bass.ds(2 * i + u, 1)].rearrange("a p f -> (a p) f"), h_sb[u][:]).then_inc(h_out[u], 16)
                    for u in range(2):
                        act.wait_ge(h_out[u], 16 * ITERS + 16)

                @block.vector
                def _(dve):
                    dve.wait_ge(primed, 1)
                    with dve.Fori(0, ITERS) as i:
                        B = lambda u, b: psum[4 * u + b]
                        new = lambda u: 2 * i + u + 2
                        old = 2 * i + 1
                        for u in range(2):
                            dve.wait_ge(x_in[u], 128 * i + 128)
                            for k in range(2 * TG):
                                nc.vector.bn_stats(stats[u][:, k, :], xg[u][:, k, 0:CS])
                                last = nc.vector.bn_stats(stats[u][:, 2 * TG + k, :], xg[u][:, k, CS:D])
                            last.then_inc(s0["stats_ready"], 1)
                            dve.wait_ge(s0["stats_ready"], new(u))
                            dve.sem_inc(go, 1)
                            for k in range(4 * TG):
                                last = nc.vector.bn_aggr(mv[u][:, k, :], stats[u][:, k, :])
                            last.then_inc(s0["mv_ready"], 1)
                            dve.wait_ge(s0["mv_ready"], new(u))
                            dve.wait_ge(s0["rstd_ready"], 2 * i + 1)
                            mean_v, var_v = mv[u][:, 2 * TG:, 0], mv[u][:, 2 * TG:, 1]
                            nc.vector.tensor_tensor(msq[u][:], mean_v, mean_v, ALU.mult).then_inc(s0["sq_ready"], 1)
                            nc.vector.tensor_scalar(q[u][:, 0:2 * TG], mv[u][:, 0:2 * TG, 1], EPS, None, ALU.add)
                            dve.wait_ge(s0["sq_ready"], 4 * i + 2 * u + 2)
                            nc.vector.tensor_tensor(msq[u][:], msq[u][:], var_v, ALU.add).then_inc(s0["sq_ready"], 1)
                            dve.wait_ge(s0["sq_ready"], 4 * i + 2 * u + 3)
                            nc.vector.tensor_scalar(q[u][:, 2 * TG:], msq[u][:], 3.0, EPS, ALU.mult, ALU.add).then_inc(s0["q_ready"], 1)
                        for u in range(2):
                            dve.wait_ge(rbf_in[u], 32 * i + 32)
                            dve.wait_ge(s0["w_vv0"], old)
                            nc.vector.tensor_tensor(r80[u][:], rbf_rep[u][:], y_rep[u][:], ALU.mult).then_inc(s0["r_ready"], 1)
                        for u in range(2):
                            dve.wait_ge(s0["rstd_ready"], new(u))
                            dve.wait_ge(s0["zT_vd"], old)
                            for side in range(2):
                                for t in range(TG):
                                    k = side * TG + t
                                    nc.vector.tensor_scalar(z[u][:, t, side * CS:(side + 1) * CS], xg[u][:, k, 0:CS],
                                                            mv[u][:, k, 0:1], rstd[u][:, k:k + 1], ALU.subtract, ALU.mult)
                                    k2 = 2 * TG + k
                                    c = 2 * CS + side * CV3
                                    last = nc.vector.tensor_scalar(z[u][:, t, c:c + CV3], xg[u][:, k, CS:D],
                                                                   rstd[u][:, k2:k2 + 1], None, ALU.mult)
                            last.then_inc(s0["z_ready"], 1)
                        for msg, msg_ok, rows, bank, wname, dst, done, freed in (
                                (msgs, "msgs_sb", 128, 1, "w_s", p_s, "p_s", "svy_ps"),
                                (msgv, "msgv_sb", 96, 2, "w_vs", p_vs, "p_vs", "valv_ps"),
                                (msgv, "msgv_sb", 96, 3, "w_next", p_next, "p_next", "valv_ps"),
                                (msgv, "msgv_sb", 96, 0, "w_prev", p_prev, "p_prev", "valv_ps"),
                                (msgv, "msgv_sb", 96, 1, "w_vv0", p_vv0, "p_vv0", "alpha_ps")):
                            for u in range(2):
                                dve.wait_ge(s0[msg_ok], new(u))
                                dve.wait_ge(s0[wname], new(u))
                                dve.wait_ge(s0[freed], old)
                                nc.vector.tensor_tensor(dst[u][:], msg[u][:], B(u, bank)[0:rows, :], ALU.mult).then_inc(s0[done], 1)
                        for u in range(2):
                            dve.wait_ge(s0["fifth_sb"], new(u))
                            nc.vector.tensor_tensor(leaky[u][:], leaky[u][:], B(u, 2)[0:64, :], ALU.max).then_inc(s0["leaky_sb"], 1)
                        for u in range(2):
                            dve.wait_ge(s0["svy_ps"], new(u))
                            dve.wait_ge(y_in[u], 96 * i + 96)
                            dve.wait_ge(s0["h_ps1"], old)
                            nc.vector.tensor_tensor(valv[u][:], ybc[u][0:96, 3, :], B(u, 0)[0:96, :], ALU.mult).then_inc(s0["svy_sb"], 1)
                        for u in range(2):
                            dve.wait_ge(s0["svy_sb"], new(u))
                            dve.wait_ge(s0["valv_ps"], new(u))
                            nc.vector.tensor_tensor(valv[u][:], valv[u][:], B(u, 1)[0:96, :], ALU.add).then_inc(s0["valv_sum"], 1)
                        for u in range(2):
                            dve.wait_ge(s0["sig_sb"], new(u))
                            nc.vector.tensor_tensor(m_s01[u][:], sig[u][:], ybc[u][:, 0, :], ALU.mult)
                            nc.vector.tensor_tensor(m_s23[u][:], sig[u][:], ybc[u][:, 1, :], ALU.mult)
                        for u in range(2):
                            dve.wait_ge(s0["valv_sum"], new(u))
                            dve.wait_ge(s0["gate_sb"], new(u))
                            nc.vector.tensor_tensor(valv[u][:], valv[u][:], gate[u][:], ALU.mult).then_inc(s0["valv_sb"], 1)
                        for u in range(2):
                            dve.wait_ge(s0["a_ps"], new(u))
                            nc.vector.tensor_scalar(a_edge[:, TG * u:TG * (u + 1), :, bass.ds(i, 1)],
                                                    B(u, 3)[:, 0:TG * HEADS].rearrange("p (t h o) -> p t h o", h=HEADS, o=1),
                                                    1.0, None, ALU.mult).then_inc(s0["a_sb"], 1)
                        for u in range(2):
                            dve.wait_ge(s0["valv_sb"], new(u))
                            for m, k in ((m_vs, 2), (m_dot, 3), (m_next, 4), (m_prev, 5)):
                                last = nc.vector.tensor_tensor(m[u][:], valv[u][:], ybc[u][0:96, k, :], ALU.mult)
                            last.then_inc(s0["prod_sb"], 1)

        with ExitStack() as ctx:
            sem = sem_in(ctx)
            stagesn = ["x1_bn", "x1_mv", "x1_q", "x1_rstd", "x1_ready", "T_s", "T_v", "Ts_sb", "Tv_sb", "o_ps", "gates_sb",
                       "sum_ready", "gv_ready", "u_ready", "u_bn", "u_mv", "u_q", "u_rstd", "out_ready"]
            sn = {n: sem("n_" + n) for n in stagesn}
            xn_in = [sem(f"xn_in{u}") for u in range(2)]
            xn_out = [sem(f"xn_out{u}") for u in range(2)]
            primed_n = sem("primed_n")
            xv_ = lambda t, i, u: t[bass.ds(i * CHUNK + u * GROUP, GROUP), :].rearrange("(p t) d -> p (t d)", t=TG)

            with nc.Block() as block:
                sb = sb_in(ctx)
                two = lambda name, shape, dt=F32: [sb(f"{name}{u}", shape, dt) for u in range(2)]
                xn, x1n, un, outn = (two(n, [P, TG, D]) for n in ("xn", "x1n", "un", "outn"))
                st1, st2 = two("st1", [P, TG, 6]), two("st2", [P, TG, 6])
                mv1, mv2 = two("mv1", [P, TG, 2]), two("mv2", [P, TG, 2])
                q1, q2, r1, r2_, r1d = (two(n, [P, TG]) for n in ("q1", "q2", "r1", "r2_", "r1d"))
                Ts, Tv = two("Ts", [64, GROUP]), two("Tv", [96, GROUP])
                gates, gv = two("gates", [P, TG, 96]), two("gv", [P, TG, CV3])

                @block.sync
                def _(sp):
                    prime(sp, sn.values())
                    sp.sem_inc(primed_n, 1)
                    for u in range(2):
                        sp.dma_start(outn[u][0:16, 0, :], x[0:16, :]).then_inc(xn_out[u], 16)
                        sp.dma_start(x1n[u][0:16, 0, :], x[0:16, :]).then_inc(xn_out[u], 16)
                    with sp.Fori(0, NODE_ITERS) as i:
                        for u in range(2):
                            sp.wait_ge(sn["x1_ready"], 2 * i + 1)
                            sp.dma_start(xn[u][:].rearrange("p t d -> p (t d)"), xv_(x, i, u)).then_inc(xn_in[u], 16)

                @block.gpsimd
                def _(pool):
                    pool.wait_ge(primed_n, 1)
                    with pool.Fori(0, NODE_ITERS) as i:
                        for u in range(2):
                            pool.wait_ge(sn["x1_q"], 2 * i + u + 2)
                            pool.tensor_tensor(r1[u][:], q1[u][:], half[:, 0:TG], ALU.pow).then_inc(sn["x1_rstd"], 1)
                        for u in range(2):
                            pool.wait_ge(sn["u_q"], 2 * i + u + 2)
                            pool.tensor_tensor(r2_[u][:], q2[u][:], half[:, 0:TG], ALU.pow).then_inc(sn["u_rstd"], 1)

                @block.tensor
                def _(pe):
                    pe.wait_ge(primed_n, 1)
                    with pe.Fori(0, NODE_ITERS) as i:
                        for u in range(2):
                            b = psum[4 * u:4 * u + 4]
                            pe.wait_ge(sn["x1_ready"], 2 * i + u + 2)
                            for bank, c, n, freed, done in ((0, 0, 64, "Ts_sb", "T_s"), (1, CS, 96, "Tv_sb", "T_v")):
                                pe.wait_ge(sn[freed], 2 * i + 1)
                                pe.sem_inc(go, 1)
                                for t in range(TG):
                                    last = pe.transpose(b[bank][0:n, t * P:(t + 1) * P], x1n[u][:, t, c:c + n], id_sb[:])
                                last.then_inc(sn[done], 1)
                        for u in range(2):
                            b = psum[4 * u:4 * u + 4]
                            pe.wait_ge(sn["Ts_sb"], 2 * i + u + 2)
                            pe.wait_ge(sn["Tv_sb"], 2 * i + u + 2)
                            pe.wait_ge(sn["gv_ready"], 2 * i + 1)
                            for t in range(TG):
                                o = b[2 + t // 2][:, (t % 2) * MSG:(t % 2 + 1) * MSG]
                                e = slice(t * P, (t + 1) * P)
                                pe.matmul(o[:, 0:96], Ts[u][:, e], W("self_s"), start=True, stop=False, skip_group_check=True)
                                last = pe.matmul(o[:, 96:192], Tv[u][:, e], W("self_v"), start=False, stop=True, skip_group_check=True)
                            last.then_inc(sn["o_ps"], 1)

                @block.scalar
                def _(act):
                    act.wait_ge(primed_n, 1)
                    with act.Fori(0, NODE_ITERS) as i:
                        for u in range(2):
                            b = psum[4 * u:4 * u + 4]
                            act.wait_ge(sn["T_s"], 2 * i + u + 2)
                            act.wait_ge(sn["o_ps"], 2 * i + 1)
                            nc.scalar.activation(Ts[u][:], b[0][0:64, :], ACT.Copy).then_inc(sn["Ts_sb"], 1)
                            act.wait_ge(sn["T_v"], 2 * i + u + 2)
                            nc.scalar.activation(Tv[u][:], b[1][0:96, :], ACT.Copy).then_inc(sn["Tv_sb"], 1)
                        for u in range(2):
                            b = psum[4 * u:4 * u + 4]
                            act.wait_ge(sn["o_ps"], 2 * i + u + 2)
                            act.wait_ge(sn["u_ready"], 2 * i + 1)
                            for k in range(2):
                                last = nc.scalar.activation(
                                    gates[u][:, 2 * k:2 * k + 2, :],
                                    b[2 + k][:, 0:2 * MSG].rearrange("p (t f) -> p t f", t=2)[:, :, 0:96], ACT.Silu)
                            last.then_inc(sn["gates_sb"], 1)
                        for u in range(2):
                            act.wait_ge(sn["x1_ready"], 2 * i + u + 2)
                            act.dma_start(xv_(x1, i, u), x1n[u][:].rearrange("p t d -> p (t d)")).then_inc(xn_out[u], 16)
                            act.wait_ge(sn["out_ready"], 2 * i + u + 2)
                            act.dma_start(xv_(out, i, u), outn[u][:].rearrange("p t d -> p (t d)")).then_inc(xn_out[u], 16)
                    for u in range(2):
                        act.wait_ge(xn_out[u], 32 * NODE_ITERS + 32)

                @block.vector
                def _(dve):
                    dve.wait_ge(primed_n, 1)
                    with dve.Fori(0, NODE_ITERS) as i:
                        new = lambda u: 2 * i + u + 2
                        for u in range(2):
                            dve.wait_ge(xn_in[u], 16 * i + 16)
                            for t in range(TG):
                                last = nc.vector.bn_stats(st1[u][:, t, :], xn[u][:, t, :])
                            last.then_inc(sn["x1_bn"], 1)
                            dve.wait_ge(sn["x1_bn"], new(u))
                            dve.sem_inc(go, 1)
                            for t in range(TG):
                                last = nc.vector.bn_aggr(mv1[u][:, t, :], st1[u][:, t, :])
                            last.then_inc(sn["x1_mv"], 1)
                            dve.wait_ge(sn["x1_mv"], new(u))
                            nc.vector.tensor_scalar(q1[u][:], mv1[u][:, :, 1], EPS / 4, None, ALU.add).then_inc(sn["x1_q"], 1)
                        for u in range(2):
                            dve.wait_ge(sn["x1_rstd"], new(u))
                            dve.wait_ge(xn_out[u], 32 * i + 32)
                            for t in range(TG):
                                last = nc.vector.tensor_scalar(x1n[u][:, t, :], xn[u][:, t, :], mv1[u][:, t, 0:1],
                                                               r1[u][:, t:t + 1], ALU.subtract, ALU.mult)
                            last.then_inc(sn["x1_ready"], 1)
                        for u in range(2):
                            dve.wait_ge(sn["gates_sb"], new(u))
                            dve.wait_ge(sn["o_ps"], new(u))
                            nc.vector.scalar_tensor_tensor(un[u][:, :, 0:CS], x1n[u][:, :, 0:CS], 2.0, gates[u][:, :, 0:CS],
                                                           ALU.mult, ALU.add)
                            for k in range(2):
                                b = psum[4 * u + 2 + k]
                                o = b[:, 0:2 * MSG].rearrange("p (t f) -> p t f", t=2)[:, :, 96:192].rearrange("p t (c k) -> p t k c", c=3)
                                g = gates[u][:, 2 * k:2 * k + 2, CS:96].unsqueeze(3).broadcast_to([P, 2, CV, 3])
                                last = nc.vector.tensor_tensor(
                                    gv[u][:, 2 * k:2 * k + 2, :].rearrange("p t (k c) -> p t k c", c=3), g, o, ALU.mult)
                            last.then_inc(sn["gv_ready"], 1)
                            dve.wait_ge(sn["gv_ready"], new(u))
                            nc.vector.scalar_tensor_tensor(un[u][:, :, CS:D], x1n[u][:, :, CS:D], 2.0, gv[u][:],
                                                           ALU.mult, ALU.add).then_inc(sn["u_ready"], 1)
                            dve.wait_ge(sn["u_ready"], new(u))
                            for t in range(TG):
                                last = nc.vector.bn_stats(st2[u][:, t, :], un[u][:, t, :])
                            last.then_inc(sn["u_bn"], 1)
                            dve.wait_ge(sn["u_bn"], new(u))
                            dve.sem_inc(go, 1)
                            for t in range(TG):
                                last = nc.vector.bn_aggr(mv2[u][:, t, :], st2[u][:, t, :])
                            last.then_inc(sn["u_mv"], 1)
                            dve.wait_ge(sn["u_mv"], new(u))
                            nc.vector.tensor_scalar(q2[u][:], mv2[u][:, :, 1], EPS, None, ALU.add).then_inc(sn["u_q"], 1)
                        for u in range(2):
                            dve.wait_ge(sn["u_rstd"], new(u))
                            for t in range(TG):
                                last = nc.vector.tensor_scalar(outn[u][:, t, :], un[u][:, t, :], mv2[u][:, t, 0:1],
                                                               r2_[u][:, t:t + 1], ALU.subtract, ALU.mult)
                            last.then_inc(sn["out_ready"], 1)

        with ExitStack() as ctx:
            sem = sem_in(ctx)
            m_in, m_t, m_ev, m_dve, m_act = sem("m_in"), sem("m_t"), sem("m_ev"), sem("m_dve"), sem("m_act")
            with nc.Block() as block:
                sb = sb_in(ctx)
                a_seg = sb("a_seg", [SEG, CHUNK])
                dq_i = sb("dq_i", [SEG, CHUNK], I32)
                dq = sb("dq", [SEG, CHUNK])
                step = sb("step", [SEG, CHUNK + 1])
                run = sb("run", [SEG, CHUNK])
                top_ = sb("top_", [SEG, CHUNK])
                other = sb("other", [SEG, CHUNK])
                ends = sb("ends", [1, 4, SEG])
                hm = sb("hm", [1, SEG])
                cont, whole, f_in, g_in = sb("cont", [1, SEG]), sb("whole", [1, SEG]), sb("f_in", [1, SEG]), sb("g_in", [1, SEG])
                carry = sb("carry", [1, 2, SEG])
                carry_col = sb("carry_col", [SEG, 2])

                @block.sync
                def _(sp):
                    for h in range(HEADS):
                        sp.dma_start(dq_i[h * ITERS:(h + 1) * ITERS, :], dst_line).then_inc(m_in, 16)
                    sp.dma_start(hm[:], head_mask).then_inc(m_in, 16)

                @block.tensor
                def _(pe):
                    for b in range(2 * TG):
                        last = pe.transpose(psum[b // 4][0:SEG, (b % 4) * P:(b % 4 + 1) * P],
                                            a_edge[:, b].rearrange("p h q -> p (h q)"), id_sb[:])
                    last.then_inc(m_t, 1)
                    pe.wait_ge(m_dve, 1)
                    for k, c in enumerate((run[:, CHUNK - 1:CHUNK], top_[:, 0:1], dq[:, 0:1], dq[:, CHUNK - 1:CHUNK])):
                        last = pe.transpose(psum[2][0:1, k * P:k * P + SEG], c, id_sb[0:SEG, 0:SEG])
                    last.then_inc(m_t, 1)
                    pe.wait_ge(m_dve, 2)
                    for k in range(2):
                        last = pe.transpose(psum[3][0:SEG, k:k + 1], carry[:, k, :], id_sb[0:1, 0:1])
                    last.then_inc(m_t, 1)
                    pe.wait_ge(m_act, 3)
                    for b in range(2 * TG):
                        last = pe.transpose(psum[4 + b // 4][:, (b % 4) * P:(b % 4) * P + SEG], a_seg[:, b * P:(b + 1) * P],
                                            id_sb[0:SEG, 0:SEG])
                    last.then_inc(m_t, 1)

                @block.scalar
                def _(act):
                    act.wait_ge(m_t, 1)
                    for k in range(2):
                        nc.scalar.activation(a_seg[:, k * 512:(k + 1) * 512], psum[k][0:SEG, :], ACT.Copy).then_inc(m_act, 1)
                    act.wait_ge(m_dve, 3)
                    nc.scalar.activation(a_seg[:], other[:], ACT.Exp).then_inc(m_act, 1)
                    act.wait_ge(m_t, 4)
                    for b in range(2 * TG):
                        nc.scalar.activation(ex_edge[:, b].rearrange("p h q -> p (h q)"),
                                             psum[4 + b // 4][:, (b % 4) * P:(b % 4) * P + SEG], ACT.Copy)

                @block.vector
                def _(dve):
                    n = [0]

                    def then(ins):
                        ins.then_inc(m_ev, 1)
                        n[0] += 1
                        dve.wait_ge(m_ev, n[0])

                    v = nc.vector
                    dve.wait_ge(m_in, 16 * (HEADS + 1))
                    v.memset(step[:], -BIG)
                    then(v.tensor_copy(dq[:], dq_i[:]))
                    then(v.tensor_tensor(step[:, 1:CHUNK], dq[:, 1:CHUNK], dq[:, 0:CHUNK - 1], ALU.is_equal))
                    then(v.tensor_scalar(step[:, 1:CHUNK], step[:, 1:CHUNK], 1.0, BIG, ALU.subtract, ALU.mult))
                    dve.wait_ge(m_act, 2)
                    then(v.tensor_tensor_scan(run[:], step[:, 0:CHUNK], a_seg[:], -BIG, ALU.add, ALU.max))
                    v.tensor_tensor_scan(top_[:, ::-1], step[:, 1:CHUNK + 1][:, ::-1], run[:, ::-1], -BIG, ALU.add,
                                         ALU.max).then_inc(m_dve, 1)
                    dve.wait_ge(m_t, 2)
                    then(v.tensor_copy(ends[:], psum[2][0:1, :].rearrange("p (k s) -> p k s", k=4)[:, :, 0:SEG]))
                    last_max, first_max, first, last = (ends[:, k, :] for k in range(4))
                    v.memset(cont[:], -BIG)
                    then(v.tensor_tensor(whole[:], first, last, ALU.is_equal))
                    then(v.tensor_tensor(cont[:, 1:], first[:, 1:], last[:, 0:SEG - 1], ALU.is_equal))
                    v.tensor_scalar(whole[:], whole[:], 1.0, BIG, ALU.subtract, ALU.mult)
                    then(v.tensor_scalar(cont[:, 1:], cont[:, 1:], 1.0, BIG, ALU.subtract, ALU.mult))
                    then(v.tensor_tensor(cont[:], cont[:], hm[:], ALU.add))
                    v.memset(carry[:], -BIG)
                    v.tensor_tensor(f_in[:, 1:], whole[:, 0:SEG - 1], cont[:, 1:], ALU.add)
                    then(v.tensor_tensor(g_in[:, 1:], last_max[:, 0:SEG - 1], cont[:, 1:], ALU.add))
                    then(v.tensor_tensor_scan(carry[:, 0, 1:], f_in[:, 1:], g_in[:, 1:], -BIG, ALU.add, ALU.max))
                    v.tensor_tensor(f_in[:, 0:SEG - 1], whole[:, 1:], cont[:, 1:], ALU.add)
                    then(v.tensor_tensor(g_in[:, 0:SEG - 1], first_max[:, 1:], cont[:, 1:], ALU.add))
                    v.tensor_tensor_scan(carry[:, 1, 0:SEG - 1][:, ::-1], f_in[:, 0:SEG - 1][:, ::-1],
                                         g_in[:, 0:SEG - 1][:, ::-1], -BIG, ALU.add, ALU.max).then_inc(m_dve, 1)
                    dve.wait_ge(m_t, 3)
                    then(v.tensor_copy(carry_col[:], psum[3][0:SEG, 0:2]))
                    for k, c in enumerate((0, CHUNK - 1)):
                        then(v.tensor_scalar(other[:], dq[:], dq[:, c:c + 1], 1.0, ALU.is_equal, ALU.subtract))
                        then(v.tensor_scalar(other[:], other[:], BIG, carry_col[:, k:k + 1], ALU.mult, ALU.add))
                        then(v.tensor_tensor(top_[:], top_[:], other[:], ALU.max))
                    v.tensor_tensor(other[:], a_seg[:], top_[:], ALU.subtract).then_inc(m_dve, 1)

        with ExitStack() as ctx:
            sem = sem_in(ctx)
            stages3 = ["e_ex", "e_sb", "sel_sb", "agg_ps", "agg_sb", "den_sb", "rden_sb", "nrm_sb", "T_s", "T_v", "Ts_sb",
                       "Tv_sb", "p_ps", "u_ready", "bn", "mv", "q", "rstd", "x1_ready", "idx_eq", "idx_ready", "prime"]
            s3 = {n: sem("a0_" + n) for n in stages3}
            ld3 = [sem(f"a0_ld{u}") for u in range(2)]
            gi3 = [sem(f"a0_gi{u}") for u in range(2)]
            xd3 = [top_sem(f"a0_xd{u}") for u in range(2)]
            st3 = [sem(f"a0_st{u}") for u in range(2)]
            sc3 = [top_sem(f"a0_sc{u}") for u in range(2)]
            primed_3 = sem("primed_3")

            with nc.Block() as block:
                sb = sb_in(ctx)
                two = lambda name, shape, dt=F32: [sb(f"{name}{u}", shape, dt) for u in range(2)]
                hh = two("hh", [P, TG, D])
                exg = two("exg", [P, TG, HEADS])
                e = two("e", [P, TG, AGG])
                xd = two("xd", [P, TG, D])
                didx = two("didx3", [P, TG], I32)
                dcol_i, dcol = two("dcol_i", [P, TG + 1], I32), two("dcol", [P, TG + 1])
                dnext = two("dnext", [P, TG], I32)
                dline = two("dline", [P, GROUP], I32)
                tidx_f, tidx = two("tidx_f", [P, TG]), two("tidx", [P, TG], I32)
                sel, sel_c = two("sel", [P, TG, P]), two("sel_c", [P, TG, P])
                agg = two("agg", [P, TG, AGG])
                den, rden = two("den", [P, TG, HEADS]), two("rden", [P, TG, HEADS])
                nrm = two("nrm", [P, TG, D])
                Ts, Tv = two("Ts3", [64, GROUP]), two("Tv3", [96, GROUP])
                uu, x1d = two("uu", [P, TG, D]), two("x1d", [P, TG, D])
                st, mv = two("st", [P, TG, 6]), two("mv3", [P, TG, 2])
                q, r = two("q3", [P, TG]), two("r3", [P, TG])

                @block.sync
                def _(sp):
                    prime(sp, s3.values())
                    sp.sem_inc(primed_3, 1)
                    for u in range(2):
                        sp.dma_start(x1d[u][0:16, 0, :], x[0:16, :]).then_inc(st3[u], 16)
                    with sp.Fori(0, ITERS) as i:
                        for u in range(2):
                            g1 = bass.ds(2 * i + u, 1)
                            two_d = "a p t -> (a p) t"
                            sp.wait_ge(s3["u_ready"], 2 * i + 1)
                            sp.dma_start(didx[u][:], dst_idx[g1].rearrange(two_d)).then_inc(gi3[u], 16)
                            sp.wait_ge(s3["e_sb"], 2 * i + 1)
                            sp.dma_start(hh[u][:].rearrange("p t d -> p (t d)"), h_rows[g1].rearrange(two_d)).then_inc(ld3[u], 16)
                            sp.wait_ge(s3["sel_sb"], 2 * i + 1)
                            sp.wait_ge(s3["idx_ready"], 2 * i + 1)
                            sp.dma_start(dcol_i[u][:], dst_cols[g1].rearrange(two_d)).then_inc(ld3[u], 16)
                            sp.dma_start(dnext[u][:], dst_next[g1].rearrange(two_d)).then_inc(ld3[u], 16)
                            sp.dma_start(dline[u][:], dst_line[bass.ds(i, 1), u * GROUP:(u + 1) * GROUP].broadcast_to([P, GROUP])).then_inc(ld3[u], 16)

                @block.gpsimd
                def _(pool):
                    pool.wait_ge(primed_3, 1)
                    for u in range(2):
                        pool.dma_start(x1d[u][0:16, 1, :], x[0:16, :]).then_inc(sc3[u], 16)
                    with pool.Fori(0, ITERS) as i:
                        for u in range(2):
                            pool.wait_ge(s3["u_ready"], 2 * i + 1)
                            pool.wait_ge(gi3[u], 16 * i + 16)
                            pool.sem_inc(go, 1)
                            for t in range(TG):
                                pool.indirect_dma_start(out=xd[u][:, t, :], out_offset=None, in_=x,
                                                        in_offset=bass.IndirectOffsetOnAxis(ap=didx[u][:, t:t + 1], axis=0)
                                                        ).then_inc(xd3[u], 16)
                        for u in range(2):
                            pool.wait_ge(s3["q"], 2 * i + u + 2)
                            pool.tensor_tensor(r[u][:], q[u][:], half[:, 0:TG], ALU.pow).then_inc(s3["rstd"], 1)
                        for u in range(2):
                            pool.wait_ge(s3["x1_ready"], 2 * i + u + 2)
                            pool.wait_ge(s3["idx_ready"], 2 * i + u + 2)
                            pool.sem_inc(go, 1)
                            for t in range(TG):
                                pool.indirect_dma_start(out=x1, in_=x1d[u][:, t, :], in_offset=None,
                                                        out_offset=bass.IndirectOffsetOnAxis(ap=tidx[u][:, t:t + 1], axis=0),
                                                        bounds_check=NP - 1, oob_is_err=False).then_inc(sc3[u], 16)
                    for u in range(2):
                        pool.wait_ge(sc3[u], 64 * ITERS + 16)

                @block.tensor
                def _(pe):
                    pe.wait_ge(primed_3, 1)
                    with pe.Fori(0, ITERS) as i:
                        new = lambda u: 2 * i + u + 2
                        for u in range(2):
                            pe.wait_ge(s3["e_sb"], new(u))
                            pe.wait_ge(s3["sel_sb"], new(u))
                            for t in range(TG):
                                o = psum[4 * u + t % 2][:, 0:AGG]
                                n = 8 * i + 4 * u + t
                                prev = agg[u][:, t - 1, :] if t else agg[1 - u][:, TG - 1, :]
                                if t >= 2 or True:
                                    pass
                                pe.wait_ge(s3["agg_sb"], n + 1)
                                pe.matmul(o, sel[u][:, t, :], e[u][:, t, :], start=True, stop=False)
                                pe.matmul(o, sel_c[u][:, t, :], prev, start=False, stop=True).then_inc(s3["agg_ps"], 1)
                        for u in range(2):
                            pe.wait_ge(s3["nrm_sb"], new(u))
                            for bank, c, n, freed, done in ((2, 0, 64, "u_ready", "T_s"), (3, CS, 96, "u_ready", "T_v")):
                                pe.wait_ge(s3[freed], 2 * i + 1)
                                pe.sem_inc(go, 1)
                                for t in range(TG):
                                    last = pe.transpose(psum[4 * u + bank][0:n, t * P:(t + 1) * P], nrm[u][:, t, c:c + n], id_sb[:])
                                last.then_inc(s3[done], 1)
                        for u in range(2):
                            pe.wait_ge(s3["Ts_sb"], new(u))
                            pe.wait_ge(s3["Tv_sb"], new(u))
                            for t in range(TG):
                                o = psum[4 * u + 2 + t // 2][:, (t % 2) * D:(t % 2 + 1) * D]
                                ee = slice(t * P, (t + 1) * P)
                                pe.matmul(o[:, 0:CS], Ts[u][:, ee], W("proj_s"), start=True, stop=False, skip_group_check=True)
                                last = pe.matmul(o[:, CS:D], Tv[u][:, ee], W("proj_v"), start=False, stop=True, skip_group_check=True)
                            last.then_inc(s3["p_ps"], 1)

                @block.scalar
                def _(act):
                    act.wait_ge(primed_3, 1)
                    with act.Fori(0, ITERS) as i:
                        new = lambda u: 2 * i + u + 2
                        for u in range(2):
                            act.wait_ge(s3["nrm_sb"], 2 * i + 1)
                            for t in range(TG):
                                act.wait_ge(s3["agg_ps"], 8 * i + 4 * u + t + 2)
                                nc.scalar.activation(agg[u][:, t, :], psum[4 * u + t % 2][:, 0:AGG], ACT.Copy).then_inc(s3["agg_sb"], 1)
                        for u in range(2):
                            act.wait_ge(s3["T_s"], new(u))
                            act.wait_ge(s3["p_ps"], 2 * i + 1)
                            nc.scalar.activation(Ts[u][:], psum[4 * u + 2][0:64, :], ACT.Copy).then_inc(s3["Ts_sb"], 1)
                            act.wait_ge(s3["T_v"], new(u))
                            nc.scalar.activation(Tv[u][:], psum[4 * u + 3][0:96, :], ACT.Copy).then_inc(s3["Tv_sb"], 1)
                        for u in range(2):
                            act.wait_ge(s3["x1_ready"], new(u))
                            act.dma_start(x1_dst[bass.ds(2 * i + u, 1)].rearrange("a p t -> (a p) t"),
                                          x1d[u][:].rearrange("p t d -> p (t d)")).then_inc(st3[u], 16)
                    for u in range(2):
                        act.wait_ge(st3[u], 16 * ITERS + 16)

                @block.vector
                def _(dve):
                    nc.vector.memset(agg[1][:], 0.0).then_inc(s3["prime"], 1)
                    dve.wait_ge(s3["prime"], 2)
                    dve.wait_ge(primed_3, 1)
                    v = nc.vector
                    with dve.Fori(0, ITERS) as i:
                        new = lambda u: 2 * i + u + 2
                        for u in range(2):
                            dve.wait_ge(ld3[u], 64 * i + 64)
                            dve.wait_ge(s3["agg_ps"], 8 * i + 1)
                            v.tensor_copy(dcol[u][:], dcol_i[u][:])
                            v.tensor_tensor(tidx_f[u][:], dcol_i[u][:, 1:], dnext[u][:], ALU.is_equal)
                            v.tensor_scalar(exg[u][:], ex_edge[:, TG * u:TG * (u + 1), :, bass.ds(i, 1)].rearrange("p t h o -> p t (h o)"),
                                            1.0, None, ALU.mult).then_inc(s3["e_ex"], 1)
                            dve.wait_ge(s3["e_ex"], new(u))
                            dve.wait_ge(sc3[u], 64 * i + 16)
                            v.scalar_tensor_tensor(tidx[u][:], tidx_f[u][:], float(SKIP), dcol[u][:, 1:], ALU.mult, ALU.add
                                                   ).then_inc(s3["idx_ready"], 1)
                            for t in range(TG):
                                line = dline[u][:, t * P:(t + 1) * P]
                                v.tensor_scalar(sel[u][:, t, :], line, dcol[u][:, t + 1:t + 2], None, ALU.is_equal)
                                last = v.tensor_scalar(sel_c[u][:, t, :], line, dcol[u][:, t:t + 1], V("last_row", P),
                                                       ALU.is_equal, ALU.mult)
                            last.then_inc(s3["sel_sb"], 1)
                            v.tensor_tensor(e[u][:, :, 0:CS].rearrange("p t (h a) -> p t h a", h=HEADS),
                                            hh[u][:, :, 0:CS].rearrange("p t (h a) -> p t h a", h=HEADS),
                                            exg[u][:].unsqueeze(3).broadcast_to([P, TG, HEADS, 16]), ALU.mult)
                            for c in range(3):
                                cc = slice(CS + c * CV, CS + (c + 1) * CV)
                                v.tensor_tensor(e[u][:, :, cc].rearrange("p t (h a) -> p t h a", h=HEADS),
                                                hh[u][:, :, cc].rearrange("p t (h a) -> p t h a", h=HEADS),
                                                exg[u][:].unsqueeze(3).broadcast_to([P, TG, HEADS, 8]), ALU.mult)
                            v.tensor_copy(e[u][:, :, D:AGG], exg[u][:]).then_inc(s3["e_sb"], 1)
                        for u in range(2):
                            dve.wait_ge(s3["agg_sb"], 8 * i + 4 * u + 5)
                            v.tensor_scalar(den[u][:], agg[u][:, :, D:AGG], 1e-16, None, ALU.add).then_inc(s3["den_sb"], 1)
                            dve.wait_ge(s3["den_sb"], new(u))
                            v.reciprocal(rden[u][:], den[u][:]).then_inc(s3["rden_sb"], 1)
                            dve.wait_ge(s3["rden_sb"], new(u))
                            dve.wait_ge(s3["T_v"], 2 * i + 1)
                            dve.wait_ge(s3["agg_ps"], 8 * i + 4 * u + 5)
                            v.tensor_tensor(nrm[u][:, :, 0:CS].rearrange("p t (h a) -> p t h a", h=HEADS),
                                            agg[u][:, :, 0:CS].rearrange("p t (h a) -> p t h a", h=HEADS),
                                            rden[u][:].unsqueeze(3).broadcast_to([P, TG, HEADS, 16]), ALU.mult)
                            for c in range(3):
                                cc = slice(CS + c * CV, CS + (c + 1) * CV)
                                last = v.tensor_tensor(nrm[u][:, :, cc].rearrange("p t (h a) -> p t h a", h=HEADS),
                                                       agg[u][:, :, cc].rearrange("p t (h a) -> p t h a", h=HEADS),
                                                       rden[u][:].unsqueeze(3).broadcast_to([P, TG, HEADS, 8]), ALU.mult)
                            last.then_inc(s3["nrm_sb"], 1)
                        for u in range(2):
                            dve.wait_ge(s3["p_ps"], new(u))
                            dve.wait_ge(xd3[u], 64 * i + 64)
                            for k in range(2):
                                last = v.scalar_tensor_tensor(
                                    uu[u][:, 2 * k:2 * k + 2, :], xd[u][:, 2 * k:2 * k + 2, :], 2.0,
                                    psum[4 * u + 2 + k][:, 0:2 * D].rearrange("p (t d) -> p t d", t=2), ALU.mult, ALU.add)
                            last.then_inc(s3["u_ready"], 1)
                            dve.wait_ge(s3["u_ready"], new(u))
                            for t in range(TG):
                                last = v.bn_stats(st[u][:, t, :], uu[u][:, t, :])
                            last.then_inc(s3["bn"], 1)
                            dve.wait_ge(s3["bn"], new(u))
                            dve.sem_inc(go, 1)
                            for t in range(TG):
                                last = v.bn_aggr(mv[u][:, t, :], st[u][:, t, :])
                            last.then_inc(s3["mv"], 1)
                            dve.wait_ge(s3["mv"], new(u))
                            v.tensor_scalar(q[u][:], mv[u][:, :, 1], EPS, None, ALU.add).then_inc(s3["q"], 1)
                        for u in range(2):
                            dve.wait_ge(s3["rstd"], new(u))
                            dve.wait_ge(st3[u], 16 * i + 16)
                            dve.wait_ge(sc3[u], 64 * i + 16)
                            for t in range(TG):
                                last = v.tensor_scalar(x1d[u][:, t, :], uu[u][:, t, :], mv[u][:, t, 0:1], r[u][:, t:t + 1],
                                                       ALU.subtract, ALU.mult)
                            last.then_inc(s3["x1_ready"], 1)

        with ExitStack() as ctx:
            sem = sem_in(ctx)
            stages4 = ["T_s", "T_v", "Ts_sb", "Tv_sb", "xs_ps", "xv_ps", "hid_ps", "hid_sb", "w_s01", "w_s23", "w_vs",
                       "w_vv", "q_s01", "q_s23", "q_vs", "q_vv", "m_s01", "m_s23", "m_vs", "m_vv", "msg_ps0", "msg_ps1",
                       "msg_sb0", "msg_sb1", "dcol_sb", "sel_sb", "idx_ready", "agg_ps", "agg_sb", "N_s", "N_v", "Ns_sb", "Nv_sb",
                       "self_ps", "o_sb", "gates_sb", "gv_ready", "u_ready", "bn", "mv", "q", "rstd", "out_ready", "prime"]
            s4 = {n: sem("e1_" + n) for n in stages4}
            ix4, y4, em4, ld4 = ([sem(f"e1_{n}{u}") for u in range(2)] for n in ("ix", "y", "em", "ld"))
            xg4, sc4 = ([top_sem(f"e1_{n}{u}") for u in range(2)] for n in ("xg", "sc"))
            primed_4 = sem("primed_4")

            with nc.Block() as block:
                sb = sb_in(ctx)
                two = lambda name, shape, dt=F32: [sb(f"{name}{u}", shape, dt) for u in range(2)]
                sidx = two("sidx4", [P, TG], I32)
                xg = two("xg4", [P, TG, D])
                ybc = two("ybc4", [P, 4, GROUP])
                emb = two("emb", [8, GROUP])
                Ts, Tv, hid = two("Ts4", [64, GROUP]), two("Tv4", [96, GROUP]), two("hid", [64, GROUP])
                m_s01, m_s23, m_vs, m_vv = (two("n_" + n, [128 if n[0] == "s" else 96, GROUP]) for n in ("s01", "s23", "vs", "vv"))
                msg = two("msg", [P, TG, MSG])
                dcol_i, dcol = two("dcol_i4", [P, TG + 1], I32), two("dcol4", [P, TG + 1])
                dnext = two("dnext4", [P, TG], I32)
                dline = two("dline4", [P, GROUP], I32)
                tidx_f, tidx = two("tidx_f4", [P, TG]), two("tidx4", [P, TG], I32)
                sel, sel_c = two("sel4", [P, TG, P]), two("sel_c4", [P, TG, P])
                agg = two("agg4", [P, TG, MSG])
                x1d = two("x1d4", [P, TG, D])
                Ns, Nv = two("Ns", [64, GROUP]), two("Nv", [96, GROUP])
                o_sb = two("o_sb", [P, TG, MSG])
                gates, gv = two("gates4", [P, TG, 96]), two("gv4", [P, TG, CV3])
                uu, od = two("uu4", [P, TG, D]), two("od", [P, TG, D])
                st, mv = two("st4", [P, TG, 6]), two("mv4", [P, TG, 2])
                q, r = two("q4", [P, TG]), two("r4", [P, TG])

                @block.sync
                def _(sp):
                    prime(sp, s4.values())
                    sp.sem_inc(primed_4, 1)
                    with sp.Fori(0, ITERS) as i:
                        two_d = "a p t -> (a p) t"
                        for u in range(2):
                            sp.wait_ge(s4["T_v"], 2 * i + 1)
                            sp.dma_start(sidx[u][:], src_idx[bass.ds(2 * i + u, 1)].rearrange(two_d)).then_inc(ix4[u], 16)
                        for u in range(2):
                            cols = bass.ds(i * CHUNK + u * GROUP, GROUP)
                            sp.wait_ge(s4["hid_ps"], 2 * i + 1)
                            sp.dma_start(emb[u][:], edge_rows[EMB:EMB + 8, cols]).then_inc(em4[u], 16)
                            sp.wait_ge(s4["q_vv"], 2 * i + 1)
                            for k, (row, n, rep) in enumerate(((Y0, 2, 64), (YX + 1, 2, 64), (Y0, 1, 96), (YX, 3, 32))):
                                sp.dma_start(ybc[u][0:n * rep, k, :],
                                             edge_rows[row:row + n, cols].unsqueeze(0).broadcast_to([rep, n, GROUP])
                                             ).then_inc(y4[u], 16)
                        for u in range(2):
                            g1 = bass.ds(2 * i + u, 1)
                            sp.wait_ge(s4["sel_sb"], 2 * i + 1)
                            sp.wait_ge(s4["idx_ready"], 2 * i + 1)
                            sp.dma_start(dcol_i[u][:], dst_cols[g1].rearrange(two_d)).then_inc(ld4[u], 16)
                            sp.dma_start(dnext[u][:], dst_next[g1].rearrange(two_d)).then_inc(ld4[u], 16)
                            sp.dma_start(dline[u][:], dst_line[bass.ds(i, 1), u * GROUP:(u + 1) * GROUP].broadcast_to([P, GROUP])).then_inc(ld4[u], 16)
                            sp.wait_ge(s4["u_ready"], 2 * i + 1)
                            sp.dma_start(x1d[u][:].rearrange("p t d -> p (t d)"), x1_dst[g1].rearrange(two_d)).then_inc(ld4[u], 16)

                @block.gpsimd
                def _(pool):
                    pool.wait_ge(primed_4, 1)
                    for u in range(2):
                        pool.dma_start(od[u][0:16, 0, :], x[0:16, :]).then_inc(sc4[u], 16)
                    with pool.Fori(0, ITERS) as i:
                        for u in range(2):
                            pool.wait_ge(s4["T_v"], 2 * i + 1)
                            pool.wait_ge(ix4[u], 16 * i + 16)
                            pool.sem_inc(go, 1)
                            for t in range(TG):
                                pool.indirect_dma_start(out=xg[u][:, t, :], out_offset=None, in_=x1,
                                                        in_offset=bass.IndirectOffsetOnAxis(ap=sidx[u][:, t:t + 1], axis=0)
                                                        ).then_inc(xg4[u], 16)
                        for u in range(2):
                            pool.wait_ge(s4["q"], 2 * i + u + 2)
                            pool.tensor_tensor(r[u][:], q[u][:], half[:, 0:TG], ALU.pow).then_inc(s4["rstd"], 1)
                        for u in range(2):
                            pool.wait_ge(s4["out_ready"], 2 * i + u + 2)
                            pool.wait_ge(s4["idx_ready"], 2 * i + u + 2)
                            pool.sem_inc(go, 1)
                            for t in range(TG):
                                pool.indirect_dma_start(out=out, in_=od[u][:, t, :], in_offset=None,
                                                        out_offset=bass.IndirectOffsetOnAxis(ap=tidx[u][:, t:t + 1], axis=0),
                                                        bounds_check=NP - 1, oob_is_err=False).then_inc(sc4[u], 16)
                    for u in range(2):
                        pool.wait_ge(sc4[u], 64 * ITERS + 16)

                @block.tensor
                def _(pe):
                    pe.wait_ge(primed_4, 1)
                    with pe.Fori(0, ITERS) as i:
                        B = lambda u, b: psum[4 * u + b]
                        new = lambda u: 2 * i + u + 2
                        old = 2 * i + 1

                        def job(u, bank, waits, w, rhs, done):
                            for name, value in waits:
                                pe.wait_ge(s4[name], value)
                            pe.matmul(B(u, bank)[0:w.shape[1], 0:GROUP], w, rhs, start=True, stop=True).then_inc(s4[done], 1)

                        for u in range(2):
                            pe.wait_ge(xg4[u], 64 * i + 64)
                            for bank, c, n, done in ((0, 0, 64, "T_s"), (1, CS, 96, "T_v")):
                                pe.wait_ge(s4["o_sb"], old)
                                pe.sem_inc(go, 1)
                                for t in range(TG):
                                    last = pe.transpose(B(u, bank)[0:n, t * P:(t + 1) * P], xg[u][:, t, c:c + n], id_sb[:])
                                last.then_inc(s4[done], 1)
                        for u in range(2):
                            pe.wait_ge(em4[u], 16 * i + 16)
                            job(u, 2, [], W("fc1"), emb[u][:], "hid_ps")
                        for u in range(2):
                            job(u, 3, [("Ts_sb", new(u))], W("l1_xs"), Ts[u][:], "xs_ps")
                        for u in range(2):
                            job(u, 0, [("Tv_sb", new(u))], W("l1_xv"), Tv[u][:], "xv_ps")
                        for u in range(2):
                            job(u, 1, [("hid_sb", new(u))], W("fc2_s01"), hid[u][:], "w_s01")
                        for u in range(2):
                            job(u, 2, [], W("fc2_s23"), hid[u][:], "w_s23")
                        for u in range(2):
                            job(u, 3, [("q_s23", new(u))], W("fc2_vs"), hid[u][:], "w_vs")
                        for u in range(2):
                            job(u, 0, [("q_vv", new(u))], W("fc2_vv"), hid[u][:], "w_vv")
                        for u in range(2):
                            pe.wait_ge(s4["m_s01"], new(u))
                            pe.wait_ge(s4["m_s23"], new(u))
                            pe.wait_ge(s4["m_vs"], new(u))
                            pe.wait_ge(s4["m_vv"], new(u))
                            for t in range(TG):
                                o = B(u, 1 + t // 2)[:, (t % 2) * MSG:(t % 2 + 1) * MSG]
                                ee = slice(t * P, (t + 1) * P)
                                pe.matmul(o[:, 0:128], m_s01[u][:, ee], W("l1_s01"), start=True, stop=False, skip_group_check=True)
                                pe.matmul(o[:, 128:192], m_s23[u][:, ee], W("l1_s23"), start=False, stop=False, skip_group_check=True)
                                pe.matmul(o[:, 96:192], m_vs[u][:, ee], W("l1_vs"), start=False, stop=False, skip_group_check=True)
                                last = pe.matmul(o[:, 0:96], m_vv[u][:, ee], W("l1_vv"), start=False, stop=True, skip_group_check=True)
                                if t == 1:
                                    last.then_inc(s4["msg_ps0"], 1)
                            last.then_inc(s4["msg_ps1"], 1)
                        for u in range(2):
                            pe.wait_ge(ld4[u], 64 * i + 64)
                            for bank, c, n, done in ((3, 0, 64, "N_s"), (0, CS, 96, "N_v")):
                                pe.sem_inc(go, 1)
                                for t in range(TG):
                                    last = pe.transpose(B(u, bank)[0:n, t * P:(t + 1) * P], x1d[u][:, t, c:c + n], id_sb[:])
                                last.then_inc(s4[done], 1)
                        for u in range(2):
                            pe.wait_ge(s4["msg_sb1"], new(u))
                            pe.wait_ge(s4["sel_sb"], new(u))
                            for t in range(TG):
                                o = B(u, 1 + t % 2)[:, 0:MSG]
                                n = 8 * i + 4 * u + t
                                prev = agg[u][:, t - 1, :] if t else agg[1 - u][:, TG - 1, :]
                                pe.wait_ge(s4["agg_sb"], n + 1)
                                pe.matmul(o, sel[u][:, t, :], msg[u][:, t, :], start=True, stop=False)
                                pe.matmul(o, sel_c[u][:, t, :], prev, start=False, stop=True).then_inc(s4["agg_ps"], 1)
                        for u in range(2):
                            pe.wait_ge(s4["Ns_sb"], new(u))
                            pe.wait_ge(s4["Nv_sb"], new(u))
                            for t in range(TG):
                                o = B(u, 3 if t < 2 else 0)[:, (t % 2) * MSG:(t % 2 + 1) * MSG]
                                ee = slice(t * P, (t + 1) * P)
                                pe.matmul(o[:, 0:96], Ns[u][:, ee], W("self_s"), start=True, stop=False, skip_group_check=True)
                                last = pe.matmul(o[:, 96:192], Nv[u][:, ee], W("self_v"), start=False, stop=True, skip_group_check=True)
                            last.then_inc(s4["self_ps"], 1)

                @block.scalar
                def _(act):
                    act.wait_ge(primed_4, 1)
                    with act.Fori(0, ITERS) as i:
                        B = lambda u, b: psum[4 * u + b]
                        new = lambda u: 2 * i + u + 2
                        old = 2 * i + 1
                        for u in range(2):
                            act.wait_ge(s4["T_s"], new(u))
                            act.wait_ge(s4["xv_ps"], old)
                            nc.scalar.activation(Ts[u][:], B(u, 0)[0:64, :], ACT.Copy).then_inc(s4["Ts_sb"], 1)
                            act.wait_ge(s4["T_v"], new(u))
                            nc.scalar.activation(Tv[u][:], B(u, 1)[0:96, :], ACT.Copy).then_inc(s4["Tv_sb"], 1)
                        for u in range(2):
                            act.wait_ge(s4["hid_ps"], new(u))
                            act.wait_ge(s4["w_vv"], old)
                            nc.scalar.activation(hid[u][:], B(u, 2)[0:64, :], ACT.Silu, bias=V("b_fc1", 64)).then_inc(s4["hid_sb"], 1)
                        for u in range(2):
                            act.wait_ge(s4["agg_ps"], 8 * i + 1)
                            act.wait_ge(s4["msg_ps0"], new(u))
                            nc.scalar.activation(msg[u][:, 0:2, :].rearrange("p t f -> p (t f)"), B(u, 1)[:, 0:2 * MSG], ACT.Copy).then_inc(s4["msg_sb0"], 1)
                            act.wait_ge(s4["msg_ps1"], new(u))
                            nc.scalar.activation(msg[u][:, 2:4, :].rearrange("p t f -> p (t f)"), B(u, 2)[:, 0:2 * MSG], ACT.Copy).then_inc(s4["msg_sb1"], 1)
                        for u in range(2):
                            act.wait_ge(s4["N_s"], new(u))
                            act.wait_ge(s4["self_ps"], old)
                            nc.scalar.activation(Ns[u][:], B(u, 3)[0:64, :], ACT.Copy).then_inc(s4["Ns_sb"], 1)
                            act.wait_ge(s4["N_v"], new(u))
                            nc.scalar.activation(Nv[u][:], B(u, 0)[0:96, :], ACT.Copy).then_inc(s4["Nv_sb"], 1)
                        for u in range(2):
                            act.wait_ge(s4["o_sb"], old)
                            for t in range(TG):
                                act.wait_ge(s4["agg_ps"], 8 * i + 4 * u + t + 2)
                                nc.scalar.activation(agg[u][:, t, :], B(u, 1 + t % 2)[:, 0:MSG], ACT.Copy).then_inc(s4["agg_sb"], 1)
                        for u in range(2):
                            act.wait_ge(s4["o_sb"], new(u))
                            act.wait_ge(s4["u_ready"], old)
                            nc.scalar.activation(gates[u][:], o_sb[u][:, :, 0:96], ACT.Silu).then_inc(s4["gates_sb"], 1)

                @block.vector
                def _(dve):
                    v = nc.vector
                    v.memset(agg[1][:], 0.0).then_inc(s4["prime"], 1)
                    dve.wait_ge(s4["prime"], 2)
                    dve.wait_ge(primed_4, 1)
                    with dve.Fori(0, ITERS) as i:
                        B = lambda u, b: psum[4 * u + b]
                        new = lambda u: 2 * i + u + 2
                        old = 2 * i + 1
                        for u in range(2):
                            dve.wait_ge(y4[u], 64 * i + 64)
                            dve.wait_ge(s4["xs_ps"], new(u))
                            dve.wait_ge(s4["msg_ps1"], old)
                            v.tensor_tensor(m_s01[u][:], ybc[u][:, 0, :], B(u, 3)[:, :], ALU.mult).then_inc(s4["q_s01"], 1)
                            v.tensor_tensor(m_s23[u][:], ybc[u][:, 1, :], B(u, 3)[:, :], ALU.mult).then_inc(s4["q_s23"], 1)
                            dve.wait_ge(s4["xv_ps"], new(u))
                            v.tensor_tensor(m_vs[u][:], ybc[u][0:96, 2, :], B(u, 0)[0:96, :], ALU.mult).then_inc(s4["q_vs"], 1)
                            v.tensor_tensor(m_vv[u][:], ybc[u][0:96, 3, :], B(u, 0)[0:96, :], ALU.mult).then_inc(s4["q_vv"], 1)
                        for u in range(2):
                            dve.wait_ge(ld4[u], 64 * i + 64)
                            dve.wait_ge(s4["agg_ps"], 8 * i + 1)
                            v.tensor_copy(dcol[u][:], dcol_i[u][:])
                            v.tensor_tensor(tidx_f[u][:], dcol_i[u][:, 1:], dnext[u][:], ALU.is_equal).then_inc(s4["dcol_sb"], 1)
                            dve.wait_ge(s4["dcol_sb"], new(u))
                            dve.wait_ge(sc4[u], 64 * i + 16)
                            v.scalar_tensor_tensor(tidx[u][:], tidx_f[u][:], float(SKIP), dcol[u][:, 1:], ALU.mult, ALU.add
                                                   ).then_inc(s4["idx_ready"], 1)
                            for t in range(TG):
                                line = dline[u][:, t * P:(t + 1) * P]
                                v.tensor_scalar(sel[u][:, t, :], line, dcol[u][:, t + 1:t + 2], None, ALU.is_equal)
                                last = v.tensor_scalar(sel_c[u][:, t, :], line, dcol[u][:, t:t + 1], V("last_row", P),
                                                       ALU.is_equal, ALU.mult)
                            last.then_inc(s4["sel_sb"], 1)
                        for bank, rows, wname, bias, m, q_ok, done in (
                                (1, 128, "w_s01", "b_s01", m_s01, "q_s01", "m_s01"), (2, 128, "w_s23", "b_s23", m_s23, "q_s23", "m_s23"),
                                (3, 96, "w_vs", "b_vs", m_vs, "q_vs", "m_vs"), (0, 96, "w_vv", "b_vv", m_vv, "q_vv", "m_vv")):
                            for u in range(2):
                                dve.wait_ge(s4[wname], new(u))
                                dve.wait_ge(s4[q_ok], new(u))
                                v.scalar_tensor_tensor(m[u][:], B(u, bank)[0:rows, :], V(bias, rows), m[u][:], ALU.add, ALU.mult
                                                       ).then_inc(s4[done], 1)
                        for u in range(2):
                            dve.wait_ge(s4["self_ps"], new(u))
                            dve.wait_ge(s4["agg_sb"], 8 * i + 4 * u + 5)
                            dve.wait_ge(s4["gates_sb"], old)
                            for k in range(2):
                                last = v.tensor_tensor(o_sb[u][:, 2 * k:2 * k + 2, :].rearrange("p t f -> p (t f)"),
                                                       agg[u][:, 2 * k:2 * k + 2, :].rearrange("p t f -> p (t f)"),
                                                       B(u, 3 if k == 0 else 0)[:, 0:2 * MSG], ALU.add)
                            last.then_inc(s4["o_sb"], 1)
                        for u in range(2):
                            dve.wait_ge(s4["gates_sb"], new(u))
                            v.scalar_tensor_tensor(uu[u][:, :, 0:CS], x1d[u][:, :, 0:CS], 2.0, gates[u][:, :, 0:CS], ALU.mult, ALU.add)
                            for k in range(2):
                                tt = slice(2 * k, 2 * k + 2)
                                last = v.tensor_tensor(gv[u][:, tt, :].rearrange("p t (k c) -> p t k c", c=3),
                                                       gates[u][:, tt, CS:96].unsqueeze(3).broadcast_to([P, 2, CV, 3]),
                                                       o_sb[u][:, tt, 96:192].rearrange("p t (c k) -> p t k c", c=3), ALU.mult)
                            last.then_inc(s4["gv_ready"], 1)
                            dve.wait_ge(s4["gv_ready"], new(u))
                            v.scalar_tensor_tensor(uu[u][:, :, CS:D], x1d[u][:, :, CS:D], 2.0, gv[u][:], ALU.mult, ALU.add
                                                   ).then_inc(s4["u_ready"], 1)
                            dve.wait_ge(s4["u_ready"], new(u))
                            for t in range(TG):
                                last = v.bn_stats(st[u][:, t, :], uu[u][:, t, :])
                            last.then_inc(s4["bn"], 1)
                            dve.wait_ge(s4["bn"], new(u))
                            dve.sem_inc(go, 1)
                            for t in range(TG):
                                last = v.bn_aggr(mv[u][:, t, :], st[u][:, t, :])
                            last.then_inc(s4["mv"], 1)
                            dve.wait_ge(s4["mv"], new(u))
                            v.tensor_scalar(q[u][:], mv[u][:, :, 1], EPS, None, ALU.add).then_inc(s4["q"], 1)
                        for u in range(2):
                            dve.wait_ge(s4["rstd"], new(u))
                            dve.wait_ge(sc4[u], 64 * i + 16)
                            for t in range(TG):
                                last = v.tensor_scalar(od[u][:, t, :], uu[u][:, t, :], mv[u][:, t, 0:1], r[u][:, t:t + 1],
                                                       ALU.subtract, ALU.mult)
                            last.then_inc(s4["out_ready"], 1)


def pack_weights(np, w):
    a = np.zeros((P, WCOLS), np.float32)
    vec = np.zeros((P, len(VECS)), np.float32)

    def blk(name):
        c, r, n = COL[name]
        return a[:r, c:c + n]

    g0 = lambda n: np.asarray(w["L0_gnn_" + n])
    g1 = lambda n: np.asarray(w["L1_gnn_" + n])
    b = blk("msg_s")
    for j in range(2):
        b[:64, j::2] = g0("Ws_src")
        b[64:, j::2] = g0("Ws_dst")
    for c in range(3):
        blk("msg_v_src")[c::3, c::3] = g0("Wv_src")
        blk("msg_v_dst")[c::3, c::3] = g0("Wv_dst")
    wr = g0("W_rbf")
    ss, sv, vs, vv0, vv1 = wr[:, 0:64], wr[:, 64:128], wr[:, 128:160], wr[:, 160:192], wr[:, 192:224]
    blk("rbf_s")[1::5, 0::2] = ss
    blk("rbf_s")[0::5, 1::2] = sv
    for c in range(3):
        nxt, prv = (c + 1) % 3, (c + 2) % 3
        blk("rbf_vv0")[2 + c::5, c::3] = vv0
        blk("rbf_vs")[1::5, c::3] = vs
        blk("rbf_vv1_next")[2 + nxt::5, c::3] = vv1
        blk("rbf_vv1_prev")[2 + prv::5, c::3] = vv1
        blk("alpha_dotv")[c::3, :] = g0("W_alpha")[64:]
        blk("gate")[0::2, c::3] = g0("Wg")
        blk("val_v_sv")[1::2, c::3] = g0("Wv_val")[0:64]
        blk("val_v_vs")[c::3, c::3] = g0("Wv_val")[64:96]
        blk("val_v_next")[c::3, prv::3] = g0("Wv_val")[96:128]
        blk("val_v_prev")[c::3, nxt::3] = g0("Wv_val")[96:128]
        blk("out_dotv")[c::3, :] = g0("Ws_vlin")[64:]
        blk("out_vs")[c::3, c * 32:c * 32 + 32] = g0("Wv_vlin")[64:96]
        blk("out_next")[c::3, prv * 32:prv * 32 + 32] = g0("Wv_vlin")[96:128]
        blk("out_prev")[c::3, nxt * 32:nxt * 32 + 32] = g0("Wv_vlin")[96:128]
        blk("proj_v")[c * 32:c * 32 + 32, c::3] = g0("Wpv")
        blk("l1_xv")[c::3, c::3] = g1("W1_v")
        blk("fc2_vs")[:, c::3] = g1("fc_w2")[:, 128:160]
        blk("fc2_vv")[:, c::3] = g1("fc_w2")[:, 160:192]
        blk("l1_vs")[c::3, c * 32:c * 32 + 32] = g1("W2_v")[64:96]
        blk("l1_vv")[c::3, :] = g1("W2_s")[64:96]
        blk("self_v")[c::3, c * 32:c * 32 + 32] = g1("Wsc_v")
        for j in range(2):
            blk("val_dotv")[c::3, j::2] = g0("Ws_val")[64:]
        for name, v in (("gamma_v3", g0("gamma_v")), ("w2_vv0", g0("w2_vv0")), ("w2_vs", g0("w2_vs")),
                        ("w2_vv1", g0("w2_vv1")), ("b_vs", g1("fc_b2")[128:160]), ("b_vv", g1("fc_b2")[160:192])):
            vec[c:96:3, VCOL[name]] = v
    blk("alpha_s")[0::2, :] = g0("W_alpha")[:64]
    for j in range(2):
        blk("val_s")[0::2, j::2] = g0("Ws_val")[:64]
        blk("l1_xs")[:, j::2] = g1("W1_s")
        blk("fc2_s01")[:, j::2] = g1("fc_w2")[:, 64 * j:64 * j + 64]
        blk("fc2_s23")[:, j::2] = g1("fc_w2")[:, 64:128]
        blk("out_s23")[j::2, 32 * j:32 * j + 32] = g0("Wv_vlin")[0:64]
        blk("l1_s23")[j::2, 32 * j:32 * j + 32] = g1("W2_v")[0:64]
        vec[64 * j:64 * j + 64, VCOL["gamma_s2"]] = g0("gamma_s")
        vec[64 * j:64 * j + 64, VCOL["beta_s2"]] = g0("beta_s")
        vec[j::2, VCOL["w2_s01"]] = (g0("w2_ss"), g0("w2_sv"))[j]
        vec[j::2, VCOL["w2_s23"]] = g0("w2_sv")
        vec[j::2, VCOL["b_s01"]] = g1("fc_b2")[64 * j:64 * j + 64]
        vec[j::2, VCOL["b_s23"]] = g1("fc_b2")[64:128]
    for h in range(HEADS):
        blk("alpha_dot")[16 * h:16 * h + 16, h] = g0("alpha_dot")[0, h]
    blk("out_s01")[0::2, 0:64] = g0("Ws_vlin")[:64]
    blk("out_s01")[1::2, 64:96] = g0("Wv_vlin")[0:64]
    blk("proj_s")[:] = g0("Wps")
    blk("fc1")[:] = g1("fc_w1")
    blk("l1_s01")[0::2, 0:96] = g1("W2_s")[:64]
    blk("l1_s01")[1::2, 96:128] = g1("W2_v")[0:64]
    blk("self_s")[:] = g1("Wsc_s")
    vec[:64, VCOL["b_fc1"]] = g1("fc_b1")
    vec[P - 1, VCOL["last_row"]] = 1.0
    return a, vec


def kernel(**inputs):
    import numpy as np
    import concourse.bacc as bacc
    from concourse import mybir as mb
    from concourse.bass_utils import run_bass_kernel_spmd as run

    def padded(a, n, fill):
        a = np.asarray(a)
        return np.concatenate([a, np.full((n - a.shape[0],) + a.shape[1:], fill, a.dtype)])

    def tiles(a):
        return np.ascontiguousarray(a.reshape(GROUPS, TG, P).transpose(0, 2, 1))

    src = padded(inputs["src"], EP, 0)
    dst = padded(inputs["dst"], EP, NP - 1)
    before = tiles(np.concatenate([np.full(P, -1, np.int32), dst[:-P]]))
    last_of_tile = dst.reshape(-1, P)[:, -1]
    prev_last = np.concatenate([np.full(1, -1, np.int32), last_of_tile[:-1]]).reshape(GROUPS, 1, TG)
    dst_t = tiles(dst)
    dst_cols = np.concatenate([before[:, :, 0:1], dst_t], axis=2)
    rows = np.zeros((EROWS, EP), np.float32)
    y = np.asarray(inputs["edge_attr_4"]).T
    rows[ONE] = 1.0
    rows[Y0:Y0 + 4, :EDGES] = y
    rows[YX + 3:YX + 5, :EDGES] = y[1:3]
    rows[RBF:RBF + 16, :EDGES] = np.asarray(inputs["edge_attr_16"]).T
    rows[EMB:EMB + 8, :EDGES] = np.asarray(inputs["edge_attr_8"]).T
    weights, vectors = pack_weights(np, inputs)
    head_mask = np.zeros((1, SEG), np.float32)
    head_mask[0, ::ITERS] = -BIG
    arrays = {
        "x": padded(inputs["x"], NP, 0), "src_idx": tiles(src), "dst_idx": dst_t,
        "dst_cols": np.ascontiguousarray(dst_cols),
        "dst_next": tiles(np.concatenate([dst[1:], np.full(1, -1, np.int32)])),
        "dst_line": dst.reshape(ITERS, CHUNK), "edge_rows": rows, "weights": weights, "vectors": vectors,
        "ident": np.eye(P, dtype=np.float32), "head_mask": head_mask,
    }
    nc = bacc.Bacc("TRN2", target_bir_lowering=False, num_devices=1)
    args, named = [], {}
    for name, a in arrays.items():
        named[f"in_{name}"] = a
        args.append(nc.dram_tensor(f"in_{name}", a.shape, mb.dt.from_np(a.dtype), kind="ExternalInput").ap())
    out = nc.dram_tensor("out_rows", (NP, D), F32, kind="ExternalOutput").ap()
    build(nc, *args, out)
    r = run(nc, [named], core_ids=[0])
    return r.results[0]["out_rows"][:NODES]
```

```python
from contextlib import ExitStack

import concourse.bass as bass
from concourse import mybir

F32 = mybir.dt.float32
I32 = mybir.dt.int32
ALU = mybir.AluOpType
ACT = mybir.ActivationFunctionType

P = 128
NODES, EDGES = 50000, 25000
CS, CV, HEADS = 64, 32, 4
CV3 = 3 * CV
D = CS + CV3
TG = 4
GROUP = TG * P
ITERS = 25
CHUNK = 2 * GROUP
EP = ITERS * CHUNK
GROUPS = 2 * ITERS
NODE_ITERS = 49
NP = NODE_ITERS * CHUNK
EPS = 1e-5
BIG = 1e30
SKIP = 1 << 20
SEG = HEADS * ITERS
AGG = D + HEADS
MSG = 96 + CV3

BLOCKS = [
    ("msg_s", 128, 128), ("msg_v_src", 96, 96), ("msg_v_dst", 96, 96),
    ("rbf_s", 80, 128), ("rbf_vv0", 80, 96), ("rbf_vs", 80, 96), ("rbf_vv1_next", 80, 96), ("rbf_vv1_prev", 80, 96),
    ("alpha_s", 128, 64), ("alpha_dotv", 96, 64), ("val_s", 128, 128), ("val_dotv", 96, 128),
    ("gate", 128, 96), ("val_v_sv", 128, 96), ("val_v_vs", 96, 96), ("val_v_next", 96, 96), ("val_v_prev", 96, 96),
    ("alpha_dot", 64, 4),
    ("out_s01", 128, 96), ("out_s23", 128, 64), ("out_dotv", 96, 64), ("out_vs", 96, 96),
    ("out_next", 96, 96), ("out_prev", 96, 96), ("proj_s", 64, 64), ("proj_v", 96, 96),
    ("l1_xs", 64, 128), ("l1_xv", 96, 96), ("fc1", 8, 64), ("fc2_s01", 64, 128), ("fc2_s23", 64, 128),
    ("fc2_vs", 64, 96), ("fc2_vv", 64, 96),
    ("l1_s01", 128, 128), ("l1_s23", 128, 64), ("l1_vs", 96, 96), ("l1_vv", 96, 96),
    ("self_s", 64, 96), ("self_v", 96, 96),
]
COL, at = {}, 0
for _name, _rows, _cols in BLOCKS:
    COL[_name] = (at, _rows, _cols)
    at += _cols
WCOLS = at
VECS = ["gamma_s2", "beta_s2", "gamma_v3", "w2_s01", "w2_s23", "w2_vv0", "w2_vs", "w2_vv1",
        "b_s01", "b_s23", "b_vs", "b_vv", "b_fc1", "last_row"]
VCOL = {n: i for i, n in enumerate(VECS)}
ONE, Y0, YX, RBF, EMB = 0, 1, 2, 7, 23
EROWS = 31


def staggered(eng, iters, half, step):
    for k in range(half):
        step(0, 0, k)
    for k in range(half):
        step(0, 0, half + k)
        step(0, 1, k)
    with eng.Fori(1, iters) as i:
        for k in range(half):
            step(i, 0, k)
            step(i - 1, 1, half + k)
        for k in range(half):
            step(i, 0, half + k)
            step(i, 1, k)
    for k in range(half):
        step(iters - 1, 1, half + k)


def new(i, u):
    return 2 * i + u + 2


def wait_old(eng, sem, i, u):
    if not (isinstance(i, int) and i == 0):
        eng.wait_ge(sem, 2 * i + u)


def wait_old_sums(eng, sem, i, u):
    if not (isinstance(i, int) and i == 0):
        eng.wait_ge(sem, 8 * i + 4 * u - 3)


def build(nc, x, src_idx, dst_idx, dst_cols, dst_next, dst_line, edge_rows, weights, vectors, ident, head_mask, out):
    h_rows = nc.dram_tensor("h_rows", [GROUPS, P, TG * D], F32).ap()
    x1 = nc.dram_tensor("x1", [NP, D], F32).ap()
    x1_dst = nc.dram_tensor("x1_dst", [GROUPS, P, TG * D], F32).ap()

    with ExitStack() as top:
        def sem_in(ctx):
            made = []

            def new_sem(name):
                made.append(ctx.enter_context(nc.semaphore(name)))
                return made[-1]

            def clear():
                with nc.Block() as block:
                    @block.gpsimd
                    def _(pool):
                        for s in made:
                            pool.sem_clear(s)

            ctx.callback(clear) if ctx is not top else None
            return new_sem

        def sb_in(ctx):
            return lambda name, shape, dt=F32: ctx.enter_context(nc.sbuf_tensor(name, shape, dt))

        sb, sem = sb_in(top), sem_in(top)
        top_sem = sem
        w_sb = sb("w_sb", [P, WCOLS])
        v_sb = sb("v_sb", [P, len(VECS)])
        id_sb = sb("id_sb", [P, P])
        go = sem("go")
        half = sb("half", [P, 2 * TG * 2])
        msg_bias = sb("msg_bias", [P, 1])
        a_edge = sb("a_edge", [P, 2 * TG, HEADS, ITERS])
        ex_edge = sb("ex_edge", [P, 2 * TG, HEADS, ITERS])

        def W(name, rows=None):
            c, r, n = COL[name]
            return w_sb[0:rows or r, c:c + n]

        def V(name, rows):
            return v_sb[0:rows, VCOL[name]:VCOL[name] + 1]

        psum = [top.enter_context(nc.psum_tensor(f"bank{b}", [P, 512], F32)) for b in range(8)]

        const_in, scaled, bias_ps, bias_ok = sem("const_in"), sem("scaled"), sem("bias_ps"), sem("bias_ok")
        with nc.Block() as block:
            @block.sync
            def _(sp):
                sp.dma_start(w_sb[:], weights).then_inc(const_in, 16)
                sp.dma_start(v_sb[:], vectors).then_inc(const_in, 16)
                sp.dma_start(id_sb[:], ident).then_inc(const_in, 16)

            @block.tensor
            def _(pe):
                pe.wait_ge(const_in, 48)
                pe.matmul(psum[0][:, 0:1], W("msg_s"), V("beta_s2", 128), start=True, stop=True).then_inc(bias_ps, 1)

            @block.vector
            def _(dve):
                dve.memset(half[:], -0.5)
                dve.wait_ge(bias_ps, 1)
                dve.tensor_copy(msg_bias[:], psum[0][:, 0:1]).then_inc(bias_ok, 1)
                dve.wait_ge(const_in, 48)
                r3, r2 = 3 ** -0.5, 2 ** -0.5
                for name, vec, scale in (
                        ("msg_s", "gamma_s2", 1.0), ("msg_v_src", "gamma_v3", 1.0), ("msg_v_dst", "gamma_v3", 1.0),
                        ("out_s01", "w2_s01", 1.0), ("out_s23", "w2_s23", 1.0), ("out_dotv", "w2_vv0", r3),
                        ("out_vs", "w2_vs", 1.0), ("out_next", "w2_vv1", r2), ("out_prev", "w2_vv1", -r2)):
                    m = W(name)
                    dve.tensor_scalar(m, m, V(vec, m.shape[0]), scale, ALU.mult, ALU.mult)
                agg = 48 ** -0.5
                for name, scale in (
                        ("alpha_dotv", r3), ("val_dotv", r3), ("val_v_next", r2), ("val_v_prev", -r2),
                        ("l1_xs", 1 / 8), ("l1_xv", 32 ** -0.5), ("l1_s01", agg), ("l1_s23", agg), ("l1_vs", agg),
                        ("l1_vv", agg * r3), ("self_s", 1 / 8), ("self_v", 32 ** -0.5)):
                    last = dve.tensor_scalar_mul(W(name), W(name), scale)
                last.then_inc(scaled, 1)

        with ExitStack() as ctx:
            sem = sem_in(ctx)
            stages = ["z_ready", "zT_s", "zT_vs", "zT_vd", "zs_sb", "zvs_sb", "zvd_sb", "msgs_ps", "msgv_ps", "msgs_sb",
                      "msgv_sb", "w_s", "w_vs", "w_next", "w_prev", "w_vv0", "p_s", "p_vs", "p_next", "p_prev", "p_vv0",
                      "alpha_ps", "vals_ps", "fifth_sb", "leaky_sb", "vals_sb", "sig_sb", "svy_ps", "valv_ps", "gate_ps",
                      "gate_sb", "svy_sb", "valv_sum", "valv_sb", "a_ps", "a_sb", "prod_sb", "h_ps0", "h_ps1", "h_sb0",
                      "h_sb1", "stats_ready", "mv_ready", "sq_ready", "q_ready", "rstd_ready", "r_ready"]
            s0 = {n: sem("e0_" + n) for n in stages}
            x_in = [top_sem(f"x_in{u}") for u in range(2)]
            idx_in, rbf_in, y_in, h_out = ([sem(f"e0_{n}{u}") for u in range(2)] for n in ("idx", "rbf", "y", "h_out"))
            primed = sem("primed")

            def prime(sp, sems):
                for s in sems:
                    sp.sem_inc(s, 1)

            with nc.Block() as block:
                sb = sb_in(ctx)
                two = lambda name, shape, dt=F32: [sb(f"{name}{u}", shape, dt) for u in range(2)]
                sidx, didx = two("sidx", [P, TG], I32), two("didx", [P, TG], I32)
                xg = two("xg", [P, 2 * TG, D])
                z = two("z", [P, TG, 2 * D])
                stats, mv = two("stats", [P, 4 * TG, 6]), two("mv", [P, 4 * TG, 2])
                msq, q, rstd = two("msq", [P, 2 * TG]), two("q", [P, 4 * TG]), two("rstd", [P, 4 * TG])
                rbf_rep, y_rep, r80 = two("rbf_rep", [80, GROUP]), two("y_rep", [80, GROUP]), two("r80", [80, GROUP])
                ybc = two("ybc", [P, 6, GROUP])
                zs, zvs, zvd = two("zs", [P, GROUP]), two("zvs", [96, GROUP]), two("zvd", [96, GROUP])
                msgs, msgv = two("msgs", [P, GROUP]), two("msgv", [96, GROUP])
                p_s, p_vs, p_next, p_prev, p_vv0 = (two(n, [128 if n == "p_s" else 96, GROUP])
                                                    for n in ("p_s", "p_vs", "p_next", "p_prev", "p_vv0"))
                leaky, vals, sig, gate = (two("leaky", [64, GROUP]), two("vals", [P, GROUP]), two("sig", [P, GROUP]),
                                          two("gate", [96, GROUP]))
                valv = two("valv", [96, GROUP])
                m_s01, m_s23, m_vs, m_dot, m_next, m_prev = (two("m_" + n, [128 if n[0] == "s" else 96, GROUP])
                                                             for n in ("s01", "s23", "vs", "dot", "next", "prev"))
                h_sb = two("h_sb", [P, TG * D])

                def B(u, b):
                    return psum[4 * u + b]

                @block.sync
                def _(sp):
                    def load_idx(i, u):
                        g1, flat = bass.ds(2 * i + u, 1), "a p t -> (a p) t"
                        sp.dma_start(sidx[u][:], src_idx[g1].rearrange(flat)).then_inc(idx_in[u], 16)
                        sp.dma_start(didx[u][:], dst_idx[g1].rearrange(flat)).then_inc(idx_in[u], 16)

                    def load_rbf(i, u):
                        cols = bass.ds(i * CHUNK + u * GROUP, GROUP)
                        sp.dma_start(rbf_rep[u][:], edge_rows[RBF:RBF + 16, cols].unsqueeze(1).broadcast_to([16, 5, GROUP])
                                     ).then_inc(rbf_in[u], 16)
                        sp.dma_start(y_rep[u][:], edge_rows[ONE:ONE + 5, cols].unsqueeze(0).broadcast_to([16, 5, GROUP])
                                     ).then_inc(rbf_in[u], 16)

                    def step(i, u, k):
                        if k == 0:
                            cols = bass.ds(i * CHUNK + u * GROUP, GROUP)
                            wait_old(sp, s0["prod_sb"], i, u)
                            for n, (row, rows, rep) in enumerate(((Y0, 2, 64), (YX + 1, 2, 64), (Y0, 1, 96), (YX, 3, 32),
                                                                  (YX + 1, 3, 32), (YX + 2, 3, 32))):
                                sp.dma_start(ybc[u][0:rows * rep, n, :],
                                             edge_rows[row:row + rows, cols].unsqueeze(0).broadcast_to([rep, rows, GROUP])
                                             ).then_inc(y_in[u], 16)
                        if k == 2:
                            sp.wait_ge(s0["z_ready"], new(i, u))
                            load_idx(i + 1, u)
                            sp.wait_ge(s0["r_ready"], new(i, u))
                            load_rbf(i + 1, u)

                    prime(sp, s0.values())
                    sp.sem_inc(primed, 1)
                    for u in range(2):
                        load_idx(0, u)
                        load_rbf(0, u)
                        sp.dma_start(h_sb[u][0:16, 0:D], x[0:16, :]).then_inc(h_out[u], 16)
                    staggered(sp, ITERS, 5, step)
                    for u in range(2):
                        sp.wait_ge(idx_in[u], 32 * ITERS + 32)
                        sp.wait_ge(rbf_in[u], 32 * ITERS + 32)

                @block.gpsimd
                def _(pool):
                    def gather(i, u):
                        pool.wait_ge(idx_in[u], 32 * i + 32)
                        pool.sem_inc(go, 1)
                        for side, idx in enumerate((sidx[u], didx[u])):
                            for t in range(TG):
                                pool.indirect_dma_start(
                                    out=xg[u][:, side * TG + t, :], out_offset=None, in_=x,
                                    in_offset=bass.IndirectOffsetOnAxis(ap=idx[:, t:t + 1], axis=0)).then_inc(x_in[u], 16)

                    def step(i, u, k):
                        if k == 0:
                            pool.wait_ge(s0["q_ready"], new(i, u))
                            pool.tensor_tensor(rstd[u][:], q[u][:], half[:], ALU.pow).then_inc(s0["rstd_ready"], 1)
                        if k == 2:
                            pool.wait_ge(s0["z_ready"], new(i, u))
                            gather(i + 1, u)

                    pool.wait_ge(primed, 1)
                    gather(0, 0)
                    gather(0, 1)
                    staggered(pool, ITERS, 5, step)
                    for u in range(2):
                        pool.wait_ge(x_in[u], 128 * ITERS + 128)

                @block.tensor
                def _(pe):
                    def job(i, u, bank, waits, mms, done):
                        for name in waits:
                            pe.wait_ge(s0[name], new(i, u))
                        for n, (w, rhs) in enumerate(mms):
                            last = pe.matmul(B(u, bank)[0:w.shape[1], 0:GROUP], w, rhs, start=(n == 0), stop=(n == len(mms) - 1))
                        last.then_inc(s0[done], 1)

                    def step(i, u, k):
                        if k == 1:
                            pe.wait_ge(s0["z_ready"], new(i, u))
                            for bank, c, n, freed, done in ((0, 0, 128, "h_sb0", "zT_s"), (1, 128, 96, "h_sb1", "zT_vs"),
                                                            (2, 224, 96, "gate_sb", "zT_vd")):
                                wait_old(pe, s0[freed], i, u)
                                pe.sem_inc(go, 1)
                                for t in range(TG):
                                    last = pe.transpose(B(u, bank)[0:n, t * P:(t + 1) * P], z[u][:, t, c:c + n], id_sb[:])
                                last.then_inc(s0[done], 1)
                        if k == 2:
                            wait_old(pe, s0["a_sb"], i, u)
                            job(i, u, 3, ["zs_sb"], [(W("msg_s"), zs[u][:])], "msgs_ps")
                            job(i, u, 0, ["zvs_sb", "zvd_sb"],
                                [(W("msg_v_src"), zvs[u][:]), (W("msg_v_dst"), zvd[u][:])], "msgv_ps")
                            job(i, u, 1, ["r_ready"], [(W("rbf_s"), r80[u][:])], "w_s")
                            job(i, u, 2, [], [(W("rbf_vs"), r80[u][:])], "w_vs")
                        if k == 3:
                            job(i, u, 3, ["msgs_sb"], [(W("rbf_vv1_next"), r80[u][:])], "w_next")
                            job(i, u, 0, ["msgv_sb"], [(W("rbf_vv1_prev"), r80[u][:])], "w_prev")
                            job(i, u, 1, ["p_s"], [(W("rbf_vv0"), r80[u][:])], "w_vv0")
                        if k == 5:
                            job(i, u, 3, ["p_next", "p_vv0"], [(W("val_s"), p_s[u][:]), (W("val_dotv"), p_vv0[u][:])], "vals_ps")
                            job(i, u, 2, ["p_vs"], [(W("alpha_s"), p_s[u][:]), (W("alpha_dotv"), p_vv0[u][:])], "alpha_ps")
                            job(i, u, 0, ["p_prev"], [(W("val_v_sv"), p_s[u][:])], "svy_ps")
                            job(i, u, 1, [], [(W("val_v_vs"), p_vs[u][:]), (W("val_v_next"), p_next[u][:]),
                                              (W("val_v_prev"), p_prev[u][:])], "valv_ps")
                        if k == 6:
                            job(i, u, 2, ["vals_sb", "leaky_sb"], [(W("gate"), vals[u][:])], "gate_ps")
                            pe.wait_ge(s0["sig_sb"], new(i, u))
                            for t in range(TG):
                                last = pe.matmul(B(u, 3)[:, t * HEADS:(t + 1) * HEADS], leaky[u][:, t * P:(t + 1) * P],
                                                 W("alpha_dot"), start=True, stop=True)
                            last.then_inc(s0["a_ps"], 1)
                        if k == 8:
                            pe.wait_ge(s0["prod_sb"], new(i, u))
                            for t in range(TG):
                                if t == 0:
                                    pe.wait_ge(s0["svy_sb"], new(i, u))
                                if t == 3:
                                    pe.wait_ge(s0["valv_sum"], new(i, u))
                                o = B(u, t // 3)[:, (t % 3) * D:(t % 3 + 1) * D]
                                e = slice(t * P, (t + 1) * P)
                                pe.matmul(o[:, 0:96], m_s01[u][:, e], W("out_s01"), start=True, stop=False, skip_group_check=True)
                                pe.matmul(o[:, 96:160], m_s23[u][:, e], W("out_s23"), start=False, stop=False, skip_group_check=True)
                                pe.matmul(o[:, 0:64], m_dot[u][:, e], W("out_dotv"), start=False, stop=False, skip_group_check=True)
                                for m, w in ((m_vs, "out_vs"), (m_next, "out_next"), (m_prev, "out_prev")):
                                    last = pe.matmul(o[:, 64:160], m[u][:, e], W(w), start=False, stop=(w == "out_prev"),
                                                     skip_group_check=True)
                                if t == 2:
                                    last.then_inc(s0["h_ps0"], 1)
                            last.then_inc(s0["h_ps1"], 1)

                    pe.wait_ge(primed, 1)
                    staggered(pe, ITERS, 5, step)

                @block.scalar
                def _(act):
                    def evict(i, u, src, freed, dst, bank, rows, done, func=ACT.Copy, **more):
                        act.wait_ge(s0[src], new(i, u))
                        wait_old(act, s0[freed], i, u)
                        nc.scalar.activation(dst[u][:], B(u, bank)[0:rows, :], func, **more).then_inc(s0[done], 1)

                    def step(i, u, k):
                        if k == 1:
                            evict(i, u, "zT_s", "msgs_ps", zs, 0, 128, "zs_sb")
                            evict(i, u, "zT_vs", "msgv_ps", zvs, 1, 96, "zvs_sb")
                            evict(i, u, "zT_vd", "msgv_ps", zvd, 2, 96, "zvd_sb")
                        if k == 2:
                            evict(i, u, "msgs_ps", "p_s", msgs, 3, 128, "msgs_sb", ACT.Identity, bias=msg_bias[:, 0:1])
                            evict(i, u, "msgv_ps", "p_vv0", msgv, 0, 96, "msgv_sb")
                        if k == 5:
                            evict(i, u, "vals_ps", "gate_ps", vals, 3, 128, "vals_sb")
                            evict(i, u, "vals_ps", "prod_sb", sig, 3, 128, "sig_sb", ACT.Sigmoid)
                            evict(i, u, "alpha_ps", "a_ps", leaky, 2, 64, "fifth_sb", scale=0.2)
                        if k == 6:
                            evict(i, u, "gate_ps", "valv_sb", gate, 2, 96, "gate_sb", ACT.Sigmoid)
                        if k == 8:
                            act.wait_ge(s0["h_ps0"], new(i, u))
                            act.wait_ge(h_out[u], 16 * i + 16)
                            nc.scalar.activation(h_sb[u][:, 0:3 * D], B(u, 0)[:, 0:3 * D], ACT.Copy).then_inc(s0["h_sb0"], 1)
                            act.wait_ge(s0["h_ps1"], new(i, u))
                            nc.scalar.activation(h_sb[u][:, 3 * D:4 * D], B(u, 1)[:, 0:D], ACT.Copy).then_inc(s0["h_sb1"], 1)
                            act.wait_ge(s0["h_sb0"], new(i, u))
                            act.wait_ge(s0["h_sb1"], new(i, u))
                            act.dma_start(h_rows[bass.ds(2 * i + u, 1)].rearrange("a p f -> (a p) f"), h_sb[u][:]).then_inc(h_out[u], 16)

                    act.wait_ge(primed, 1)
                    staggered(act, ITERS, 5, step)
                    for u in range(2):
                        act.wait_ge(h_out[u], 16 * ITERS + 16)

                @block.vector
                def _(dve):
                    v = nc.vector

                    def product(i, u, msg, msg_ok, rows, bank, wname, dst, done, freed):
                        dve.wait_ge(s0[msg_ok], new(i, u))
                        dve.wait_ge(s0[wname], new(i, u))
                        wait_old(dve, s0[freed], i, u)
                        v.tensor_tensor(dst[u][:], msg[u][:], B(u, bank)[0:rows, :], ALU.mult).then_inc(s0[done], 1)

                    def step(i, u, k):
                        if k == 0:
                            dve.wait_ge(x_in[u], 128 * i + 128)
                            for n in range(2 * TG):
                                v.bn_stats(stats[u][:, n, :], xg[u][:, n, 0:CS])
                                last = v.bn_stats(stats[u][:, 2 * TG + n, :], xg[u][:, n, CS:D])
                            last.then_inc(s0["stats_ready"], 1)
                            dve.wait_ge(s0["stats_ready"], new(i, u))
                            dve.sem_inc(go, 1)
                            for n in range(4 * TG):
                                last = v.bn_aggr(mv[u][:, n, :], stats[u][:, n, :])
                            last.then_inc(s0["mv_ready"], 1)
                            dve.wait_ge(s0["mv_ready"], new(i, u))
                            wait_old(dve, s0["rstd_ready"], i, u)
                            mean_v, var_v = mv[u][:, 2 * TG:, 0], mv[u][:, 2 * TG:, 1]
                            v.tensor_tensor(msq[u][:], mean_v, mean_v, ALU.mult).then_inc(s0["sq_ready"], 1)
                            v.tensor_scalar(q[u][:, 0:2 * TG], mv[u][:, 0:2 * TG, 1], EPS, None, ALU.add)
                            dve.wait_ge(s0["sq_ready"], 4 * i + 2 * u + 2)
                            v.tensor_tensor(msq[u][:], msq[u][:], var_v, ALU.add).then_inc(s0["sq_ready"], 1)
                            dve.wait_ge(s0["sq_ready"], 4 * i + 2 * u + 3)
                            v.tensor_scalar(q[u][:, 2 * TG:], msq[u][:], 3.0, EPS, ALU.mult, ALU.add).then_inc(s0["q_ready"], 1)
                            dve.wait_ge(rbf_in[u], 32 * i + 32)
                            wait_old(dve, s0["w_vv0"], i, u)
                            v.tensor_tensor(r80[u][:], rbf_rep[u][:], y_rep[u][:], ALU.mult).then_inc(s0["r_ready"], 1)
                        if k == 1:
                            dve.wait_ge(s0["rstd_ready"], new(i, u))
                            wait_old(dve, s0["zT_vd"], i, u)
                            for side in range(2):
                                for t in range(TG):
                                    n = side * TG + t
                                    v.tensor_scalar(z[u][:, t, side * CS:(side + 1) * CS], xg[u][:, n, 0:CS],
                                                    mv[u][:, n, 0:1], rstd[u][:, n:n + 1], ALU.subtract, ALU.mult)
                                    n2, c = 2 * TG + n, 2 * CS + side * CV3
                                    last = v.tensor_scalar(z[u][:, t, c:c + CV3], xg[u][:, n, CS:D],
                                                           rstd[u][:, n2:n2 + 1], None, ALU.mult)
                            last.then_inc(s0["z_ready"], 1)
                        if k == 3:
                            product(i, u, msgs, "msgs_sb", 128, 1, "w_s", p_s, "p_s", "svy_ps")
                            product(i, u, msgv, "msgv_sb", 96, 2, "w_vs", p_vs, "p_vs", "valv_ps")
                            product(i, u, msgv, "msgv_sb", 96, 3, "w_next", p_next, "p_next", "valv_ps")
                        if k == 4:
                            product(i, u, msgv, "msgv_sb", 96, 0, "w_prev", p_prev, "p_prev", "valv_ps")
                            product(i, u, msgv, "msgv_sb", 96, 1, "w_vv0", p_vv0, "p_vv0", "alpha_ps")
                        if k == 6:
                            dve.wait_ge(s0["fifth_sb"], new(i, u))
                            v.tensor_tensor(leaky[u][:], leaky[u][:], B(u, 2)[0:64, :], ALU.max).then_inc(s0["leaky_sb"], 1)
                            dve.wait_ge(s0["svy_ps"], new(i, u))
                            dve.wait_ge(y_in[u], 96 * i + 96)
                            wait_old(dve, s0["h_ps1"], i, u)
                            v.tensor_tensor(valv[u][:], ybc[u][0:96, 3, :], B(u, 0)[0:96, :], ALU.mult).then_inc(s0["svy_sb"], 1)
                            dve.wait_ge(s0["sig_sb"], new(i, u))
                            v.tensor_tensor(m_s01[u][:], sig[u][:], ybc[u][:, 0, :], ALU.mult)
                            dve.wait_ge(s0["svy_sb"], new(i, u))
                            dve.wait_ge(s0["valv_ps"], new(i, u))
                            v.tensor_tensor(valv[u][:], valv[u][:], B(u, 1)[0:96, :], ALU.add).then_inc(s0["valv_sum"], 1)
                            v.tensor_tensor(m_s23[u][:], sig[u][:], ybc[u][:, 1, :], ALU.mult)
                        if k == 7:
                            dve.wait_ge(s0["valv_sum"], new(i, u))
                            dve.wait_ge(s0["gate_sb"], new(i, u))
                            v.tensor_tensor(valv[u][:], valv[u][:], gate[u][:], ALU.mult).then_inc(s0["valv_sb"], 1)
                            dve.wait_ge(s0["a_ps"], new(i, u))
                            v.tensor_scalar(a_edge[:, TG * u:TG * (u + 1), :, bass.ds(i, 1)],
                                            B(u, 3)[:, 0:TG * HEADS].rearrange("p (t h o) -> p t h o", h=HEADS, o=1),
                                            1.0, None, ALU.mult).then_inc(s0["a_sb"], 1)
                            dve.wait_ge(s0["valv_sb"], new(i, u))
                            for m, n in ((m_vs, 2), (m_dot, 3), (m_next, 4), (m_prev, 5)):
                                last = v.tensor_tensor(m[u][:], valv[u][:], ybc[u][0:96, n, :], ALU.mult)
                            last.then_inc(s0["prod_sb"], 1)

                    dve.wait_ge(primed, 1)
                    staggered(dve, ITERS, 5, step)

        with ExitStack() as ctx:
            sem = sem_in(ctx)
            stages = ["x1_bn", "x1_mv", "x1_q", "x1_rstd", "x1_shift", "x1_ready", "T_s", "T_v", "Ts_sb", "Tv_sb", "o_ps",
                      "gates_sb", "gv_ready", "u_ready", "u_bn", "u_mv", "u_q", "u_rstd", "u_shift", "out_a", "out_b"]
            sn = {n: sem("n_" + n) for n in stages}
            xn_in, x1_out, xn_out = ([sem(f"n_{n}{u}") for u in range(2)] for n in ("xn_in", "x1_out", "xn_out"))
            primed_n = sem("primed_n")

            def node_rows(t, i, u):
                return t[bass.ds(i * CHUNK + u * GROUP, GROUP), :].rearrange("(p t) d -> p (t d)", t=TG)

            with nc.Block() as block:
                sb = sb_in(ctx)
                two = lambda name, shape, dt=F32: [sb(f"{name}{u}", shape, dt) for u in range(2)]
                xn, x1n, un, outn = (two(n, [P, TG, D]) for n in ("xn", "x1n", "un", "outn"))
                st1, st2 = two("st1", [P, TG, 6]), two("st2", [P, TG, 6])
                mv1, mv2 = two("mv1", [P, TG, 2]), two("mv2", [P, TG, 2])
                q1, q2, r1, r2_, shift1, shift2 = (two(n, [P, TG]) for n in ("q1", "q2", "r1", "r2_", "shift1", "shift2"))
                Ts, Tv = two("Ts", [64, GROUP]), two("Tv", [96, GROUP])
                gates, gv = two("gates", [P, TG, 96]), two("gv", [P, TG, CV3])
                flat = "p t d -> p (t d)"

                @block.sync
                def _(sp):
                    def step(i, u, k):
                        if k == 0:
                            wait_old(sp, sn["x1_ready"], i, u)
                            sp.dma_start(xn[u][:].rearrange(flat), node_rows(x, i, u)).then_inc(xn_in[u], 16)
                        if k == 4:
                            sp.wait_ge(sn["x1_ready"], new(i, u))
                            sp.dma_start(node_rows(x1, i, u), x1n[u][:].rearrange(flat)).then_inc(x1_out[u], 16)
                        if k == 7:
                            sp.wait_ge(sn["out_a"], new(i, u))
                            sp.wait_ge(sn["out_b"], new(i, u))
                            sp.dma_start(node_rows(out, i, u), outn[u][:].rearrange(flat)).then_inc(xn_out[u], 16)

                    prime(sp, sn.values())
                    sp.sem_inc(primed_n, 1)
                    for u in range(2):
                        sp.dma_start(outn[u][0:16, 0, :], x[0:16, :]).then_inc(xn_out[u], 16)
                        sp.dma_start(x1n[u][0:16, 0, :], x[0:16, :]).then_inc(x1_out[u], 16)
                    staggered(sp, NODE_ITERS, 4, step)
                    for u in range(2):
                        sp.wait_ge(xn_out[u], 16 * NODE_ITERS + 16)
                        sp.wait_ge(x1_out[u], 16 * NODE_ITERS + 16)

                @block.gpsimd
                def _(pool):
                    def step(i, u, k):
                        if k == 2:
                            pool.wait_ge(sn["x1_q"], new(i, u))
                            pool.tensor_tensor(r1[u][:], q1[u][:], half[:, 0:TG], ALU.pow).then_inc(sn["x1_rstd"], 1)
                        if k == 6:
                            pool.wait_ge(sn["u_q"], new(i, u))
                            pool.tensor_tensor(r2_[u][:], q2[u][:], half[:, 0:TG], ALU.pow).then_inc(sn["u_rstd"], 1)

                    pool.wait_ge(primed_n, 1)
                    staggered(pool, NODE_ITERS, 4, step)

                @block.tensor
                def _(pe):
                    def step(i, u, k):
                        b = psum[4 * u:4 * u + 4]
                        if k == 4:
                            pe.wait_ge(sn["x1_ready"], new(i, u))
                            for bank, c, n, freed, done in ((0, 0, 64, "Ts_sb", "T_s"), (1, CS, 96, "Tv_sb", "T_v")):
                                wait_old(pe, sn[freed], i, u)
                                pe.sem_inc(go, 1)
                                for t in range(TG):
                                    last = pe.transpose(b[bank][0:n, t * P:(t + 1) * P], x1n[u][:, t, c:c + n], id_sb[:])
                                last.then_inc(sn[done], 1)
                        if k == 5:
                            pe.wait_ge(sn["Ts_sb"], new(i, u))
                            pe.wait_ge(sn["Tv_sb"], new(i, u))
                            wait_old(pe, sn["gv_ready"], i, u)
                            for t in range(TG):
                                o = b[2 + t // 2][:, (t % 2) * MSG:(t % 2 + 1) * MSG]
                                e = slice(t * P, (t + 1) * P)
                                pe.matmul(o[:, 0:96], Ts[u][:, e], W("self_s"), start=True, stop=False, skip_group_check=True)
                                last = pe.matmul(o[:, 96:192], Tv[u][:, e], W("self_v"), start=False, stop=True, skip_group_check=True)
                            last.then_inc(sn["o_ps"], 1)

                    pe.wait_ge(primed_n, 1)
                    staggered(pe, NODE_ITERS, 4, step)

                @block.scalar
                def _(act):
                    def step(i, u, k):
                        b = psum[4 * u:4 * u + 4]
                        if k == 3:
                            act.wait_ge(sn["x1_shift"], new(i, u))
                            act.wait_ge(x1_out[u], 16 * i + 16)
                            for t in range(TG):
                                last = nc.scalar.activation(x1n[u][:, t, :], xn[u][:, t, :], ACT.Identity,
                                                            scale=r1[u][:, t:t + 1], bias=shift1[u][:, t:t + 1])
                            last.then_inc(sn["x1_ready"], 1)
                        if k == 4:
                            act.wait_ge(sn["T_s"], new(i, u))
                            wait_old(act, sn["o_ps"], i, u)
                            nc.scalar.activation(Ts[u][:], b[0][0:64, :], ACT.Copy).then_inc(sn["Ts_sb"], 1)
                            act.wait_ge(sn["T_v"], new(i, u))
                            nc.scalar.activation(Tv[u][:], b[1][0:96, :], ACT.Copy).then_inc(sn["Tv_sb"], 1)
                        if k == 5:
                            act.wait_ge(sn["o_ps"], new(i, u))
                            wait_old(act, sn["u_ready"], i, u)
                            for n in range(2):
                                last = nc.scalar.activation(
                                    gates[u][:, 2 * n:2 * n + 2, :],
                                    b[2 + n][:, 0:2 * MSG].rearrange("p (t f) -> p t f", t=2)[:, :, 0:96], ACT.Silu)
                            last.then_inc(sn["gates_sb"], 1)
                        if k == 7:
                            act.wait_ge(sn["u_shift"], new(i, u))
                            act.wait_ge(xn_out[u], 16 * i + 16)
                            for t in range(2, TG):
                                last = nc.scalar.activation(outn[u][:, t, :], un[u][:, t, :], ACT.Identity,
                                                            scale=r2_[u][:, t:t + 1], bias=shift2[u][:, t:t + 1])
                            last.then_inc(sn["out_b"], 1)

                    act.wait_ge(primed_n, 1)
                    staggered(act, NODE_ITERS, 4, step)

                @block.vector
                def _(dve):
                    v = nc.vector

                    def step(i, u, k):
                        if k == 2:
                            dve.wait_ge(xn_in[u], 16 * i + 16)
                            for t in range(TG):
                                last = v.bn_stats(st1[u][:, t, :], xn[u][:, t, :])
                            last.then_inc(sn["x1_bn"], 1)
                            dve.wait_ge(sn["x1_bn"], new(i, u))
                            wait_old(dve, sn["x1_shift"], i, u)
                            dve.sem_inc(go, 1)
                            for t in range(TG):
                                last = v.bn_aggr(mv1[u][:, t, :], st1[u][:, t, :])
                            last.then_inc(sn["x1_mv"], 1)
                            dve.wait_ge(sn["x1_mv"], new(i, u))
                            v.tensor_scalar(q1[u][:], mv1[u][:, :, 1], EPS / 4, None, ALU.add).then_inc(sn["x1_q"], 1)
                        if k == 3:
                            dve.wait_ge(sn["x1_rstd"], new(i, u))
                            wait_old(dve, sn["x1_ready"], i, u)
                            v.scalar_tensor_tensor(shift1[u][:], mv1[u][:, :, 0], -1.0, r1[u][:], ALU.mult, ALU.mult
                                                   ).then_inc(sn["x1_shift"], 1)
                        if k == 6:
                            dve.wait_ge(sn["gates_sb"], new(i, u))
                            dve.wait_ge(sn["o_ps"], new(i, u))
                            for n in range(2):
                                b = psum[4 * u + 2 + n]
                                o = b[:, 0:2 * MSG].rearrange("p (t f) -> p t f", t=2)[:, :, 96:192].rearrange("p t (c k) -> p t k c", c=3)
                                g = gates[u][:, 2 * n:2 * n + 2, CS:96].unsqueeze(3).broadcast_to([P, 2, CV, 3])
                                last = v.tensor_tensor(
                                    gv[u][:, 2 * n:2 * n + 2, :].rearrange("p t (k c) -> p t k c", c=3), g, o, ALU.mult)
                            last.then_inc(sn["gv_ready"], 1)
                            wait_old(dve, sn["out_b"], i, u)
                            v.scalar_tensor_tensor(un[u][:, :, 0:CS], x1n[u][:, :, 0:CS], 2.0, gates[u][:, :, 0:CS],
                                                   ALU.mult, ALU.add)
                            dve.wait_ge(sn["gv_ready"], new(i, u))
                            v.scalar_tensor_tensor(un[u][:, :, CS:D], x1n[u][:, :, CS:D], 2.0, gv[u][:],
                                                   ALU.mult, ALU.add).then_inc(sn["u_ready"], 1)
                            dve.wait_ge(sn["u_ready"], new(i, u))
                            for t in range(TG):
                                last = v.bn_stats(st2[u][:, t, :], un[u][:, t, :])
                            last.then_inc(sn["u_bn"], 1)
                            dve.wait_ge(sn["u_bn"], new(i, u))
                            dve.sem_inc(go, 1)
                            for t in range(TG):
                                last = v.bn_aggr(mv2[u][:, t, :], st2[u][:, t, :])
                            last.then_inc(sn["u_mv"], 1)
                            dve.wait_ge(sn["u_mv"], new(i, u))
                            v.tensor_scalar(q2[u][:], mv2[u][:, :, 1], EPS, None, ALU.add).then_inc(sn["u_q"], 1)
                        if k == 7:
                            dve.wait_ge(sn["u_rstd"], new(i, u))
                            v.scalar_tensor_tensor(shift2[u][:], mv2[u][:, :, 0], -1.0, r2_[u][:], ALU.mult, ALU.mult
                                                   ).then_inc(sn["u_shift"], 1)
                            dve.wait_ge(xn_out[u], 16 * i + 16)
                            for t in range(2):
                                last = v.tensor_scalar(outn[u][:, t, :], un[u][:, t, :], mv2[u][:, t, 0:1],
                                                       r2_[u][:, t:t + 1], ALU.subtract, ALU.mult)
                            last.then_inc(sn["out_a"], 1)

                    dve.wait_ge(primed_n, 1)
                    staggered(dve, NODE_ITERS, 4, step)

        with ExitStack() as ctx:
            sem = sem_in(ctx)
            m_in, m_t, m_ev, m_dve, m_act = sem("m_in"), sem("m_t"), sem("m_ev"), sem("m_dve"), sem("m_act")
            with nc.Block() as block:
                sb = sb_in(ctx)
                a_seg = sb("a_seg", [SEG, CHUNK])
                dq_i = sb("dq_i", [SEG, CHUNK], I32)
                dq = sb("dq", [SEG, CHUNK])
                step = sb("step", [SEG, CHUNK + 1])
                run = sb("run", [SEG, CHUNK])
                top_ = sb("top_", [SEG, CHUNK])
                other = sb("other", [SEG, CHUNK])
                ends = sb("ends", [1, 4, SEG])
                hm = sb("hm", [1, SEG])
                cont, whole, f_in, g_in = sb("cont", [1, SEG]), sb("whole", [1, SEG]), sb("f_in", [1, SEG]), sb("g_in", [1, SEG])
                carry = sb("carry", [1, 2, SEG])
                carry_col = sb("carry_col", [SEG, 2])

                @block.sync
                def _(sp):
                    for h in range(HEADS):
                        sp.dma_start(dq_i[h * ITERS:(h + 1) * ITERS, :], dst_line).then_inc(m_in, 16)
                    sp.dma_start(hm[:], head_mask).then_inc(m_in, 16)

                @block.tensor
                def _(pe):
                    for b in range(2 * TG):
                        last = pe.transpose(psum[b // 4][0:SEG, (b % 4) * P:(b % 4 + 1) * P],
                                            a_edge[:, b].rearrange("p h q -> p (h q)"), id_sb[:])
                    last.then_inc(m_t, 1)
                    pe.wait_ge(m_dve, 1)
                    for k, c in enumerate((run[:, CHUNK - 1:CHUNK], top_[:, 0:1], dq[:, 0:1], dq[:, CHUNK - 1:CHUNK])):
                        last = pe.transpose(psum[2][0:1, k * P:k * P + SEG], c, id_sb[0:SEG, 0:SEG])
                    last.then_inc(m_t, 1)
                    pe.wait_ge(m_dve, 2)
                    for k in range(2):
                        last = pe.transpose(psum[3][0:SEG, k:k + 1], carry[:, k, :], id_sb[0:1, 0:1])
                    last.then_inc(m_t, 1)
                    pe.wait_ge(m_act, 3)
                    for b in range(2 * TG):
                        last = pe.transpose(psum[4 + b // 4][:, (b % 4) * P:(b % 4) * P + SEG], a_seg[:, b * P:(b + 1) * P],
                                            id_sb[0:SEG, 0:SEG])
                    last.then_inc(m_t, 1)

                @block.scalar
                def _(act):
                    act.wait_ge(m_t, 1)
                    for k in range(2):
                        nc.scalar.activation(a_seg[:, k * 512:(k + 1) * 512], psum[k][0:SEG, :], ACT.Copy).then_inc(m_act, 1)
                    act.wait_ge(m_dve, 3)
                    nc.scalar.activation(a_seg[:], other[:], ACT.Exp).then_inc(m_act, 1)
                    act.wait_ge(m_t, 4)
                    for b in range(2 * TG):
                        nc.scalar.activation(ex_edge[:, b].rearrange("p h q -> p (h q)"),
                                             psum[4 + b // 4][:, (b % 4) * P:(b % 4) * P + SEG], ACT.Copy)

                @block.vector
                def _(dve):
                    n = [0]

                    def then(ins):
                        ins.then_inc(m_ev, 1)
                        n[0] += 1
                        dve.wait_ge(m_ev, n[0])

                    v = nc.vector
                    dve.wait_ge(m_in, 16 * (HEADS + 1))
                    v.memset(step[:], -BIG)
                    then(v.tensor_copy(dq[:], dq_i[:]))
                    then(v.tensor_tensor(step[:, 1:CHUNK], dq[:, 1:CHUNK], dq[:, 0:CHUNK - 1], ALU.is_equal))
                    then(v.tensor_scalar(step[:, 1:CHUNK], step[:, 1:CHUNK], 1.0, BIG, ALU.subtract, ALU.mult))
                    dve.wait_ge(m_act, 2)
                    then(v.tensor_tensor_scan(run[:], step[:, 0:CHUNK], a_seg[:], -BIG, ALU.add, ALU.max))
                    v.tensor_tensor_scan(top_[:, ::-1], step[:, 1:CHUNK + 1][:, ::-1], run[:, ::-1], -BIG, ALU.add,
                                         ALU.max).then_inc(m_dve, 1)
                    dve.wait_ge(m_t, 2)
                    then(v.tensor_copy(ends[:], psum[2][0:1, :].rearrange("p (k s) -> p k s", k=4)[:, :, 0:SEG]))
                    last_max, first_max, first, last = (ends[:, k, :] for k in range(4))
                    v.memset(cont[:], -BIG)
                    then(v.tensor_tensor(whole[:], first, last, ALU.is_equal))
                    then(v.tensor_tensor(cont[:, 1:], first[:, 1:], last[:, 0:SEG - 1], ALU.is_equal))
                    v.tensor_scalar(whole[:], whole[:], 1.0, BIG, ALU.subtract, ALU.mult)
                    then(v.tensor_scalar(cont[:, 1:], cont[:, 1:], 1.0, BIG, ALU.subtract, ALU.mult))
                    then(v.tensor_tensor(cont[:], cont[:], hm[:], ALU.add))
                    v.memset(carry[:], -BIG)
                    v.tensor_tensor(f_in[:, 1:], whole[:, 0:SEG - 1], cont[:, 1:], ALU.add)
                    then(v.tensor_tensor(g_in[:, 1:], last_max[:, 0:SEG - 1], cont[:, 1:], ALU.add))
                    then(v.tensor_tensor_scan(carry[:, 0, 1:], f_in[:, 1:], g_in[:, 1:], -BIG, ALU.add, ALU.max))
                    v.tensor_tensor(f_in[:, 0:SEG - 1], whole[:, 1:], cont[:, 1:], ALU.add)
                    then(v.tensor_tensor(g_in[:, 0:SEG - 1], first_max[:, 1:], cont[:, 1:], ALU.add))
                    v.tensor_tensor_scan(carry[:, 1, 0:SEG - 1][:, ::-1], f_in[:, 0:SEG - 1][:, ::-1],
                                         g_in[:, 0:SEG - 1][:, ::-1], -BIG, ALU.add, ALU.max).then_inc(m_dve, 1)
                    dve.wait_ge(m_t, 3)
                    then(v.tensor_copy(carry_col[:], psum[3][0:SEG, 0:2]))
                    for k, c in enumerate((0, CHUNK - 1)):
                        then(v.tensor_scalar(other[:], dq[:], dq[:, c:c + 1], 1.0, ALU.is_equal, ALU.subtract))
                        then(v.tensor_scalar(other[:], other[:], BIG, carry_col[:, k:k + 1], ALU.mult, ALU.add))
                        then(v.tensor_tensor(top_[:], top_[:], other[:], ALU.max))
                    v.tensor_tensor(other[:], a_seg[:], top_[:], ALU.subtract).then_inc(m_dve, 1)

        with ExitStack() as ctx:
            sem = sem_in(ctx)
            stages = ["e_ex", "e_sb", "sel_sb", "agg_ps", "agg_sb", "den_sb", "rden_sb", "nrm_sb", "T_s", "T_v", "Ts_sb",
                      "Tv_sb", "p_ps", "u_ready", "bn", "mv", "q", "rstd", "x1_ready", "idx_ready", "prime"]
            s3 = {n: sem("a0_" + n) for n in stages}
            ld3, gi3, st3 = ([sem(f"a0_{n}{u}") for u in range(2)] for n in ("ld", "gi", "st"))
            xd3, sc3 = ([top_sem(f"a0_{n}{u}") for u in range(2)] for n in ("xd", "sc"))
            primed_3 = sem("primed_3")

            with nc.Block() as block:
                sb = sb_in(ctx)
                two = lambda name, shape, dt=F32: [sb(f"{name}{u}", shape, dt) for u in range(2)]
                hh = two("hh", [P, TG, D])
                exg = two("exg", [P, TG, HEADS])
                e = two("e", [P, TG, AGG])
                xd = two("xd", [P, TG, D])
                didx = two("didx3", [P, TG], I32)
                dcol_i, dcol = two("dcol_i", [P, TG + 1], I32), two("dcol", [P, TG + 1])
                dnext = two("dnext", [P, TG], I32)
                dline = two("dline", [P, GROUP], I32)
                tidx_f, tidx = two("tidx_f", [P, TG]), two("tidx", [P, TG], I32)
                sel, sel_c = two("sel", [P, TG, P]), two("sel_c", [P, TG, P])
                agg = two("agg", [P, TG, AGG])
                den, rden = two("den", [P, TG, HEADS]), two("rden", [P, TG, HEADS])
                nrm = two("nrm", [P, TG, D])
                Ts, Tv = two("Ts3", [64, GROUP]), two("Tv3", [96, GROUP])
                uu, x1d = two("uu", [P, TG, D]), two("x1d", [P, TG, D])
                st, mv = two("st", [P, TG, 6]), two("mv3", [P, TG, 2])
                q, r = two("q3", [P, TG]), two("r3", [P, TG])
                flat, group = "p t d -> p (t d)", "a p t -> (a p) t"

                @block.sync
                def _(sp):
                    def load_idx(i, u):
                        sp.dma_start(didx[u][:], dst_idx[bass.ds(2 * i + u, 1)].rearrange(group)).then_inc(gi3[u], 16)

                    def step(i, u, k):
                        if k == 0:
                            g1 = bass.ds(2 * i + u, 1)
                            wait_old(sp, s3["e_sb"], i, u)
                            wait_old(sp, s3["sel_sb"], i, u)
                            wait_old(sp, s3["idx_ready"], i, u)
                            sp.dma_start(hh[u][:].rearrange(flat), h_rows[g1].rearrange(group)).then_inc(ld3[u], 16)
                            sp.dma_start(dcol_i[u][:], dst_cols[g1].rearrange(group)).then_inc(ld3[u], 16)
                            sp.dma_start(dnext[u][:], dst_next[g1].rearrange(group)).then_inc(ld3[u], 16)
                            sp.dma_start(dline[u][:], dst_line[bass.ds(i, 1), u * GROUP:(u + 1) * GROUP].broadcast_to([P, GROUP])
                                         ).then_inc(ld3[u], 16)
                        if k == 8:
                            sp.wait_ge(s3["u_ready"], new(i, u))
                            load_idx(i + 1, u)
                        if k == 10:
                            sp.wait_ge(s3["x1_ready"], new(i, u))
                            sp.dma_start(x1_dst[bass.ds(2 * i + u, 1)].rearrange(group), x1d[u][:].rearrange(flat)
                                         ).then_inc(st3[u], 16)

                    prime(sp, s3.values())
                    sp.sem_inc(primed_3, 1)
                    for u in range(2):
                        load_idx(0, u)
                        sp.dma_start(x1d[u][0:16, 0, :], x[0:16, :]).then_inc(st3[u], 16)
                    staggered(sp, ITERS, 6, step)
                    for u in range(2):
                        sp.wait_ge(st3[u], 16 * ITERS + 16)
                        sp.wait_ge(gi3[u], 16 * ITERS + 16)

                @block.gpsimd
                def _(pool):
                    def gather(i, u):
                        pool.wait_ge(gi3[u], 16 * i + 16)
                        pool.sem_inc(go, 1)
                        for t in range(TG):
                            pool.indirect_dma_start(out=xd[u][:, t, :], out_offset=None, in_=x,
                                                    in_offset=bass.IndirectOffsetOnAxis(ap=didx[u][:, t:t + 1], axis=0)
                                                    ).then_inc(xd3[u], 16)

                    def step(i, u, k):
                        if k == 8:
                            pool.wait_ge(s3["q"], new(i, u))
                            pool.tensor_tensor(r[u][:], q[u][:], half[:, 0:TG], ALU.pow).then_inc(s3["rstd"], 1)
                        if k == 10:
                            gather(i + 1, u)
                        if k == 11:
                            pool.wait_ge(s3["x1_ready"], new(i, u))
                            pool.sem_inc(go, 1)
                            for t in range(TG):
                                pool.indirect_dma_start(out=x1, in_=x1d[u][:, t, :], in_offset=None,
                                                        out_offset=bass.IndirectOffsetOnAxis(ap=tidx[u][:, t:t + 1], axis=0),
                                                        bounds_check=NP - 1, oob_is_err=False).then_inc(sc3[u], 16)

                    pool.wait_ge(primed_3, 1)
                    for u in range(2):
                        pool.dma_start(x1d[u][0:16, 1, :], x[0:16, :]).then_inc(sc3[u], 16)
                        gather(0, u)
                    staggered(pool, ITERS, 6, step)
                    for u in range(2):
                        pool.wait_ge(sc3[u], 64 * ITERS + 16)
                        pool.wait_ge(xd3[u], 64 * ITERS + 64)

                @block.tensor
                def _(pe):
                    def step(i, u, k):
                        if 3 <= k < 3 + TG:
                            t = k - 3
                            n = 8 * i + 4 * u + t
                            o = psum[4 * u + t % 2][:, 0:AGG]
                            prev = agg[u][:, t - 1, :] if t else agg[1 - u][:, TG - 1, :]
                            if t == 0:
                                pe.wait_ge(s3["e_sb"], new(i, u))
                                pe.wait_ge(s3["sel_sb"], new(i, u))
                                wait_old(pe, s3["nrm_sb"], i, u)
                            if t >= 2:
                                pe.wait_ge(s3["agg_sb"], n)
                            pe.matmul(o, sel[u][:, t, :], e[u][:, t, :], start=True, stop=False)
                            pe.wait_ge(s3["agg_sb"], n + 1)
                            pe.matmul(o, sel_c[u][:, t, :], prev, start=False, stop=True).then_inc(s3["agg_ps"], 1)
                        if k == 7:
                            pe.wait_ge(s3["nrm_sb"], new(i, u))
                            wait_old(pe, s3["u_ready"], i, u)
                            for bank, c, n, done in ((2, 0, 64, "T_s"), (3, CS, 96, "T_v")):
                                pe.sem_inc(go, 1)
                                for t in range(TG):
                                    last = pe.transpose(psum[4 * u + bank][0:n, t * P:(t + 1) * P], nrm[u][:, t, c:c + n], id_sb[:])
                                last.then_inc(s3[done], 1)
                        if k == 8:
                            pe.wait_ge(s3["Ts_sb"], new(i, u))
                            pe.wait_ge(s3["Tv_sb"], new(i, u))
                            for t in range(TG):
                                o = psum[4 * u + 2 + t // 2][:, (t % 2) * D:(t % 2 + 1) * D]
                                ee = slice(t * P, (t + 1) * P)
                                pe.matmul(o[:, 0:CS], Ts[u][:, ee], W("proj_s"), start=True, stop=False, skip_group_check=True)
                                last = pe.matmul(o[:, CS:D], Tv[u][:, ee], W("proj_v"), start=False, stop=True, skip_group_check=True)
                            last.then_inc(s3["p_ps"], 1)

                    pe.wait_ge(primed_3, 1)
                    staggered(pe, ITERS, 6, step)

                @block.scalar
                def _(act):
                    def step(i, u, k):
                        if 3 <= k < 3 + TG:
                            t = k - 3
                            act.wait_ge(s3["agg_ps"], 8 * i + 4 * u + t + 2)
                            nc.scalar.activation(agg[u][:, t, :], psum[4 * u + t % 2][:, 0:AGG], ACT.Copy).then_inc(s3["agg_sb"], 1)
                        if k == 7:
                            act.wait_ge(s3["T_s"], new(i, u))
                            wait_old(act, s3["p_ps"], i, u)
                            nc.scalar.activation(Ts[u][:], psum[4 * u + 2][0:64, :], ACT.Copy).then_inc(s3["Ts_sb"], 1)
                            act.wait_ge(s3["T_v"], new(i, u))
                            nc.scalar.activation(Tv[u][:], psum[4 * u + 3][0:96, :], ACT.Copy).then_inc(s3["Tv_sb"], 1)

                    act.wait_ge(primed_3, 1)
                    staggered(act, ITERS, 6, step)

                @block.vector
                def _(dve):
                    v = nc.vector

                    def by_head(dst, src, factor):
                        for c0, c1, a in ((0, CS, 16), *((CS + c * CV, CS + (c + 1) * CV, 8) for c in range(3))):
                            last = v.tensor_tensor(dst[:, :, c0:c1].rearrange("p t (h a) -> p t h a", h=HEADS),
                                                   src[:, :, c0:c1].rearrange("p t (h a) -> p t h a", h=HEADS),
                                                   factor[:].unsqueeze(3).broadcast_to([P, TG, HEADS, a]), ALU.mult)
                        return last

                    def step(i, u, k):
                        if k == 2:
                            dve.wait_ge(ld3[u], 64 * i + 64)
                            wait_old_sums(dve, s3["agg_ps"], i, u)
                            v.tensor_copy(dcol[u][:], dcol_i[u][:])
                            v.tensor_tensor(tidx_f[u][:], dcol_i[u][:, 1:], dnext[u][:], ALU.is_equal)
                            v.tensor_scalar(exg[u][:], ex_edge[:, TG * u:TG * (u + 1), :, bass.ds(i, 1)].rearrange("p t h o -> p t (h o)"),
                                            1.0, None, ALU.mult).then_inc(s3["e_ex"], 1)
                            dve.wait_ge(s3["e_ex"], new(i, u))
                            by_head(e[u], hh[u], exg[u])
                            v.tensor_copy(e[u][:, :, D:AGG], exg[u][:]).then_inc(s3["e_sb"], 1)
                            for t in range(TG):
                                line = dline[u][:, t * P:(t + 1) * P]
                                v.tensor_scalar(sel[u][:, t, :], line, dcol[u][:, t + 1:t + 2], None, ALU.is_equal)
                                last = v.tensor_scalar(sel_c[u][:, t, :], line, dcol[u][:, t:t + 1], V("last_row", P),
                                                       ALU.is_equal, ALU.mult)
                            last.then_inc(s3["sel_sb"], 1)
                            dve.wait_ge(sc3[u], 64 * i + 16)
                            v.scalar_tensor_tensor(tidx[u][:], tidx_f[u][:], float(SKIP), dcol[u][:, 1:], ALU.mult, ALU.add
                                                   ).then_inc(s3["idx_ready"], 1)
                        if k == 7:
                            dve.wait_ge(s3["agg_sb"], 8 * i + 4 * u + 5)
                            v.tensor_scalar(den[u][:], agg[u][:, :, D:AGG], 1e-16, None, ALU.add).then_inc(s3["den_sb"], 1)
                            dve.wait_ge(s3["den_sb"], new(i, u))
                            v.reciprocal(rden[u][:], den[u][:]).then_inc(s3["rden_sb"], 1)
                            dve.wait_ge(s3["rden_sb"], new(i, u))
                            wait_old(dve, s3["T_v"], i, u)
                            by_head(nrm[u], agg[u], rden[u]).then_inc(s3["nrm_sb"], 1)
                        if k == 8:
                            dve.wait_ge(s3["p_ps"], new(i, u))
                            dve.wait_ge(xd3[u], 64 * i + 64)
                            for n in range(2):
                                last = v.scalar_tensor_tensor(
                                    uu[u][:, 2 * n:2 * n + 2, :], xd[u][:, 2 * n:2 * n + 2, :], 2.0,
                                    psum[4 * u + 2 + n][:, 0:2 * D].rearrange("p (t d) -> p t d", t=2), ALU.mult, ALU.add)
                            last.then_inc(s3["u_ready"], 1)
                            dve.wait_ge(s3["u_ready"], new(i, u))
                            for t in range(TG):
                                last = v.bn_stats(st[u][:, t, :], uu[u][:, t, :])
                            last.then_inc(s3["bn"], 1)
                            dve.wait_ge(s3["bn"], new(i, u))
                            dve.sem_inc(go, 1)
                            for t in range(TG):
                                last = v.bn_aggr(mv[u][:, t, :], st[u][:, t, :])
                            last.then_inc(s3["mv"], 1)
                            dve.wait_ge(s3["mv"], new(i, u))
                            v.tensor_scalar(q[u][:], mv[u][:, :, 1], EPS, None, ALU.add).then_inc(s3["q"], 1)
                        if k == 9:
                            dve.wait_ge(s3["rstd"], new(i, u))
                            dve.wait_ge(st3[u], 16 * i + 16)
                            dve.wait_ge(sc3[u], 64 * i + 16)
                            for t in range(TG):
                                last = v.tensor_scalar(x1d[u][:, t, :], uu[u][:, t, :], mv[u][:, t, 0:1], r[u][:, t:t + 1],
                                                       ALU.subtract, ALU.mult)
                            last.then_inc(s3["x1_ready"], 1)

                    v.memset(agg[1][:], 0.0).then_inc(s3["prime"], 1)
                    dve.wait_ge(s3["prime"], 2)
                    dve.wait_ge(primed_3, 1)
                    staggered(dve, ITERS, 6, step)

        with ExitStack() as ctx:
            sem = sem_in(ctx)
            stages = ["T_s", "T_v", "Ts_sb", "Tv_sb", "xs_ps", "xv_ps", "hid_ps", "hid_sb", "w_s01", "w_s23", "w_vs",
                      "w_vv", "q_s01", "q_s23", "q_vs", "q_vv", "m_s01", "m_s23", "m_vs", "m_vv", "msg_ps0", "msg_ps1",
                      "msg_sb0", "msg_sb1", "dcol_sb", "sel_sb", "idx_ready", "agg_ps", "agg_sb", "N_s", "N_v", "Ns_sb",
                      "Nv_sb", "self_ps", "o_sb", "gates_sb", "gv_ready", "u_ready", "bn", "mv", "q", "rstd", "out_ready",
                      "prime"]
            s4 = {n: sem("e1_" + n) for n in stages}
            ix4, y4, em4, ld4 = ([sem(f"e1_{n}{u}") for u in range(2)] for n in ("ix", "y", "em", "ld"))
            xg4, sc4 = ([top_sem(f"e1_{n}{u}") for u in range(2)] for n in ("xg", "sc"))
            primed_4 = sem("primed_4")

            with nc.Block() as block:
                sb = sb_in(ctx)
                two = lambda name, shape, dt=F32: [sb(f"{name}{u}", shape, dt) for u in range(2)]
                sidx = two("sidx4", [P, TG], I32)
                xg = two("xg4", [P, TG, D])
                ybc = two("ybc4", [P, 4, GROUP])
                emb = two("emb", [8, GROUP])
                Ts, Tv, hid = two("Ts4", [64, GROUP]), two("Tv4", [96, GROUP]), two("hid", [64, GROUP])
                m_s01, m_s23, m_vs, m_vv = (two("n_" + n, [128 if n[0] == "s" else 96, GROUP]) for n in ("s01", "s23", "vs", "vv"))
                msg = two("msg", [P, TG, MSG])
                dcol_i, dcol = two("dcol_i4", [P, TG + 1], I32), two("dcol4", [P, TG + 1])
                dnext = two("dnext4", [P, TG], I32)
                dline = two("dline4", [P, GROUP], I32)
                tidx_f, tidx = two("tidx_f4", [P, TG]), two("tidx4", [P, TG], I32)
                sel, sel_c = two("sel4", [P, TG, P]), two("sel_c4", [P, TG, P])
                agg = two("agg4", [P, TG, MSG])
                x1d = two("x1d4", [P, TG, D])
                Ns, Nv = two("Ns", [64, GROUP]), two("Nv", [96, GROUP])
                o_sb = two("o_sb", [P, TG, MSG])
                gates, gv = two("gates4", [P, TG, 96]), two("gv4", [P, TG, CV3])
                uu, od = two("uu4", [P, TG, D]), two("od", [P, TG, D])
                st, mv = two("st4", [P, TG, 6]), two("mv4", [P, TG, 2])
                q, r = two("q4", [P, TG]), two("r4", [P, TG])
                flat, group = "p t d -> p (t d)", "a p t -> (a p) t"

                @block.sync
                def _(sp):
                    def load_idx(i, u):
                        sp.dma_start(sidx[u][:], src_idx[bass.ds(2 * i + u, 1)].rearrange(group)).then_inc(ix4[u], 16)

                    def step(i, u, k):
                        g1 = bass.ds(2 * i + u, 1)
                        cols = bass.ds(i * CHUNK + u * GROUP, GROUP)
                        if k == 0:
                            wait_old(sp, s4["hid_ps"], i, u)
                            sp.dma_start(emb[u][:], edge_rows[EMB:EMB + 8, cols]).then_inc(em4[u], 16)
                            wait_old(sp, s4["q_vv"], i, u)
                            for n, (row, rows, rep) in enumerate(((Y0, 2, 64), (YX + 1, 2, 64), (Y0, 1, 96), (YX, 3, 32))):
                                sp.dma_start(ybc[u][0:rows * rep, n, :],
                                             edge_rows[row:row + rows, cols].unsqueeze(0).broadcast_to([rep, rows, GROUP])
                                             ).then_inc(y4[u], 16)
                            wait_old(sp, s4["sel_sb"], i, u)
                            wait_old(sp, s4["idx_ready"], i, u)
                            sp.dma_start(dcol_i[u][:], dst_cols[g1].rearrange(group)).then_inc(ld4[u], 16)
                            sp.dma_start(dnext[u][:], dst_next[g1].rearrange(group)).then_inc(ld4[u], 16)
                            sp.dma_start(dline[u][:], dst_line[bass.ds(i, 1), u * GROUP:(u + 1) * GROUP].broadcast_to([P, GROUP])
                                         ).then_inc(ld4[u], 16)
                            wait_old(sp, s4["u_ready"], i, u)
                            sp.dma_start(x1d[u][:].rearrange(flat), x1_dst[g1].rearrange(group)).then_inc(ld4[u], 16)
                        if k == 2:
                            sp.wait_ge(s4["T_v"], new(i, u))
                            load_idx(i + 1, u)

                    prime(sp, s4.values())
                    sp.sem_inc(primed_4, 1)
                    load_idx(0, 0)
                    load_idx(0, 1)
                    staggered(sp, ITERS, 7, step)
                    for u in range(2):
                        sp.wait_ge(ix4[u], 16 * ITERS + 16)

                @block.gpsimd
                def _(pool):
                    def gather(i, u):
                        pool.wait_ge(ix4[u], 16 * i + 16)
                        pool.sem_inc(go, 1)
                        for t in range(TG):
                            pool.indirect_dma_start(out=xg[u][:, t, :], out_offset=None, in_=x1,
                                                    in_offset=bass.IndirectOffsetOnAxis(ap=sidx[u][:, t:t + 1], axis=0)
                                                    ).then_inc(xg4[u], 16)

                    def step(i, u, k):
                        if k == 2:
                            pool.wait_ge(s4["T_v"], new(i, u))
                            gather(i + 1, u)
                        if k == 12:
                            pool.wait_ge(s4["q"], new(i, u))
                            pool.tensor_tensor(r[u][:], q[u][:], half[:, 0:TG], ALU.pow).then_inc(s4["rstd"], 1)
                        if k == 13:
                            pool.wait_ge(s4["out_ready"], new(i, u))
                            pool.sem_inc(go, 1)
                            for t in range(TG):
                                pool.indirect_dma_start(out=out, in_=od[u][:, t, :], in_offset=None,
                                                        out_offset=bass.IndirectOffsetOnAxis(ap=tidx[u][:, t:t + 1], axis=0),
                                                        bounds_check=NP - 1, oob_is_err=False).then_inc(sc4[u], 16)

                    pool.wait_ge(primed_4, 1)
                    for u in range(2):
                        pool.dma_start(od[u][0:16, 0, :], x[0:16, :]).then_inc(sc4[u], 16)
                        gather(0, u)
                    staggered(pool, ITERS, 7, step)
                    for u in range(2):
                        pool.wait_ge(sc4[u], 64 * ITERS + 16)
                        pool.wait_ge(xg4[u], 64 * ITERS + 64)

                @block.tensor
                def _(pe):
                    def job(i, u, bank, waits, w, rhs, done):
                        for name in waits:
                            pe.wait_ge(s4[name], new(i, u))
                        pe.matmul(B(u, bank)[0:w.shape[1], 0:GROUP], w, rhs, start=True, stop=True).then_inc(s4[done], 1)

                    def step(i, u, k):
                        if k == 1:
                            pe.wait_ge(xg4[u], 64 * i + 64)
                            wait_old(pe, s4["o_sb"], i, u)
                            for bank, c, n, done in ((0, 0, 64, "T_s"), (1, CS, 96, "T_v")):
                                pe.sem_inc(go, 1)
                                for t in range(TG):
                                    last = pe.transpose(B(u, bank)[0:n, t * P:(t + 1) * P], xg[u][:, t, c:c + n], id_sb[:])
                                last.then_inc(s4[done], 1)
                            pe.wait_ge(em4[u], 16 * i + 16)
                            job(i, u, 2, [], W("fc1"), emb[u][:], "hid_ps")
                        if k == 2:
                            job(i, u, 3, ["Ts_sb"], W("l1_xs"), Ts[u][:], "xs_ps")
                            job(i, u, 0, ["Tv_sb"], W("l1_xv"), Tv[u][:], "xv_ps")
                            job(i, u, 1, ["hid_sb"], W("fc2_s01"), hid[u][:], "w_s01")
                            job(i, u, 2, [], W("fc2_s23"), hid[u][:], "w_s23")
                        if k == 4:
                            job(i, u, 3, ["q_s23"], W("fc2_vs"), hid[u][:], "w_vs")
                            job(i, u, 0, ["q_vv"], W("fc2_vv"), hid[u][:], "w_vv")
                        if k == 5:
                            for name in ("m_s01", "m_s23", "m_vs", "m_vv"):
                                pe.wait_ge(s4[name], new(i, u))
                            for t in range(TG):
                                o = B(u, 1 + t // 2)[:, (t % 2) * MSG:(t % 2 + 1) * MSG]
                                ee = slice(t * P, (t + 1) * P)
                                pe.matmul(o[:, 0:128], m_s01[u][:, ee], W("l1_s01"), start=True, stop=False, skip_group_check=True)
                                pe.matmul(o[:, 128:192], m_s23[u][:, ee], W("l1_s23"), start=False, stop=False, skip_group_check=True)
                                pe.matmul(o[:, 96:192], m_vs[u][:, ee], W("l1_vs"), start=False, stop=False, skip_group_check=True)
                                last = pe.matmul(o[:, 0:96], m_vv[u][:, ee], W("l1_vv"), start=False, stop=True, skip_group_check=True)
                                if t == 1:
                                    last.then_inc(s4["msg_ps0"], 1)
                            last.then_inc(s4["msg_ps1"], 1)
                        if k == 6:
                            pe.wait_ge(ld4[u], 64 * i + 64)
                            for bank, c, n, done in ((3, 0, 64, "N_s"), (0, CS, 96, "N_v")):
                                pe.sem_inc(go, 1)
                                for t in range(TG):
                                    last = pe.transpose(B(u, bank)[0:n, t * P:(t + 1) * P], x1d[u][:, t, c:c + n], id_sb[:])
                                last.then_inc(s4[done], 1)
                        if 7 <= k < 7 + TG:
                            t = k - 7
                            o = B(u, 1 + t % 2)[:, 0:MSG]
                            n = 8 * i + 4 * u + t
                            prev = agg[u][:, t - 1, :] if t else agg[1 - u][:, TG - 1, :]
                            if t == 0:
                                pe.wait_ge(s4["msg_sb0"], new(i, u))
                                pe.wait_ge(s4["msg_sb1"], new(i, u))
                                pe.wait_ge(s4["sel_sb"], new(i, u))
                            if t >= 2:
                                pe.wait_ge(s4["agg_sb"], n)
                            pe.matmul(o, sel[u][:, t, :], msg[u][:, t, :], start=True, stop=False)
                            pe.wait_ge(s4["agg_sb"], n + 1)
                            pe.matmul(o, sel_c[u][:, t, :], prev, start=False, stop=True).then_inc(s4["agg_ps"], 1)
                        if k == 8:
                            pe.wait_ge(s4["Ns_sb"], new(i, u))
                            pe.wait_ge(s4["Nv_sb"], new(i, u))
                            for t in range(TG):
                                o = B(u, 3 if t < 2 else 0)[:, (t % 2) * MSG:(t % 2 + 1) * MSG]
                                ee = slice(t * P, (t + 1) * P)
                                pe.matmul(o[:, 0:96], Ns[u][:, ee], W("self_s"), start=True, stop=False, skip_group_check=True)
                                last = pe.matmul(o[:, 96:192], Nv[u][:, ee], W("self_v"), start=False, stop=True, skip_group_check=True)
                            last.then_inc(s4["self_ps"], 1)

                    pe.wait_ge(primed_4, 1)
                    staggered(pe, ITERS, 7, step)

                @block.scalar
                def _(act):
                    def step(i, u, k):
                        if k == 1:
                            act.wait_ge(s4["T_s"], new(i, u))
                            wait_old(act, s4["xv_ps"], i, u)
                            nc.scalar.activation(Ts[u][:], B(u, 0)[0:64, :], ACT.Copy).then_inc(s4["Ts_sb"], 1)
                            act.wait_ge(s4["T_v"], new(i, u))
                            nc.scalar.activation(Tv[u][:], B(u, 1)[0:96, :], ACT.Copy).then_inc(s4["Tv_sb"], 1)
                            act.wait_ge(s4["hid_ps"], new(i, u))
                            wait_old(act, s4["w_vv"], i, u)
                            nc.scalar.activation(hid[u][:], B(u, 2)[0:64, :], ACT.Silu, bias=V("b_fc1", 64)).then_inc(s4["hid_sb"], 1)
                        if k == 5:
                            wait_old_sums(act, s4["agg_ps"], i, u)
                            act.wait_ge(s4["msg_ps0"], new(i, u))
                            nc.scalar.activation(msg[u][:, 0:2, :].rearrange("p t f -> p (t f)"), B(u, 1)[:, 0:2 * MSG], ACT.Copy).then_inc(s4["msg_sb0"], 1)
                            act.wait_ge(s4["msg_ps1"], new(i, u))
                            nc.scalar.activation(msg[u][:, 2:4, :].rearrange("p t f -> p (t f)"), B(u, 2)[:, 0:2 * MSG], ACT.Copy).then_inc(s4["msg_sb1"], 1)
                        if k == 6:
                            act.wait_ge(s4["N_s"], new(i, u))
                            wait_old(act, s4["self_ps"], i, u)
                            nc.scalar.activation(Ns[u][:], B(u, 3)[0:64, :], ACT.Copy).then_inc(s4["Ns_sb"], 1)
                            act.wait_ge(s4["N_v"], new(i, u))
                            nc.scalar.activation(Nv[u][:], B(u, 0)[0:96, :], ACT.Copy).then_inc(s4["Nv_sb"], 1)
                        if 7 <= k < 7 + TG:
                            t = k - 7
                            if t == 0:
                                wait_old(act, s4["o_sb"], i, u)
                            act.wait_ge(s4["agg_ps"], 8 * i + 4 * u + t + 2)
                            nc.scalar.activation(agg[u][:, t, :], B(u, 1 + t % 2)[:, 0:MSG], ACT.Copy).then_inc(s4["agg_sb"], 1)
                        if k == 12:
                            act.wait_ge(s4["o_sb"], new(i, u))
                            wait_old(act, s4["u_ready"], i, u)
                            nc.scalar.activation(gates[u][:], o_sb[u][:, :, 0:96], ACT.Silu).then_inc(s4["gates_sb"], 1)

                    act.wait_ge(primed_4, 1)
                    staggered(act, ITERS, 7, step)

                @block.vector
                def _(dve):
                    v = nc.vector

                    def step(i, u, k):
                        if k == 2:
                            dve.wait_ge(ld4[u], 64 * i + 64)
                            wait_old_sums(dve, s4["agg_ps"], i, u)
                            v.tensor_copy(dcol[u][:], dcol_i[u][:])
                            v.tensor_tensor(tidx_f[u][:], dcol_i[u][:, 1:], dnext[u][:], ALU.is_equal).then_inc(s4["dcol_sb"], 1)
                            dve.wait_ge(s4["dcol_sb"], new(i, u))
                            for t in range(TG):
                                line = dline[u][:, t * P:(t + 1) * P]
                                v.tensor_scalar(sel[u][:, t, :], line, dcol[u][:, t + 1:t + 2], None, ALU.is_equal)
                                last = v.tensor_scalar(sel_c[u][:, t, :], line, dcol[u][:, t:t + 1], V("last_row", P),
                                                       ALU.is_equal, ALU.mult)
                            last.then_inc(s4["sel_sb"], 1)
                        if k == 3:
                            dve.wait_ge(y4[u], 64 * i + 64)
                            dve.wait_ge(s4["xs_ps"], new(i, u))
                            wait_old(dve, s4["msg_ps1"], i, u)
                            v.tensor_tensor(m_s01[u][:], ybc[u][:, 0, :], B(u, 3)[:, :], ALU.mult).then_inc(s4["q_s01"], 1)
                            v.tensor_tensor(m_s23[u][:], ybc[u][:, 1, :], B(u, 3)[:, :], ALU.mult).then_inc(s4["q_s23"], 1)
                            dve.wait_ge(s4["xv_ps"], new(i, u))
                            v.tensor_tensor(m_vs[u][:], ybc[u][0:96, 2, :], B(u, 0)[0:96, :], ALU.mult).then_inc(s4["q_vs"], 1)
                            v.tensor_tensor(m_vv[u][:], ybc[u][0:96, 3, :], B(u, 0)[0:96, :], ALU.mult).then_inc(s4["q_vv"], 1)
                        if k == 4:
                            for bank, rows, wname, bias, m, q_ok, done in (
                                    (1, 128, "w_s01", "b_s01", m_s01, "q_s01", "m_s01"), (2, 128, "w_s23", "b_s23", m_s23, "q_s23", "m_s23"),
                                    (3, 96, "w_vs", "b_vs", m_vs, "q_vs", "m_vs"), (0, 96, "w_vv", "b_vv", m_vv, "q_vv", "m_vv")):
                                dve.wait_ge(s4[wname], new(i, u))
                                dve.wait_ge(s4[q_ok], new(i, u))
                                v.scalar_tensor_tensor(m[u][:], B(u, bank)[0:rows, :], V(bias, rows), m[u][:], ALU.add, ALU.mult
                                                       ).then_inc(s4[done], 1)
                        if k == 11:
                            dve.wait_ge(s4["self_ps"], new(i, u))
                            dve.wait_ge(s4["agg_sb"], 8 * i + 4 * u + 5)
                            wait_old(dve, s4["gates_sb"], i, u)
                            for n in range(2):
                                last = v.tensor_tensor(o_sb[u][:, 2 * n:2 * n + 2, :].rearrange("p t f -> p (t f)"),
                                                       agg[u][:, 2 * n:2 * n + 2, :].rearrange("p t f -> p (t f)"),
                                                       B(u, 3 if n == 0 else 0)[:, 0:2 * MSG], ALU.add)
                            last.then_inc(s4["o_sb"], 1)
                            dve.wait_ge(sc4[u], 64 * i + 16)
                            v.scalar_tensor_tensor(tidx[u][:], tidx_f[u][:], float(SKIP), dcol[u][:, 1:], ALU.mult, ALU.add
                                                   ).then_inc(s4["idx_ready"], 1)
                        if k == 12:
                            dve.wait_ge(s4["gates_sb"], new(i, u))
                            for n in range(2):
                                tt = slice(2 * n, 2 * n + 2)
                                last = v.tensor_tensor(gv[u][:, tt, :].rearrange("p t (k c) -> p t k c", c=3),
                                                       gates[u][:, tt, CS:96].unsqueeze(3).broadcast_to([P, 2, CV, 3]),
                                                       o_sb[u][:, tt, 96:192].rearrange("p t (c k) -> p t k c", c=3), ALU.mult)
                            last.then_inc(s4["gv_ready"], 1)
                            v.scalar_tensor_tensor(uu[u][:, :, 0:CS], x1d[u][:, :, 0:CS], 2.0, gates[u][:, :, 0:CS], ALU.mult, ALU.add)
                            dve.wait_ge(s4["gv_ready"], new(i, u))
                            v.scalar_tensor_tensor(uu[u][:, :, CS:D], x1d[u][:, :, CS:D], 2.0, gv[u][:], ALU.mult, ALU.add
                                                   ).then_inc(s4["u_ready"], 1)
                            dve.wait_ge(s4["u_ready"], new(i, u))
                            for t in range(TG):
                                last = v.bn_stats(st[u][:, t, :], uu[u][:, t, :])
                            last.then_inc(s4["bn"], 1)
                            dve.wait_ge(s4["bn"], new(i, u))
                            dve.sem_inc(go, 1)
                            for t in range(TG):
                                last = v.bn_aggr(mv[u][:, t, :], st[u][:, t, :])
                            last.then_inc(s4["mv"], 1)
                            dve.wait_ge(s4["mv"], new(i, u))
                            v.tensor_scalar(q[u][:], mv[u][:, :, 1], EPS, None, ALU.add).then_inc(s4["q"], 1)
                        if k == 13:
                            dve.wait_ge(s4["rstd"], new(i, u))
                            dve.wait_ge(sc4[u], 64 * i + 16)
                            for t in range(TG):
                                last = v.tensor_scalar(od[u][:, t, :], uu[u][:, t, :], mv[u][:, t, 0:1], r[u][:, t:t + 1],
                                                       ALU.subtract, ALU.mult)
                            last.then_inc(s4["out_ready"], 1)

                    v.memset(agg[1][:], 0.0).then_inc(s4["prime"], 1)
                    dve.wait_ge(s4["prime"], 2)
                    dve.wait_ge(primed_4, 1)
                    staggered(dve, ITERS, 7, step)


def pack_weights(np, w):
    a = np.zeros((P, WCOLS), np.float32)
    vec = np.zeros((P, len(VECS)), np.float32)

    def blk(name):
        c, r, n = COL[name]
        return a[:r, c:c + n]

    g0 = lambda n: np.asarray(w["L0_gnn_" + n])
    g1 = lambda n: np.asarray(w["L1_gnn_" + n])
    b = blk("msg_s")
    for j in range(2):
        b[:64, j::2] = g0("Ws_src")
        b[64:, j::2] = g0("Ws_dst")
    for c in range(3):
        blk("msg_v_src")[c::3, c::3] = g0("Wv_src")
        blk("msg_v_dst")[c::3, c::3] = g0("Wv_dst")
    wr = g0("W_rbf")
    ss, sv, vs, vv0, vv1 = wr[:, 0:64], wr[:, 64:128], wr[:, 128:160], wr[:, 160:192], wr[:, 192:224]
    blk("rbf_s")[1::5, 0::2] = ss
    blk("rbf_s")[0::5, 1::2] = sv
    for c in range(3):
        nxt, prv = (c + 1) % 3, (c + 2) % 3
        blk("rbf_vv0")[2 + c::5, c::3] = vv0
        blk("rbf_vs")[1::5, c::3] = vs
        blk("rbf_vv1_next")[2 + nxt::5, c::3] = vv1
        blk("rbf_vv1_prev")[2 + prv::5, c::3] = vv1
        blk("alpha_dotv")[c::3, :] = g0("W_alpha")[64:]
        blk("gate")[0::2, c::3] = g0("Wg")
        blk("val_v_sv")[1::2, c::3] = g0("Wv_val")[0:64]
        blk("val_v_vs")[c::3, c::3] = g0("Wv_val")[64:96]
        blk("val_v_next")[c::3, prv::3] = g0("Wv_val")[96:128]
        blk("val_v_prev")[c::3, nxt::3] = g0("Wv_val")[96:128]
        blk("out_dotv")[c::3, :] = g0("Ws_vlin")[64:]
        blk("out_vs")[c::3, c * 32:c * 32 + 32] = g0("Wv_vlin")[64:96]
        blk("out_next")[c::3, prv * 32:prv * 32 + 32] = g0("Wv_vlin")[96:128]
        blk("out_prev")[c::3, nxt * 32:nxt * 32 + 32] = g0("Wv_vlin")[96:128]
        blk("proj_v")[c * 32:c * 32 + 32, c::3] = g0("Wpv")
        blk("l1_xv")[c::3, c::3] = g1("W1_v")
        blk("fc2_vs")[:, c::3] = g1("fc_w2")[:, 128:160]
        blk("fc2_vv")[:, c::3] = g1("fc_w2")[:, 160:192]
        blk("l1_vs")[c::3, c * 32:c * 32 + 32] = g1("W2_v")[64:96]
        blk("l1_vv")[c::3, :] = g1("W2_s")[64:96]
        blk("self_v")[c::3, c * 32:c * 32 + 32] = g1("Wsc_v")
        for j in range(2):
            blk("val_dotv")[c::3, j::2] = g0("Ws_val")[64:]
        for name, v in (("gamma_v3", g0("gamma_v")), ("w2_vv0", g0("w2_vv0")), ("w2_vs", g0("w2_vs")),
                        ("w2_vv1", g0("w2_vv1")), ("b_vs", g1("fc_b2")[128:160]), ("b_vv", g1("fc_b2")[160:192])):
            vec[c:96:3, VCOL[name]] = v
    blk("alpha_s")[0::2, :] = g0("W_alpha")[:64]
    for j in range(2):
        blk("val_s")[0::2, j::2] = g0("Ws_val")[:64]
        blk("l1_xs")[:, j::2] = g1("W1_s")
        blk("fc2_s01")[:, j::2] = g1("fc_w2")[:, 64 * j:64 * j + 64]
        blk("fc2_s23")[:, j::2] = g1("fc_w2")[:, 64:128]
        blk("out_s23")[j::2, 32 * j:32 * j + 32] = g0("Wv_vlin")[0:64]
        blk("l1_s23")[j::2, 32 * j:32 * j + 32] = g1("W2_v")[0:64]
        vec[64 * j:64 * j + 64, VCOL["gamma_s2"]] = g0("gamma_s")
        vec[64 * j:64 * j + 64, VCOL["beta_s2"]] = g0("beta_s")
        vec[j::2, VCOL["w2_s01"]] = (g0("w2_ss"), g0("w2_sv"))[j]
        vec[j::2, VCOL["w2_s23"]] = g0("w2_sv")
        vec[j::2, VCOL["b_s01"]] = g1("fc_b2")[64 * j:64 * j + 64]
        vec[j::2, VCOL["b_s23"]] = g1("fc_b2")[64:128]
    for h in range(HEADS):
        blk("alpha_dot")[16 * h:16 * h + 16, h] = g0("alpha_dot")[0, h]
    blk("out_s01")[0::2, 0:64] = g0("Ws_vlin")[:64]
    blk("out_s01")[1::2, 64:96] = g0("Wv_vlin")[0:64]
    blk("proj_s")[:] = g0("Wps")
    blk("fc1")[:] = g1("fc_w1")
    blk("l1_s01")[0::2, 0:96] = g1("W2_s")[:64]
    blk("l1_s01")[1::2, 96:128] = g1("W2_v")[0:64]
    blk("self_s")[:] = g1("Wsc_s")
    vec[:64, VCOL["b_fc1"]] = g1("fc_b1")
    vec[P - 1, VCOL["last_row"]] = 1.0
    return a, vec


def kernel(**inputs):
    import numpy as np
    import concourse.bacc as bacc
    from concourse import mybir as mb
    from concourse.bass_utils import run_bass_kernel_spmd as run

    def padded(a, n, fill):
        a = np.asarray(a)
        return np.concatenate([a, np.full((n - a.shape[0],) + a.shape[1:], fill, a.dtype)])

    def tiles(a):
        return np.ascontiguousarray(a.reshape(GROUPS, TG, P).transpose(0, 2, 1))

    src = padded(inputs["src"], EP, 0)
    dst = padded(inputs["dst"], EP, NP - 1)
    before = tiles(np.concatenate([np.full(P, -1, np.int32), dst[:-P]]))
    dst_t = tiles(dst)
    dst_cols = np.concatenate([before[:, :, 0:1], dst_t], axis=2)
    rows = np.zeros((EROWS, EP + CHUNK), np.float32)
    y = np.asarray(inputs["edge_attr_4"]).T
    rows[ONE] = 1.0
    rows[Y0:Y0 + 4, :EDGES] = y
    rows[YX + 3:YX + 5, :EDGES] = y[1:3]
    rows[RBF:RBF + 16, :EDGES] = np.asarray(inputs["edge_attr_16"]).T
    rows[EMB:EMB + 8, :EDGES] = np.asarray(inputs["edge_attr_8"]).T
    weights, vectors = pack_weights(np, inputs)
    head_mask = np.zeros((1, SEG), np.float32)
    head_mask[0, ::ITERS] = -BIG
    arrays = {
        "x": padded(inputs["x"], NP, 0), "src_idx": padded(tiles(src), GROUPS + 2, 0), "dst_idx": padded(dst_t, GROUPS + 2, 0),
        "dst_cols": np.ascontiguousarray(dst_cols),
        "dst_next": tiles(np.concatenate([dst[1:], np.full(1, -1, np.int32)])),
        "dst_line": dst.reshape(ITERS, CHUNK), "edge_rows": rows, "weights": weights, "vectors": vectors,
        "ident": np.eye(P, dtype=np.float32), "head_mask": head_mask,
    }
    nc = bacc.Bacc("TRN2", target_bir_lowering=False, num_devices=1)
    args, named = [], {}
    for name, a in arrays.items():
        named[f"in_{name}"] = a
        args.append(nc.dram_tensor(f"in_{name}", a.shape, mb.dt.from_np(a.dtype), kind="ExternalInput").ap())
    out = nc.dram_tensor("out_rows", (NP, D), F32, kind="ExternalOutput").ap()
    build(nc, *args, out)
    r = run(nc, [named], core_ids=[0])
    return r.results[0]["out_rows"][:NODES]
```

```python
from contextlib import ExitStack

import concourse.bass as bass
from concourse import mybir

F32 = mybir.dt.float32
I32 = mybir.dt.int32
ALU = mybir.AluOpType
ACT = mybir.ActivationFunctionType

P = 128
NODES, EDGES = 50000, 25000
CS, CV, HEADS = 64, 32, 4
CV3 = 3 * CV
D = CS + CV3
TG = 4
GROUP = TG * P
ITERS = 25
CHUNK = 2 * GROUP
EP = ITERS * CHUNK
GROUPS = 2 * ITERS
TILES = EP // P
NODE_GROUPS = 4
NP = NODE_GROUPS * ITERS * GROUP
assert NP >= NODES
EPS = 1e-5
BIG = 1e30
SKIP = 1 << 20
SEG = HEADS * ITERS
AGG = D + HEADS
MSG = 96 + CV3

BLOCKS = [
    ("msg_s", 128, 128), ("msg_v_src", 96, 96), ("msg_v_dst", 96, 96),
    ("rbf_s", 80, 128), ("rbf_vv0", 80, 96), ("rbf_vs", 80, 96), ("rbf_vv1_next", 80, 96), ("rbf_vv1_prev", 80, 96),
    ("alpha_s", 128, 64), ("alpha_dotv", 96, 64), ("val_s", 128, 128), ("val_dotv", 96, 128),
    ("gate", 128, 96), ("val_v_sv", 128, 96), ("val_v_vs", 96, 96), ("val_v_next", 96, 96), ("val_v_prev", 96, 96),
    ("alpha_dot", 64, 4),
    ("out_s01", 128, 96), ("out_s23", 128, 64), ("out_dotv", 96, 64), ("out_vs", 96, 96),
    ("out_next", 96, 96), ("out_prev", 96, 96), ("proj_s", 64, 64), ("proj_v", 96, 96),
    ("l1_xs", 64, 128), ("l1_xv", 96, 96), ("fc1", 8, 64), ("fc2_s01", 64, 128), ("fc2_s23", 64, 128),
    ("fc2_vs", 64, 96), ("fc2_vv", 64, 96),
    ("l1_s01", 128, 128), ("l1_s23", 128, 64), ("l1_vs", 96, 96), ("l1_vv", 96, 96),
    ("self_s", 64, 96), ("self_v", 96, 96),
]
COL, at = {}, 0
for _name, _rows, _cols in BLOCKS:
    COL[_name] = (at, _rows, _cols)
    at += _cols
WCOLS = at
VECS = ["gamma_s2", "beta_s2", "gamma_v3", "w2_s01", "w2_s23", "w2_vv0", "w2_vs", "w2_vv1",
        "b_s01", "b_s23", "b_vs", "b_vv", "b_fc1", "last_row"]
VCOL = {n: i for i, n in enumerate(VECS)}
ONE, Y0, YX, RBF, EMB = 0, 1, 2, 7, 23
EROWS = 31
ATTRS = 4 + 16 + 8


def staggered(eng, iters, period, depth, step):
    apart = (period - 1) | 1
    assert 2 * depth + apart <= 4 * period

    def turn(i, first=False, last=False):
        for place in range(2 * period):
            for back in (1, 0):
                if (first and back) or (last and not back):
                    continue
                at = place + 2 * period * back
                for u in range(2):
                    if (at - apart * u) % 2 == 0 and 0 <= at - apart * u < 2 * depth:
                        step(i - back, u, (at - apart * u) // 2)

    turn(0, first=True)
    with eng.Fori(1, iters) as i:
        turn(i)
    turn(iters, last=True)


def interleaved(eng, iters, edge_step, node_step):
    def turn(i, first=False, last=False):
        for place in range(20):
            for back in (1, 0):
                if (first and back) or (last and not back):
                    continue
                at = place + 20 * back
                for u in range(2):
                    if (at - 9 * u) % 2 == 0 and 0 <= at - 9 * u < 24:
                        edge_step(i - back, u, (at - 9 * u) // 2)
                for n in range(NODE_GROUPS):
                    if 0 <= at - 5 * n < 13:
                        node_step(i - back, n, at - 5 * n)

    turn(0, first=True)
    with eng.Fori(1, iters) as i:
        turn(i)
    turn(iters, last=True)


def new(i, u):
    return 2 * i + u + 2


def wait_old(eng, sem, i, u):
    if not (isinstance(i, int) and i == 0):
        eng.wait_ge(sem, 2 * i + u)


def wait_old_sums(eng, sem, i, u):
    if not (isinstance(i, int) and i == 0):
        eng.wait_ge(sem, 8 * i + 4 * u - 3)


def new_node(i, n):
    return NODE_GROUPS * i + n + 2


def wait_old_node(eng, sem, i, n, back=2):
    if not isinstance(i, int) or NODE_GROUPS * i + n >= back:
        eng.wait_ge(sem, NODE_GROUPS * i + n + 2 - back)


def build(nc, x, given, records, edge_ids, dst_grid, next_grid, before_mask, weights, vectors, ident, head_mask, out):
    src_idx, dst_idx, dst_cols, dst_next, dst_line, edge_rows = (
        nc.dram_tensor(name, list(a.shape), a.dtype).ap() for name, a in given.items())
    h_rows = nc.dram_tensor("h_rows", [GROUPS, P, TG * D], F32).ap()
    x1 = nc.dram_tensor("x1", [NP, D], F32).ap()
    x1_dst = nc.dram_tensor("x1_dst", [GROUPS, P, TG * D], F32).ap()

    with ExitStack() as top:
        def sem_in(ctx):
            made = []

            def new_sem(name):
                made.append(ctx.enter_context(nc.semaphore(name)))
                return made[-1]

            def clear():
                with nc.Block() as block:
                    @block.gpsimd
                    def _(pool):
                        for s in made:
                            pool.sem_clear(s)

            ctx.callback(clear) if ctx is not top else None
            return new_sem

        def sb_in(ctx):
            return lambda name, shape, dt=F32: ctx.enter_context(nc.sbuf_tensor(name, shape, dt))

        sb, sem = sb_in(top), sem_in(top)
        top_sem = sem
        w_sb = sb("w_sb", [P, WCOLS])
        v_sb = sb("v_sb", [P, len(VECS)])
        id_sb = sb("id_sb", [P, P])
        go = sem("go")
        half = sb("half", [P, 2 * TG * 2])
        msg_bias = sb("msg_bias", [P, 1])
        a_edge = sb("a_edge", [P, 2 * TG, HEADS, ITERS])
        ex_edge = sb("ex_edge", [P, 2 * TG, HEADS, ITERS])

        def W(name, rows=None):
            c, r, n = COL[name]
            return w_sb[0:rows or r, c:c + n]

        def V(name, rows):
            return v_sb[0:rows, VCOL[name]:VCOL[name] + 1]

        psum = [top.enter_context(nc.psum_tensor(f"bank{b}", [P, 512], F32)) for b in range(8)]

        def B(u, b):
            return psum[4 * u + b]

        const_in, scaled, bias_ps, bias_ok = sem("const_in"), sem("scaled"), sem("bias_ps"), sem("bias_ok")
        with nc.Block() as block:
            @block.sync
            def _(sp):
                sp.dma_start(w_sb[:], weights).then_inc(const_in, 16)
                sp.dma_start(v_sb[:], vectors).then_inc(const_in, 16)
                sp.dma_start(id_sb[:], ident).then_inc(const_in, 16)

            @block.tensor
            def _(pe):
                pe.wait_ge(const_in, 48)
                pe.matmul(psum[0][:, 0:1], W("msg_s"), V("beta_s2", 128), start=True, stop=True).then_inc(bias_ps, 1)

            @block.vector
            def _(dve):
                dve.memset(half[:], -0.5)
                dve.wait_ge(bias_ps, 1)
                dve.tensor_copy(msg_bias[:], psum[0][:, 0:1]).then_inc(bias_ok, 1)
                dve.wait_ge(const_in, 48)
                r3, r2 = 3 ** -0.5, 2 ** -0.5
                for name, vec, scale in (
                        ("msg_s", "gamma_s2", 1.0), ("msg_v_src", "gamma_v3", 1.0), ("msg_v_dst", "gamma_v3", 1.0),
                        ("out_s01", "w2_s01", 1.0), ("out_s23", "w2_s23", 1.0), ("out_dotv", "w2_vv0", r3),
                        ("out_vs", "w2_vs", 1.0), ("out_next", "w2_vv1", r2), ("out_prev", "w2_vv1", -r2)):
                    m = W(name)
                    dve.tensor_scalar(m, m, V(vec, m.shape[0]), scale, ALU.mult, ALU.mult)
                agg = 48 ** -0.5
                for name, scale in (
                        ("alpha_dotv", r3), ("val_dotv", r3), ("val_v_next", r2), ("val_v_prev", -r2),
                        ("l1_xs", 1 / 8), ("l1_xv", 32 ** -0.5), ("l1_s01", agg), ("l1_s23", agg), ("l1_vs", agg),
                        ("l1_vv", agg * r3), ("self_s", 1 / 8), ("self_v", 32 ** -0.5)):
                    last = dve.tensor_scalar_mul(W(name), W(name), scale)
                last.then_inc(scaled, 1)

        grid_in, line_in, rows_in, placed = sem("grid_in"), sem("line_in"), sem("rows_in"), top_sem("placed")
        copied, permuted = sem("copied"), sem("permuted")
        disorder, total, flag_ok, raw = sem("disorder"), sem("total"), sem("flag_ok"), sem("raw_line")
        swept, in_tile, ranked, keyed, lowered = (sem(n) for n in ("swept", "in_tile", "ranked", "keyed", "lowered"))
        in_step = sem("in_step")
        with ExitStack() as ctx:
            sb = sb_in(ctx)
            SWEEP = EP // 5
            grid, grid_next, falls = sb("grid", [P, TILES], I32), sb("grid_next", [P, TILES], I32), sb("falls", [P, TILES])
            any_fall, ones, flag = sb("any_fall", [P, 1]), sb("ones_col", [P, 1]), sb("flag", [1, 1], I32)
            line, key = sb("line", [P, EP]), sb("key", [P, TILES])
            line_i = sb("line_i", [P, CHUNK], I32)
            less, same, before = sb("less", [P, SWEEP]), sb("same", [P, P]), sb("before", [P, P])
            counts, rank = sb("counts", [P, 6]), sb("rank", [P, 1], I32)
            rank_f = sb("rank_f", [P, 1])
            rec, ids = sb("rec", [P, ATTRS]), sb("ids", [P, 2], I32)
            sorted_rec = nc.dram_tensor("sorted_rec", [EP, ATTRS], F32).ap()
            sorted_ids = nc.dram_tensor("sorted_ids", [EP + 1, 2], I32).ap()
            with nc.Block() as block:
                @block.sync
                def _(sp):
                    sp.dma_start(grid[:], dst_grid).then_inc(grid_in, 16)
                    sp.dma_start(grid_next[:], next_grid).then_inc(grid_in, 16)
                    for a, b in zip((src_idx, dst_idx, dst_cols, dst_next, dst_line, edge_rows), given.values()):
                        sp.dma_start(a, b).then_inc(copied, 16)
                    sp.wait_ge(copied, 96)
                    sp.wait_ge(flag_ok, 1)
                    unordered = sp.value_load(flag[0:1, 0:1], min_val=0, max_val=1)
                    with sp.If(unordered > 0):
                        sp.dma_start(before[:], before_mask).then_inc(grid_in, 16)
                        with sp.Fori(0, ITERS) as c:
                            sp.wait_ge(keyed, c + 1)
                            sp.dma_start(line_i[:], given["dst_line"][bass.ds(c, 1), :].broadcast_to([P, CHUNK])).then_inc(line_in, 16)
                        with sp.Fori(0, TILES) as t:
                            sp.wait_ge(placed, 32 * t + 16)
                            sp.dma_start(rec[:], records[bass.ds(t * P, P), :]).then_inc(rows_in, 16)
                            sp.dma_start(ids[:], edge_ids[bass.ds(t * P, P), :]).then_inc(rows_in, 16)
                        sp.wait_ge(placed, 32 * TILES + 16)
                        with sp.Fori(0, GROUPS) as g:
                            for array, at, shift, column in ((src_idx, 0, 0, 0), (dst_idx, 0, 0, 1), (dst_cols, 1, 0, 1),
                                                             (dst_next, 0, 1, 1)):
                                sp.dma_start(array[bass.ds(g, 1), :, at:at + TG].rearrange("a p t -> (a p) t"),
                                             sorted_ids[bass.ds(g * GROUP + shift, GROUP), column:column + 1].rearrange(
                                                 "(t p) c -> p (t c)", p=P), allow_slow_non_contiguous=True).then_inc(permuted, 16)
                        with sp.Fori(1, GROUPS) as g:
                            sp.dma_start(dst_cols[bass.ds(g, 1), :, 0:1].rearrange("a p t -> (a p) t"),
                                         sorted_ids[bass.ds(g * GROUP - P, P), 1:2], allow_slow_non_contiguous=True).then_inc(permuted, 16)
                        n = 5 * GROUPS - 1
                        sp.dma_start(dst_line.rearrange("i c -> (i c)"), sorted_ids[0:EP, 1],
                                     allow_slow_non_contiguous=True).then_inc(permuted, 16)
                        for row, first, count in ((Y0, 0, 4), (YX + 3, 1, 2), (RBF, 4, 16), (EMB, 20, 8)):
                            for j in range(count):
                                sp.dma_start(edge_rows[row + j, 0:EP], sorted_rec[:, first + j],
                                             allow_slow_non_contiguous=True).then_inc(permuted, 16)
                                n += 1
                        sp.wait_ge(permuted, 16 * (n + 1))

                @block.gpsimd
                def _(pool):
                    pool.wait_ge(flag_ok, 1)
                    unordered = pool.value_load(flag[0:1, 0:1], min_val=0, max_val=1)
                    with pool.If(unordered > 0):
                        pool.memset(rank[:], NP).then_inc(lowered, 1)
                        pool.wait_ge(lowered, 1)
                        pool.dma_start(sorted_ids[EP:, 1:2], rank[0:1, :]).then_inc(placed, 16)
                        pool.wait_ge(placed, 16)
                        with pool.Fori(0, TILES) as t:
                            pool.wait_ge(ranked, t + 1)
                            pool.wait_ge(rows_in, 32 * t + 32)
                            pool.sem_inc(go, 1)
                            for rows, buf in ((sorted_rec, rec), (sorted_ids, ids)):
                                pool.indirect_dma_start(out=rows, out_offset=bass.IndirectOffsetOnAxis(ap=rank[:, 0:1], axis=0),
                                                        in_=buf[:], in_offset=None).then_inc(placed, 16)

                @block.tensor
                def _(pe):
                    pe.wait_ge(disorder, 1)
                    pe.matmul(psum[1][0:1, 0:1], any_fall[:], ones[:], start=True, stop=True).then_inc(total, 1)

                @block.vector
                def _(dve):
                    v = nc.vector
                    v.memset(ones[:], 1.0)
                    dve.wait_ge(grid_in, 32)
                    v.tensor_tensor(falls[:], grid_next[:], grid[:], ALU.is_lt).then_inc(raw, 1)
                    dve.wait_ge(raw, 1)
                    v.tensor_reduce(any_fall[:], falls[:], mybir.AxisListType.X, ALU.max).then_inc(disorder, 1)
                    dve.wait_ge(total, 1)
                    v.tensor_scalar(flag[:], psum[1][0:1, 0:1], 0.0, None, ALU.is_gt).then_inc(flag_ok, 1)
                    dve.wait_ge(flag_ok, 1)
                    unordered = dve.value_load(flag[0:1, 0:1], min_val=0, max_val=1)
                    with dve.If(unordered > 0):
                        v.tensor_scalar(key[:], grid[:], 2.0, 1.0, ALU.mult, ALU.add).then_inc(keyed, 1)
                        with dve.Fori(0, ITERS) as c:
                            dve.wait_ge(line_in, 16 * c + 16)
                            v.tensor_scalar(line[:, bass.ds(c * CHUNK, CHUNK)], line_i[:], 2.0, 1.0, ALU.mult, ALU.add
                                            ).then_inc(keyed, 1)
                        dve.wait_ge(keyed, ITERS + 1)
                        dve.wait_ge(grid_in, 48)
                        with dve.Fori(0, TILES) as t:
                            k = key[:, bass.ds(t, 1)]
                            for c in range(5):
                                v.tensor_scalar(less[:], line[:, c * SWEEP:(c + 1) * SWEEP], k, None, ALU.is_lt).then_inc(swept, 1)
                                dve.wait_ge(swept, 5 * t + c + 1)
                                last = v.tensor_reduce(counts[:, c:c + 1], less[:], mybir.AxisListType.X, ALU.add)
                                last.then_inc(in_tile, 1)
                                dve.wait_ge(in_tile, 7 * t + c + 1)
                            tile_line = line[:, bass.ds(t * P, P)]
                            v.scalar_tensor_tensor(same[:], tile_line, k, before[:], ALU.is_equal, ALU.mult).then_inc(in_tile, 1)
                            dve.wait_ge(in_tile, 7 * t + 6)
                            v.tensor_reduce(counts[:, 5:6], same[:], mybir.AxisListType.X, ALU.add).then_inc(in_tile, 1)
                            dve.wait_ge(in_tile, 7 * t + 7)
                            v.tensor_scalar(tile_line, tile_line, -1.0, None, ALU.add).then_inc(in_step, 1)
                            v.tensor_reduce(rank_f[:], counts[:], mybir.AxisListType.X, ALU.add).then_inc(in_step, 1)
                            dve.wait_ge(in_step, 2 * t + 2)
                            dve.wait_ge(placed, 32 * t + 16)
                            v.tensor_copy(rank[:], rank_f[:]).then_inc(ranked, 1)

        with ExitStack() as ctx:
            sem = sem_in(ctx)
            stages = ["z_ready", "zT_s", "zT_vs", "zT_vd", "zs_sb", "zvs_sb", "zvd_sb", "msgs_ps", "msgv_ps", "msgs_sb",
                      "msgv_sb", "w_s", "w_vs", "w_next", "w_prev", "w_vv0", "p_s", "p_vs", "p_next", "p_prev", "p_vv0",
                      "alpha_ps", "vals_ps", "fifth_sb", "leaky_sb", "vals_sb", "sig_sb", "svy_ps", "valv_ps", "gate_ps",
                      "gate_sb", "svy_sb", "valv_sum", "valv_sb", "a_ps", "a_sb", "prod_sb", "h_ps0", "h_ps1", "h_sb0",
                      "h_sb1", "stats_ready", "mv_ready", "sq_ready", "q_ready", "rstd_ready", "r_ready"]
            s0 = {n: sem("e0_" + n) for n in stages}
            x_in = [top_sem(f"x_in{u}") for u in range(2)]
            idx_in, rbf_in, y_in, h_out = ([sem(f"e0_{n}{u}") for u in range(2)] for n in ("idx", "rbf", "y", "h_out"))
            node_stages = ["x1_bn", "x1_mv", "x1_q", "x1_rstd", "x1_shift", "x1_ready", "T_s", "T_v", "Ts_sb", "Tv_sb", "o_ps",
                      "gates_sb", "gv_ready", "u_ready", "u_bn", "u_mv", "u_q", "u_rstd", "u_shift", "out_a", "out_b"]
            sn = {n: sem("n_" + n) for n in node_stages}
            xn_in, x1_out, xn_out = ([sem(f"n_{n}{u}") for u in range(2)] for n in ("xn_in", "x1_out", "xn_out"))
            primed = sem("primed")

            def node_rows(t, i, n):
                return t[bass.ds((NODE_GROUPS * i + n) * GROUP, GROUP), :].rearrange("(p t) d -> p (t d)", t=TG)

            def prime(sp, sems):
                for s in sems:
                    sp.sem_inc(s, 1)

            with nc.Block() as block:
                sb = sb_in(ctx)
                two = lambda name, shape, dt=F32: [sb(f"{name}{u}", shape, dt) for u in range(2)]
                sidx, didx = two("sidx", [P, TG], I32), two("didx", [P, TG], I32)
                xg = two("xg", [P, 2 * TG, D])
                z = two("z", [P, TG, 2 * D])
                stats, mv = two("stats", [P, 4 * TG, 6]), two("mv", [P, 4 * TG, 2])
                msq, q, rstd = two("msq", [P, 2 * TG]), two("q", [P, 4 * TG]), two("rstd", [P, 4 * TG])
                rbf_rep, y_rep, r80 = two("rbf_rep", [80, GROUP]), two("y_rep", [80, GROUP]), two("r80", [80, GROUP])
                ybc = two("ybc", [P, 6, GROUP])
                zs, zvs, zvd = two("zs", [P, GROUP]), two("zvs", [96, GROUP]), two("zvd", [96, GROUP])
                msgs, msgv = two("msgs", [P, GROUP]), two("msgv", [96, GROUP])
                p_s, p_vs, p_next, p_prev, p_vv0 = (two(n, [128 if n == "p_s" else 96, GROUP])
                                                    for n in ("p_s", "p_vs", "p_next", "p_prev", "p_vv0"))
                leaky, vals, sig, gate = (two("leaky", [64, GROUP]), two("vals", [P, GROUP]), two("sig", [P, GROUP]),
                                          two("gate", [96, GROUP]))
                valv = two("valv", [96, GROUP])
                m_s01, m_s23, m_vs, m_dot, m_next, m_prev = (two("m_" + n, [128 if n[0] == "s" else 96, GROUP])
                                                             for n in ("s01", "s23", "vs", "dot", "next", "prev"))
                h_sb = two("h_sb", [P, TG * D])

                xn, x1n, un, outn = (two(n, [P, TG, D]) for n in ("xn", "x1n", "un", "outn"))
                st1, st2 = two("st1", [P, TG, 6]), two("st2", [P, TG, 6])
                mv1, mv2 = two("mv1", [P, TG, 2]), two("mv2", [P, TG, 2])
                q1, q2, r1, r2_, shift1, shift2 = (two(n, [P, TG]) for n in ("q1", "q2", "r1", "r2_", "shift1", "shift2"))
                Ts, Tv = two("Ts", [64, GROUP]), two("Tv", [96, GROUP])
                gates, gv = two("gates", [P, TG, 96]), two("gv", [P, TG, CV3])
                flat = "p t d -> p (t d)"

                def E(u, b):
                    return psum[3 * u + b]

                @block.sync
                def _(sp):
                    def load_idx(i, u):
                        g1, flat = bass.ds(2 * i + u, 1), "a p t -> (a p) t"
                        sp.dma_start(sidx[u][:], src_idx[g1].rearrange(flat)).then_inc(idx_in[u], 16)
                        sp.dma_start(didx[u][:], dst_idx[g1].rearrange(flat)).then_inc(idx_in[u], 16)

                    def load_rbf(i, u):
                        cols = bass.ds(i * CHUNK + u * GROUP, GROUP)
                        sp.dma_start(rbf_rep[u][:], edge_rows[RBF:RBF + 16, cols].unsqueeze(1).broadcast_to([16, 5, GROUP])
                                     ).then_inc(rbf_in[u], 16)
                        sp.dma_start(y_rep[u][:], edge_rows[ONE:ONE + 5, cols].unsqueeze(0).broadcast_to([16, 5, GROUP])
                                     ).then_inc(rbf_in[u], 16)

                    def step(i, u, k):
                        if k == 2:
                            sp.wait_ge(x_in[u], 128 * i + 128)
                            load_idx(i + 1, u)
                            sp.wait_ge(s0["r_ready"], new(i, u))
                            load_rbf(i + 1, u)
                            cols = bass.ds(i * CHUNK + u * GROUP, GROUP)
                            wait_old(sp, s0["prod_sb"], i, u)
                            for n, (row, rows, rep) in enumerate(((Y0, 2, 64), (YX + 1, 2, 64), (Y0, 1, 96), (YX, 3, 32),
                                                                  (YX + 1, 3, 32), (YX + 2, 3, 32))):
                                sp.dma_start(ybc[u][0:rows * rep, n, :],
                                             edge_rows[row:row + rows, cols].unsqueeze(0).broadcast_to([rep, rows, GROUP])
                                             ).then_inc(y_in[u], 16)

                    def node_step(i, n, j):
                        u, turns = n % 2, 2 * i + n // 2
                        if j == 0:
                            wait_old_node(sp, sn["x1_ready"], i, n)
                            sp.dma_start(xn[u][:].rearrange(flat), node_rows(x, i, n)).then_inc(xn_in[u], 16)

                    prime(sp, s0.values())
                    prime(sp, sn.values())
                    sp.sem_inc(primed, 1)
                    for u in range(2):
                        load_idx(0, u)
                        load_rbf(0, u)
                        sp.dma_start(h_sb[u][0:16, 0:D], x[0:16, :]).then_inc(h_out[u], 16)
                        sp.dma_start(outn[u][0:16, 0, :], x[0:16, :]).then_inc(xn_out[u], 16)
                        sp.dma_start(x1n[u][0:16, 0, :], x[0:16, :]).then_inc(x1_out[u], 16)
                    interleaved(sp, ITERS, step, node_step)
                    for u in range(2):
                        sp.wait_ge(idx_in[u], 32 * ITERS + 32)
                        sp.wait_ge(rbf_in[u], 32 * ITERS + 32)
                        sp.wait_ge(xn_out[u], 32 * ITERS + 16)
                        sp.wait_ge(x1_out[u], 32 * ITERS + 16)

                @block.gpsimd
                def _(pool):
                    def gather(i, u, sides=(0, 1)):
                        if 0 in sides:
                            pool.wait_ge(idx_in[u], 32 * i + 32)
                            pool.sem_inc(go, 1)
                        for side in sides:
                            idx = (sidx, didx)[side][u]
                            for t in range(TG):
                                pool.indirect_dma_start(
                                    out=xg[u][:, side * TG + t, :], out_offset=None, in_=x,
                                    in_offset=bass.IndirectOffsetOnAxis(ap=idx[:, t:t + 1], axis=0)).then_inc(x_in[u], 16)

                    def step(i, u, k):
                        if k == 0:
                            pool.wait_ge(s0["q_ready"], new(i, u))
                            pool.tensor_tensor(rstd[u][:], q[u][:], half[:], ALU.pow).then_inc(s0["rstd_ready"], 1)
                        if k == 4:
                            pool.wait_ge(s0["z_ready"], new(i, u))
                            gather(i + 1, u, (0,))
                        if k == 5:
                            gather(i + 1, u, (1,))

                    def node_step(i, n, j):
                        u, turns = n % 2, 2 * i + n // 2
                        if j == 2:
                            pool.wait_ge(sn["x1_q"], new_node(i, n))
                            pool.tensor_tensor(r1[u][:], q1[u][:], half[:, 0:TG], ALU.pow).then_inc(sn["x1_rstd"], 1)
                        if j == 10:
                            pool.wait_ge(sn["u_q"], new_node(i, n))
                            pool.tensor_tensor(r2_[u][:], q2[u][:], half[:, 0:TG], ALU.pow).then_inc(sn["u_rstd"], 1)

                    pool.wait_ge(primed, 1)
                    gather(0, 0)
                    gather(0, 1)
                    interleaved(pool, ITERS, step, node_step)
                    for u in range(2):
                        pool.wait_ge(x_in[u], 128 * ITERS + 128)

                @block.tensor
                def _(pe):
                    def job(i, u, bank, waits, mms, done):
                        for name in waits:
                            pe.wait_ge(s0[name], new(i, u))
                        for n, (w, rhs) in enumerate(mms):
                            last = pe.matmul(E(u, bank)[0:w.shape[1], 0:GROUP], w, rhs, start=(n == 0), stop=(n == len(mms) - 1))
                        last.then_inc(s0[done], 1)

                    def step(i, u, k):
                        if k == 2:
                            pe.wait_ge(s0["z_ready"], new(i, u))
                            for bank, c, n, freed, done in ((0, 0, 128, "h_sb0", "zT_s"), (1, 128, 96, "h_sb1", "zT_vs"),
                                                            (2, 224, 96, "gate_sb", "zT_vd")):
                                wait_old(pe, s0[freed], i, u)
                                pe.sem_inc(go, 1)
                                for t in range(TG):
                                    last = pe.transpose(E(u, bank)[0:n, t * P:(t + 1) * P], z[u][:, t, c:c + n], id_sb[:])
                                last.then_inc(s0[done], 1)
                        if k == 3:
                            job(i, u, 0, ["zs_sb"], [(W("msg_s"), zs[u][:])], "msgs_ps")
                            job(i, u, 1, ["zvs_sb", "zvd_sb"],
                                [(W("msg_v_src"), zvs[u][:]), (W("msg_v_dst"), zvd[u][:])], "msgv_ps")
                            job(i, u, 2, ["r_ready"], [(W("rbf_s"), r80[u][:])], "w_s")
                        if k == 4:
                            job(i, u, 0, ["msgs_sb"], [(W("rbf_vs"), r80[u][:])], "w_vs")
                        if k == 5:
                            job(i, u, 1, ["msgv_sb"], [(W("rbf_vv1_next"), r80[u][:])], "w_next")
                            job(i, u, 2, ["p_s"], [(W("rbf_vv1_prev"), r80[u][:])], "w_prev")
                            job(i, u, 0, ["p_vs"], [(W("rbf_vv0"), r80[u][:])], "w_vv0")
                        if k == 7:
                            job(i, u, 1, ["p_next", "p_vv0"], [(W("val_s"), p_s[u][:]), (W("val_dotv"), p_vv0[u][:])], "vals_ps")
                            job(i, u, 2, ["p_prev"], [(W("alpha_s"), p_s[u][:]), (W("alpha_dotv"), p_vv0[u][:])], "alpha_ps")
                            job(i, u, 0, [], [(W("val_v_sv"), p_s[u][:])], "svy_ps")
                        if k == 8:
                            job(i, u, 1, ["vals_sb", "sig_sb"],
                                [(W("val_v_vs"), p_vs[u][:]), (W("val_v_next"), p_next[u][:]),
                                 (W("val_v_prev"), p_prev[u][:])], "valv_ps")
                            job(i, u, 2, ["leaky_sb"], [(W("gate"), vals[u][:])], "gate_ps")
                            pe.wait_ge(s0["svy_sb"], new(i, u))
                            for t in range(TG):
                                last = pe.matmul(E(u, 0)[:, t * HEADS:(t + 1) * HEADS], leaky[u][:, t * P:(t + 1) * P],
                                                 W("alpha_dot"), start=True, stop=True)
                            last.then_inc(s0["a_ps"], 1)
                        if k == 10:
                            pe.wait_ge(s0["prod_sb"], new(i, u))
                            for t in range(TG):
                                if t == 0:
                                    pe.wait_ge(s0["a_sb"], new(i, u))
                                if t == 3:
                                    pe.wait_ge(s0["valv_sum"], new(i, u))
                                o = E(u, t // 3)[:, (t % 3) * D:(t % 3 + 1) * D]
                                e = slice(t * P, (t + 1) * P)
                                pe.matmul(o[:, 0:96], m_s01[u][:, e], W("out_s01"), start=True, stop=False, skip_group_check=True)
                                pe.matmul(o[:, 96:160], m_s23[u][:, e], W("out_s23"), start=False, stop=False, skip_group_check=True)
                                pe.matmul(o[:, 0:64], m_dot[u][:, e], W("out_dotv"), start=False, stop=False, skip_group_check=True)
                                for m, w in ((m_vs, "out_vs"), (m_next, "out_next"), (m_prev, "out_prev")):
                                    last = pe.matmul(o[:, 64:160], m[u][:, e], W(w), start=False, stop=(w == "out_prev"),
                                                     skip_group_check=True)
                                if t == 2:
                                    last.then_inc(s0["h_ps0"], 1)
                            last.then_inc(s0["h_ps1"], 1)

                    def node_step(i, n, j):
                        u, turns = n % 2, 2 * i + n // 2
                        if j == 6:
                            pe.wait_ge(sn["x1_ready"], new_node(i, n))
                            wait_old_node(pe, sn["gv_ready"], i, n, back=1)
                            for bank, c, width, done in ((6, 0, 64, "T_s"), (7, CS, 96, "T_v")):
                                pe.sem_inc(go, 1)
                                for t in range(TG):
                                    last = pe.transpose(psum[bank][0:width, t * P:(t + 1) * P], x1n[u][:, t, c:c + width], id_sb[:])
                                last.then_inc(sn[done], 1)
                        if j == 7:
                            pe.wait_ge(sn["Ts_sb"], new_node(i, n))
                            pe.wait_ge(sn["Tv_sb"], new_node(i, n))
                            for t in range(TG):
                                o = psum[6 + t // 2][:, (t % 2) * MSG:(t % 2 + 1) * MSG]
                                e = slice(t * P, (t + 1) * P)
                                pe.matmul(o[:, 0:96], Ts[u][:, e], W("self_s"), start=True, stop=False, skip_group_check=True)
                                last = pe.matmul(o[:, 96:192], Tv[u][:, e], W("self_v"), start=False, stop=True, skip_group_check=True)
                            last.then_inc(sn["o_ps"], 1)

                    pe.wait_ge(primed, 1)
                    interleaved(pe, ITERS, step, node_step)

                @block.scalar
                def _(act):
                    def evict(i, u, src, freed, dst, bank, rows, done, func=ACT.Copy, **more):
                        act.wait_ge(s0[src], new(i, u))
                        wait_old(act, s0[freed], i, u)
                        nc.scalar.activation(dst[u][:], E(u, bank)[0:rows, :], func, **more).then_inc(s0[done], 1)

                    def step(i, u, k):
                        if k == 2:
                            evict(i, u, "zT_s", "msgs_ps", zs, 0, 128, "zs_sb")
                            evict(i, u, "zT_vs", "msgv_ps", zvs, 1, 96, "zvs_sb")
                            evict(i, u, "zT_vd", "msgv_ps", zvd, 2, 96, "zvd_sb")
                        if k == 3:
                            evict(i, u, "msgs_ps", "p_s", msgs, 0, 128, "msgs_sb", ACT.Identity, bias=msg_bias[:, 0:1])
                            evict(i, u, "msgv_ps", "p_vv0", msgv, 1, 96, "msgv_sb")
                        if k == 7:
                            evict(i, u, "vals_ps", "gate_ps", vals, 1, 128, "vals_sb")
                            evict(i, u, "vals_ps", "prod_sb", sig, 1, 128, "sig_sb", ACT.Sigmoid)
                            evict(i, u, "alpha_ps", "a_ps", leaky, 2, 64, "fifth_sb", scale=0.2)
                        if k == 8:
                            evict(i, u, "gate_ps", "valv_sb", gate, 2, 96, "gate_sb", ACT.Sigmoid)
                        if k == 10:
                            act.wait_ge(s0["h_ps0"], new(i, u))
                            act.wait_ge(h_out[u], 16 * i + 16)
                            nc.scalar.activation(h_sb[u][:, 0:3 * D], E(u, 0)[:, 0:3 * D], ACT.Copy).then_inc(s0["h_sb0"], 1)
                            act.wait_ge(s0["h_ps1"], new(i, u))
                            nc.scalar.activation(h_sb[u][:, 3 * D:4 * D], E(u, 1)[:, 0:D], ACT.Copy).then_inc(s0["h_sb1"], 1)
                            act.wait_ge(s0["h_sb0"], new(i, u))
                            act.wait_ge(s0["h_sb1"], new(i, u))
                            act.dma_start(h_rows[bass.ds(2 * i + u, 1)].rearrange("a p f -> (a p) f"), h_sb[u][:]).then_inc(h_out[u], 16)

                    def node_step(i, n, j):
                        u, turns = n % 2, 2 * i + n // 2
                        if j == 4:
                            act.wait_ge(sn["x1_shift"], new_node(i, n))
                            act.wait_ge(x1_out[u], 16 * turns + 16)
                            for t in range(TG):
                                last = nc.scalar.activation(x1n[u][:, t, :], xn[u][:, t, :], ACT.Identity,
                                                            scale=r1[u][:, t:t + 1], bias=shift1[u][:, t:t + 1])
                            last.then_inc(sn["x1_ready"], 1)
                        if j == 6:
                            act.wait_ge(sn["x1_ready"], new_node(i, n))
                            act.dma_start(node_rows(x1, i, n), x1n[u][:].rearrange(flat)).then_inc(x1_out[u], 16)
                            act.wait_ge(sn["T_s"], new_node(i, n))
                            wait_old_node(act, sn["o_ps"], i, n)
                            nc.scalar.activation(Ts[u][:], psum[6][0:64, :], ACT.Copy).then_inc(sn["Ts_sb"], 1)
                            act.wait_ge(sn["T_v"], new_node(i, n))
                            nc.scalar.activation(Tv[u][:], psum[7][0:96, :], ACT.Copy).then_inc(sn["Tv_sb"], 1)
                        if j == 8:
                            act.wait_ge(sn["o_ps"], new_node(i, n))
                            wait_old_node(act, sn["u_ready"], i, n)
                            for m in range(2):
                                last = nc.scalar.activation(
                                    gates[u][:, 2 * m:2 * m + 2, :],
                                    psum[6 + m][:, 0:2 * MSG].rearrange("p (t f) -> p t f", t=2)[:, :, 0:96], ACT.Silu)
                            last.then_inc(sn["gates_sb"], 1)
                        if j == 12:
                            act.wait_ge(sn["u_shift"], new_node(i, n))
                            act.wait_ge(xn_out[u], 16 * turns + 16)
                            for t in range(2, TG):
                                last = nc.scalar.activation(outn[u][:, t, :], un[u][:, t, :], ACT.Identity,
                                                            scale=r2_[u][:, t:t + 1], bias=shift2[u][:, t:t + 1])
                            last.then_inc(sn["out_b"], 1)
                            act.wait_ge(sn["out_a"], new_node(i, n))
                            act.wait_ge(sn["out_b"], new_node(i, n))
                            act.dma_start(node_rows(out, i, n), outn[u][:].rearrange(flat)).then_inc(xn_out[u], 16)

                    act.wait_ge(primed, 1)
                    interleaved(act, ITERS, step, node_step)
                    for u in range(2):
                        act.wait_ge(h_out[u], 16 * ITERS + 16)

                @block.vector
                def _(dve):
                    v = nc.vector

                    def product(i, u, msg, msg_ok, rows, bank, wname, dst, done, freed):
                        dve.wait_ge(s0[msg_ok], new(i, u))
                        dve.wait_ge(s0[wname], new(i, u))
                        wait_old(dve, s0[freed], i, u)
                        v.tensor_tensor(dst[u][:], msg[u][:], E(u, bank)[0:rows, :], ALU.mult).then_inc(s0[done], 1)

                    def step(i, u, k):
                        if k == 0:
                            dve.wait_ge(x_in[u], 128 * i + 128)
                            for n in range(2 * TG):
                                v.bn_stats(stats[u][:, n, :], xg[u][:, n, 0:CS])
                                last = v.bn_stats(stats[u][:, 2 * TG + n, :], xg[u][:, n, CS:D])
                            last.then_inc(s0["stats_ready"], 1)
                            dve.wait_ge(s0["stats_ready"], new(i, u))
                            dve.sem_inc(go, 1)
                            for n in range(4 * TG):
                                last = v.bn_aggr(mv[u][:, n, :], stats[u][:, n, :])
                            last.then_inc(s0["mv_ready"], 1)
                            dve.wait_ge(s0["mv_ready"], new(i, u))
                            wait_old(dve, s0["rstd_ready"], i, u)
                            mean_v, var_v = mv[u][:, 2 * TG:, 0], mv[u][:, 2 * TG:, 1]
                            v.tensor_tensor(msq[u][:], mean_v, mean_v, ALU.mult).then_inc(s0["sq_ready"], 1)
                            v.tensor_scalar(q[u][:, 0:2 * TG], mv[u][:, 0:2 * TG, 1], EPS, None, ALU.add)
                            dve.wait_ge(s0["sq_ready"], 4 * i + 2 * u + 2)
                            v.tensor_tensor(msq[u][:], msq[u][:], var_v, ALU.add).then_inc(s0["sq_ready"], 1)
                            dve.wait_ge(s0["sq_ready"], 4 * i + 2 * u + 3)
                            v.tensor_scalar(q[u][:, 2 * TG:], msq[u][:], 3.0, EPS, ALU.mult, ALU.add).then_inc(s0["q_ready"], 1)
                            dve.wait_ge(rbf_in[u], 32 * i + 32)
                            wait_old(dve, s0["w_vv0"], i, u)
                            v.tensor_tensor(r80[u][:], rbf_rep[u][:], y_rep[u][:], ALU.mult).then_inc(s0["r_ready"], 1)
                        if k == 1:
                            dve.wait_ge(s0["rstd_ready"], new(i, u))
                            wait_old(dve, s0["zT_vd"], i, u)
                            for side in range(2):
                                for t in range(TG):
                                    n = side * TG + t
                                    v.tensor_scalar(z[u][:, t, side * CS:(side + 1) * CS], xg[u][:, n, 0:CS],
                                                    mv[u][:, n, 0:1], rstd[u][:, n:n + 1], ALU.subtract, ALU.mult)
                                    n2, c = 2 * TG + n, 2 * CS + side * CV3
                                    last = v.tensor_scalar(z[u][:, t, c:c + CV3], xg[u][:, n, CS:D],
                                                           rstd[u][:, n2:n2 + 1], None, ALU.mult)
                            last.then_inc(s0["z_ready"], 1)
                        if k == 5:
                            product(i, u, msgs, "msgs_sb", 128, 2, "w_s", p_s, "p_s", "svy_ps")
                            product(i, u, msgv, "msgv_sb", 96, 0, "w_vs", p_vs, "p_vs", "valv_ps")
                        if k == 6:
                            product(i, u, msgv, "msgv_sb", 96, 1, "w_next", p_next, "p_next", "valv_ps")
                            product(i, u, msgv, "msgv_sb", 96, 2, "w_prev", p_prev, "p_prev", "valv_ps")
                            product(i, u, msgv, "msgv_sb", 96, 0, "w_vv0", p_vv0, "p_vv0", "alpha_ps")
                        if k == 8:
                            dve.wait_ge(s0["fifth_sb"], new(i, u))
                            v.tensor_tensor(leaky[u][:], leaky[u][:], E(u, 2)[0:64, :], ALU.max).then_inc(s0["leaky_sb"], 1)
                            dve.wait_ge(s0["svy_ps"], new(i, u))
                            dve.wait_ge(y_in[u], 96 * i + 96)
                            wait_old(dve, s0["h_ps1"], i, u)
                            v.tensor_tensor(valv[u][:], ybc[u][0:96, 3, :], E(u, 0)[0:96, :], ALU.mult).then_inc(s0["svy_sb"], 1)
                            dve.wait_ge(s0["sig_sb"], new(i, u))
                            v.tensor_tensor(m_s01[u][:], sig[u][:], ybc[u][:, 0, :], ALU.mult)
                            v.tensor_tensor(m_s23[u][:], sig[u][:], ybc[u][:, 1, :], ALU.mult)
                        if k == 9:
                            dve.wait_ge(s0["svy_sb"], new(i, u))
                            dve.wait_ge(s0["valv_ps"], new(i, u))
                            v.tensor_tensor(valv[u][:], valv[u][:], E(u, 1)[0:96, :], ALU.add).then_inc(s0["valv_sum"], 1)
                            dve.wait_ge(s0["valv_sum"], new(i, u))
                            dve.wait_ge(s0["gate_sb"], new(i, u))
                            v.tensor_tensor(valv[u][:], valv[u][:], gate[u][:], ALU.mult).then_inc(s0["valv_sb"], 1)
                            dve.wait_ge(s0["a_ps"], new(i, u))
                            v.tensor_scalar(a_edge[:, TG * u:TG * (u + 1), :, bass.ds(i, 1)],
                                            E(u, 0)[:, 0:TG * HEADS].rearrange("p (t h o) -> p t h o", h=HEADS, o=1),
                                            1.0, None, ALU.mult).then_inc(s0["a_sb"], 1)
                            dve.wait_ge(s0["valv_sb"], new(i, u))
                            for m, n in ((m_vs, 2), (m_dot, 3), (m_next, 4), (m_prev, 5)):
                                last = v.tensor_tensor(m[u][:], valv[u][:], ybc[u][0:96, n, :], ALU.mult)
                            last.then_inc(s0["prod_sb"], 1)

                    def node_step(i, n, j):
                        u, turns = n % 2, 2 * i + n // 2
                        if j == 2:
                            dve.wait_ge(xn_in[u], 16 * turns + 16)
                            for t in range(TG):
                                last = v.bn_stats(st1[u][:, t, :], xn[u][:, t, :])
                            last.then_inc(sn["x1_bn"], 1)
                            dve.wait_ge(sn["x1_bn"], new_node(i, n))
                            wait_old_node(dve, sn["x1_shift"], i, n)
                            dve.sem_inc(go, 1)
                            for t in range(TG):
                                last = v.bn_aggr(mv1[u][:, t, :], st1[u][:, t, :])
                            last.then_inc(sn["x1_mv"], 1)
                            dve.wait_ge(sn["x1_mv"], new_node(i, n))
                            v.tensor_scalar(q1[u][:], mv1[u][:, :, 1], EPS / 4, None, ALU.add).then_inc(sn["x1_q"], 1)
                        if j == 4:
                            dve.wait_ge(sn["x1_rstd"], new_node(i, n))
                            wait_old_node(dve, sn["x1_ready"], i, n)
                            v.scalar_tensor_tensor(shift1[u][:], mv1[u][:, :, 0], -1.0, r1[u][:], ALU.mult, ALU.mult
                                                   ).then_inc(sn["x1_shift"], 1)
                        if j == 10:
                            dve.wait_ge(sn["gates_sb"], new_node(i, n))
                            dve.wait_ge(sn["o_ps"], new_node(i, n))
                            for m in range(2):
                                b = psum[6 + m]
                                o = b[:, 0:2 * MSG].rearrange("p (t f) -> p t f", t=2)[:, :, 96:192].rearrange("p t (c k) -> p t k c", c=3)
                                g = gates[u][:, 2 * m:2 * m + 2, CS:96].unsqueeze(3).broadcast_to([P, 2, CV, 3])
                                last = v.tensor_tensor(
                                    gv[u][:, 2 * m:2 * m + 2, :].rearrange("p t (k c) -> p t k c", c=3), g, o, ALU.mult)
                            last.then_inc(sn["gv_ready"], 1)
                            wait_old_node(dve, sn["out_b"], i, n)
                            v.scalar_tensor_tensor(un[u][:, :, 0:CS], x1n[u][:, :, 0:CS], 2.0, gates[u][:, :, 0:CS],
                                                   ALU.mult, ALU.add)
                            dve.wait_ge(sn["gv_ready"], new_node(i, n))
                            v.scalar_tensor_tensor(un[u][:, :, CS:D], x1n[u][:, :, CS:D], 2.0, gv[u][:],
                                                   ALU.mult, ALU.add).then_inc(sn["u_ready"], 1)
                            dve.wait_ge(sn["u_ready"], new_node(i, n))
                            for t in range(TG):
                                last = v.bn_stats(st2[u][:, t, :], un[u][:, t, :])
                            last.then_inc(sn["u_bn"], 1)
                            dve.wait_ge(sn["u_bn"], new_node(i, n))
                            dve.sem_inc(go, 1)
                            for t in range(TG):
                                last = v.bn_aggr(mv2[u][:, t, :], st2[u][:, t, :])
                            last.then_inc(sn["u_mv"], 1)
                            dve.wait_ge(sn["u_mv"], new_node(i, n))
                            v.tensor_scalar(q2[u][:], mv2[u][:, :, 1], EPS, None, ALU.add).then_inc(sn["u_q"], 1)
                        if j == 12:
                            dve.wait_ge(sn["u_rstd"], new_node(i, n))
                            v.scalar_tensor_tensor(shift2[u][:], mv2[u][:, :, 0], -1.0, r2_[u][:], ALU.mult, ALU.mult
                                                   ).then_inc(sn["u_shift"], 1)
                            dve.wait_ge(xn_out[u], 16 * turns + 16)
                            for t in range(2):
                                last = v.tensor_scalar(outn[u][:, t, :], un[u][:, t, :], mv2[u][:, t, 0:1],
                                                       r2_[u][:, t:t + 1], ALU.subtract, ALU.mult)
                            last.then_inc(sn["out_a"], 1)

                    dve.wait_ge(primed, 1)
                    interleaved(dve, ITERS, step, node_step)

        with ExitStack() as ctx:
            sem = sem_in(ctx)
            m_in, m_t, m_ev, m_dve, m_act = sem("m_in"), sem("m_t"), sem("m_ev"), sem("m_dve"), sem("m_act")
            with nc.Block() as block:
                sb = sb_in(ctx)
                a_seg = sb("a_seg", [SEG, CHUNK])
                dq_i = sb("dq_i", [SEG, CHUNK], I32)
                dq = sb("dq", [SEG, CHUNK])
                step = sb("step", [SEG, CHUNK + 1])
                run = sb("run", [SEG, CHUNK])
                top_ = sb("top_", [SEG, CHUNK])
                other = sb("other", [SEG, CHUNK])
                ends = sb("ends", [1, 4, SEG])
                hm = sb("hm", [1, SEG])
                cont, whole, f_in, g_in = sb("cont", [1, SEG]), sb("whole", [1, SEG]), sb("f_in", [1, SEG]), sb("g_in", [1, SEG])
                carry = sb("carry", [1, 2, SEG])
                carry_col = sb("carry_col", [SEG, 2])

                @block.sync
                def _(sp):
                    for h in range(HEADS):
                        sp.dma_start(dq_i[h * ITERS:(h + 1) * ITERS, :], dst_line).then_inc(m_in, 16)
                    sp.dma_start(hm[:], head_mask).then_inc(m_in, 16)

                @block.tensor
                def _(pe):
                    for b in range(2 * TG):
                        last = pe.transpose(psum[b // 4][0:SEG, (b % 4) * P:(b % 4 + 1) * P],
                                            a_edge[:, b].rearrange("p h q -> p (h q)"), id_sb[:])
                    last.then_inc(m_t, 1)
                    pe.wait_ge(m_dve, 1)
                    for k, c in enumerate((run[:, CHUNK - 1:CHUNK], top_[:, 0:1], dq[:, 0:1], dq[:, CHUNK - 1:CHUNK])):
                        last = pe.transpose(psum[2][0:1, k * P:k * P + SEG], c, id_sb[0:SEG, 0:SEG])
                    last.then_inc(m_t, 1)
                    pe.wait_ge(m_dve, 2)
                    for k in range(2):
                        last = pe.transpose(psum[3][0:SEG, k:k + 1], carry[:, k, :], id_sb[0:1, 0:1])
                    last.then_inc(m_t, 1)
                    pe.wait_ge(m_act, 3)
                    for b in range(2 * TG):
                        last = pe.transpose(psum[4 + b // 4][:, (b % 4) * P:(b % 4) * P + SEG], a_seg[:, b * P:(b + 1) * P],
                                            id_sb[0:SEG, 0:SEG])
                    last.then_inc(m_t, 1)

                @block.scalar
                def _(act):
                    act.wait_ge(m_t, 1)
                    for k in range(2):
                        nc.scalar.activation(a_seg[:, k * 512:(k + 1) * 512], psum[k][0:SEG, :], ACT.Copy).then_inc(m_act, 1)
                    act.wait_ge(m_dve, 3)
                    nc.scalar.activation(a_seg[:], other[:], ACT.Exp).then_inc(m_act, 1)
                    act.wait_ge(m_t, 4)
                    for b in range(2 * TG):
                        nc.scalar.activation(ex_edge[:, b].rearrange("p h q -> p (h q)"),
                                             psum[4 + b // 4][:, (b % 4) * P:(b % 4) * P + SEG], ACT.Copy)

                @block.vector
                def _(dve):
                    n = [0]

                    def then(ins):
                        ins.then_inc(m_ev, 1)
                        n[0] += 1
                        dve.wait_ge(m_ev, n[0])

                    v = nc.vector
                    dve.wait_ge(m_in, 16 * (HEADS + 1))
                    v.memset(step[:], -BIG)
                    then(v.tensor_copy(dq[:], dq_i[:]))
                    then(v.tensor_tensor(step[:, 1:CHUNK], dq[:, 1:CHUNK], dq[:, 0:CHUNK - 1], ALU.is_equal))
                    then(v.tensor_scalar(step[:, 1:CHUNK], step[:, 1:CHUNK], 1.0, BIG, ALU.subtract, ALU.mult))
                    dve.wait_ge(m_act, 2)
                    then(v.tensor_tensor_scan(run[:], step[:, 0:CHUNK], a_seg[:], -BIG, ALU.add, ALU.max))
                    v.tensor_tensor_scan(top_[:, ::-1], step[:, 1:CHUNK + 1][:, ::-1], run[:, ::-1], -BIG, ALU.add,
                                         ALU.max).then_inc(m_dve, 1)
                    dve.wait_ge(m_t, 2)
                    then(v.tensor_copy(ends[:], psum[2][0:1, :].rearrange("p (k s) -> p k s", k=4)[:, :, 0:SEG]))
                    last_max, first_max, first, last = (ends[:, k, :] for k in range(4))
                    v.memset(cont[:], -BIG)
                    then(v.tensor_tensor(whole[:], first, last, ALU.is_equal))
                    then(v.tensor_tensor(cont[:, 1:], first[:, 1:], last[:, 0:SEG - 1], ALU.is_equal))
                    v.tensor_scalar(whole[:], whole[:], 1.0, BIG, ALU.subtract, ALU.mult)
                    then(v.tensor_scalar(cont[:, 1:], cont[:, 1:], 1.0, BIG, ALU.subtract, ALU.mult))
                    then(v.tensor_tensor(cont[:], cont[:], hm[:], ALU.add))
                    v.memset(carry[:], -BIG)
                    v.tensor_tensor(f_in[:, 1:], whole[:, 0:SEG - 1], cont[:, 1:], ALU.add)
                    then(v.tensor_tensor(g_in[:, 1:], last_max[:, 0:SEG - 1], cont[:, 1:], ALU.add))
                    then(v.tensor_tensor_scan(carry[:, 0, 1:], f_in[:, 1:], g_in[:, 1:], -BIG, ALU.add, ALU.max))
                    v.tensor_tensor(f_in[:, 0:SEG - 1], whole[:, 1:], cont[:, 1:], ALU.add)
                    then(v.tensor_tensor(g_in[:, 0:SEG - 1], first_max[:, 1:], cont[:, 1:], ALU.add))
                    v.tensor_tensor_scan(carry[:, 1, 0:SEG - 1][:, ::-1], f_in[:, 0:SEG - 1][:, ::-1],
                                         g_in[:, 0:SEG - 1][:, ::-1], -BIG, ALU.add, ALU.max).then_inc(m_dve, 1)
                    dve.wait_ge(m_t, 3)
                    then(v.tensor_copy(carry_col[:], psum[3][0:SEG, 0:2]))
                    for k, c in enumerate((0, CHUNK - 1)):
                        then(v.tensor_scalar(other[:], dq[:], dq[:, c:c + 1], 1.0, ALU.is_equal, ALU.subtract))
                        then(v.tensor_scalar(other[:], other[:], BIG, carry_col[:, k:k + 1], ALU.mult, ALU.add))
                        then(v.tensor_tensor(top_[:], top_[:], other[:], ALU.max))
                    v.tensor_tensor(other[:], a_seg[:], top_[:], ALU.subtract).then_inc(m_dve, 1)

        with ExitStack() as ctx:
            sem = sem_in(ctx)
            stages = ["e_ex", "e_sb", "sel_sb", "agg_ps", "agg_sb", "den_sb", "rden_sb", "nrm_sb", "T_s", "T_v", "Ts_sb",
                      "Tv_sb", "p_ps", "u_ready", "bn", "mv", "q", "rstd", "x1_ready", "idx_ready", "prime"]
            s3 = {n: sem("a0_" + n) for n in stages}
            ld3, gi3, st3 = ([sem(f"a0_{n}{u}") for u in range(2)] for n in ("ld", "gi", "st"))
            xd3, sc3 = ([top_sem(f"a0_{n}{u}") for u in range(2)] for n in ("xd", "sc"))
            primed_3 = sem("primed_3")

            with nc.Block() as block:
                sb = sb_in(ctx)
                two = lambda name, shape, dt=F32: [sb(f"{name}{u}", shape, dt) for u in range(2)]
                hh = two("hh", [P, TG, D])
                exg = two("exg", [P, TG, HEADS])
                e = two("e", [P, TG, AGG])
                xd = two("xd", [P, TG, D])
                didx = two("didx3", [P, TG], I32)
                dcol_i, dcol = two("dcol_i", [P, TG + 1], I32), two("dcol", [P, TG + 1])
                dnext = two("dnext", [P, TG], I32)
                dline = two("dline", [P, GROUP], I32)
                tidx_f, tidx = two("tidx_f", [P, TG]), two("tidx", [P, TG], I32)
                sel, sel_c = two("sel", [P, TG, P]), two("sel_c", [P, TG, P])
                agg = two("agg", [P, TG, AGG])
                den, rden = two("den", [P, TG, HEADS]), two("rden", [P, TG, HEADS])
                nrm = two("nrm", [P, TG, D])
                Ts, Tv = two("Ts3", [64, GROUP]), two("Tv3", [96, GROUP])
                uu, x1d = two("uu", [P, TG, D]), two("x1d", [P, TG, D])
                st, mv = two("st", [P, TG, 6]), two("mv3", [P, TG, 2])
                q, r = two("q3", [P, TG]), two("r3", [P, TG])
                flat, group = "p t d -> p (t d)", "a p t -> (a p) t"

                @block.sync
                def _(sp):
                    def load_idx(i, u):
                        sp.dma_start(didx[u][:], dst_idx[bass.ds(2 * i + u, 1)].rearrange(group)).then_inc(gi3[u], 16)

                    def step(i, u, k):
                        if k == 0:
                            g1 = bass.ds(2 * i + u, 1)
                            wait_old(sp, s3["e_sb"], i, u)
                            wait_old(sp, s3["sel_sb"], i, u)
                            sp.dma_start(hh[u][:].rearrange(flat), h_rows[g1].rearrange(group)).then_inc(ld3[u], 16)
                            sp.dma_start(dcol_i[u][:], dst_cols[g1].rearrange(group)).then_inc(ld3[u], 16)
                            sp.dma_start(dnext[u][:], dst_next[g1].rearrange(group)).then_inc(ld3[u], 16)
                            sp.dma_start(dline[u][:], dst_line[bass.ds(i, 1), u * GROUP:(u + 1) * GROUP].broadcast_to([P, GROUP])
                                         ).then_inc(ld3[u], 16)
                        if k == 2:
                            sp.wait_ge(xd3[u], 64 * i + 64)
                            load_idx(i + 1, u)
                        if k == 14:
                            sp.wait_ge(s3["x1_ready"], new(i, u))
                            sp.dma_start(x1_dst[bass.ds(2 * i + u, 1)].rearrange(group), x1d[u][:].rearrange(flat)
                                         ).then_inc(st3[u], 16)

                    prime(sp, s3.values())
                    sp.sem_inc(primed_3, 1)
                    for u in range(2):
                        load_idx(0, u)
                        sp.dma_start(x1d[u][0:16, 0, :], x[0:16, :]).then_inc(st3[u], 16)
                    staggered(sp, ITERS, 11, 15, step)
                    for u in range(2):
                        sp.wait_ge(st3[u], 16 * ITERS + 16)
                        sp.wait_ge(gi3[u], 16 * ITERS + 16)

                @block.gpsimd
                def _(pool):
                    def gather(i, u):
                        pool.wait_ge(gi3[u], 16 * i + 16)
                        pool.sem_inc(go, 1)
                        for t in range(TG):
                            pool.indirect_dma_start(out=xd[u][:, t, :], out_offset=None, in_=x,
                                                    in_offset=bass.IndirectOffsetOnAxis(ap=didx[u][:, t:t + 1], axis=0)
                                                    ).then_inc(xd3[u], 16)

                    def step(i, u, k):
                        if k == 10:
                            pool.wait_ge(s3["q"], new(i, u))
                            pool.tensor_tensor(r[u][:], q[u][:], half[:, 0:TG], ALU.pow).then_inc(s3["rstd"], 1)
                        if k == 12:
                            gather(i + 1, u)
                        if k == 14:
                            pool.wait_ge(s3["idx_ready"], new(i, u))
                            pool.wait_ge(s3["x1_ready"], new(i, u))
                            pool.sem_inc(go, 1)
                            for t in range(TG):
                                pool.indirect_dma_start(out=x1, in_=x1d[u][:, t, :], in_offset=None,
                                                        out_offset=bass.IndirectOffsetOnAxis(ap=tidx[u][:, t:t + 1], axis=0),
                                                        bounds_check=NP - 1, oob_is_err=False).then_inc(sc3[u], 16)

                    pool.wait_ge(primed_3, 1)
                    for u in range(2):
                        pool.dma_start(x1d[u][0:16, 1, :], x[0:16, :]).then_inc(sc3[u], 16)
                        gather(0, u)
                    staggered(pool, ITERS, 11, 15, step)
                    for u in range(2):
                        pool.wait_ge(sc3[u], 64 * ITERS + 16)
                        pool.wait_ge(xd3[u], 64 * ITERS + 64)

                @block.tensor
                def _(pe):
                    def step(i, u, k):
                        if 3 <= k < 3 + TG:
                            t = k - 3
                            n = 8 * i + 4 * u + t
                            o = psum[4 * u + t % 2][:, 0:AGG]
                            prev = agg[u][:, t - 1, :] if t else agg[1 - u][:, TG - 1, :]
                            if t == 0:
                                pe.wait_ge(s3["e_sb"], new(i, u))
                                pe.wait_ge(s3["sel_sb"], new(i, u))
                                wait_old(pe, s3["nrm_sb"], i, u)
                            if t >= 2:
                                pe.wait_ge(s3["agg_sb"], n)
                            pe.matmul(o, sel[u][:, t, :], e[u][:, t, :], start=True, stop=False)
                            pe.wait_ge(s3["agg_sb"], n + 1)
                            pe.matmul(o, sel_c[u][:, t, :], prev, start=False, stop=True).then_inc(s3["agg_ps"], 1)
                        if k == 8:
                            pe.wait_ge(s3["nrm_sb"], new(i, u))
                            wait_old(pe, s3["u_ready"], i, u)
                            for bank, c, n, done in ((2, 0, 64, "T_s"), (3, CS, 96, "T_v")):
                                pe.sem_inc(go, 1)
                                for t in range(TG):
                                    last = pe.transpose(psum[4 * u + bank][0:n, t * P:(t + 1) * P], nrm[u][:, t, c:c + n], id_sb[:])
                                last.then_inc(s3[done], 1)
                        if k == 9:
                            pe.wait_ge(s3["Ts_sb"], new(i, u))
                            pe.wait_ge(s3["Tv_sb"], new(i, u))
                            for t in range(TG):
                                o = psum[4 * u + 2 + t // 2][:, (t % 2) * D:(t % 2 + 1) * D]
                                ee = slice(t * P, (t + 1) * P)
                                pe.matmul(o[:, 0:CS], Ts[u][:, ee], W("proj_s"), start=True, stop=False, skip_group_check=True)
                                last = pe.matmul(o[:, CS:D], Tv[u][:, ee], W("proj_v"), start=False, stop=True, skip_group_check=True)
                            last.then_inc(s3["p_ps"], 1)

                    pe.wait_ge(primed_3, 1)
                    staggered(pe, ITERS, 11, 15, step)

                @block.scalar
                def _(act):
                    def step(i, u, k):
                        if 3 <= k < 3 + TG:
                            t = k - 3
                            act.wait_ge(s3["agg_ps"], 8 * i + 4 * u + t + 2)
                            nc.scalar.activation(agg[u][:, t, :], psum[4 * u + t % 2][:, 0:AGG], ACT.Copy).then_inc(s3["agg_sb"], 1)
                        if k == 8:
                            act.wait_ge(s3["T_s"], new(i, u))
                            wait_old(act, s3["p_ps"], i, u)
                            nc.scalar.activation(Ts[u][:], psum[4 * u + 2][0:64, :], ACT.Copy).then_inc(s3["Ts_sb"], 1)
                            act.wait_ge(s3["T_v"], new(i, u))
                            nc.scalar.activation(Tv[u][:], psum[4 * u + 3][0:96, :], ACT.Copy).then_inc(s3["Tv_sb"], 1)

                    act.wait_ge(primed_3, 1)
                    staggered(act, ITERS, 11, 15, step)

                @block.vector
                def _(dve):
                    v = nc.vector

                    def by_head(dst, src, factor):
                        for c0, c1, a in ((0, CS, 16), *((CS + c * CV, CS + (c + 1) * CV, 8) for c in range(3))):
                            last = v.tensor_tensor(dst[:, :, c0:c1].rearrange("p t (h a) -> p t h a", h=HEADS),
                                                   src[:, :, c0:c1].rearrange("p t (h a) -> p t h a", h=HEADS),
                                                   factor[:].unsqueeze(3).broadcast_to([P, TG, HEADS, a]), ALU.mult)
                        return last

                    def step(i, u, k):
                        if k == 3:
                            dve.wait_ge(ld3[u], 64 * i + 64)
                            wait_old_sums(dve, s3["agg_ps"], i, u)
                            wait_old(dve, s3["idx_ready"], i, u)
                            v.tensor_copy(dcol[u][:], dcol_i[u][:])
                            v.tensor_tensor(tidx_f[u][:], dcol_i[u][:, 1:], dnext[u][:], ALU.is_equal)
                            v.tensor_scalar(exg[u][:], ex_edge[:, TG * u:TG * (u + 1), :, bass.ds(i, 1)].rearrange("p t h o -> p t (h o)"),
                                            1.0, None, ALU.mult).then_inc(s3["e_ex"], 1)
                            dve.wait_ge(s3["e_ex"], new(i, u))
                            by_head(e[u], hh[u], exg[u])
                            v.tensor_copy(e[u][:, :, D:AGG], exg[u][:]).then_inc(s3["e_sb"], 1)
                            for t in range(TG):
                                line = dline[u][:, t * P:(t + 1) * P]
                                v.tensor_scalar(sel[u][:, t, :], line, dcol[u][:, t + 1:t + 2], None, ALU.is_equal)
                                last = v.tensor_scalar(sel_c[u][:, t, :], line, dcol[u][:, t:t + 1], V("last_row", P),
                                                       ALU.is_equal, ALU.mult)
                            last.then_inc(s3["sel_sb"], 1)
                        if k == 7:
                            dve.wait_ge(s3["agg_sb"], 8 * i + 4 * u + 5)
                            v.tensor_scalar(den[u][:], agg[u][:, :, D:AGG], 1e-16, None, ALU.add).then_inc(s3["den_sb"], 1)
                            dve.wait_ge(s3["den_sb"], new(i, u))
                            v.reciprocal(rden[u][:], den[u][:]).then_inc(s3["rden_sb"], 1)
                            dve.wait_ge(s3["rden_sb"], new(i, u))
                            wait_old(dve, s3["T_v"], i, u)
                            by_head(nrm[u], agg[u], rden[u]).then_inc(s3["nrm_sb"], 1)
                        if k == 10:
                            dve.wait_ge(s3["p_ps"], new(i, u))
                            dve.wait_ge(xd3[u], 64 * i + 64)
                            for n in range(2):
                                last = v.scalar_tensor_tensor(
                                    uu[u][:, 2 * n:2 * n + 2, :], xd[u][:, 2 * n:2 * n + 2, :], 2.0,
                                    psum[4 * u + 2 + n][:, 0:2 * D].rearrange("p (t d) -> p t d", t=2), ALU.mult, ALU.add)
                            last.then_inc(s3["u_ready"], 1)
                            dve.wait_ge(s3["u_ready"], new(i, u))
                            for t in range(TG):
                                last = v.bn_stats(st[u][:, t, :], uu[u][:, t, :])
                            last.then_inc(s3["bn"], 1)
                            dve.wait_ge(s3["bn"], new(i, u))
                            dve.sem_inc(go, 1)
                            for t in range(TG):
                                last = v.bn_aggr(mv[u][:, t, :], st[u][:, t, :])
                            last.then_inc(s3["mv"], 1)
                            dve.wait_ge(s3["mv"], new(i, u))
                            v.tensor_scalar(q[u][:], mv[u][:, :, 1], EPS, None, ALU.add).then_inc(s3["q"], 1)
                        if k == 13:
                            dve.wait_ge(sc3[u], 64 * i + 16)
                            v.scalar_tensor_tensor(tidx[u][:], tidx_f[u][:], float(SKIP), dcol[u][:, 1:], ALU.mult, ALU.add
                                                   ).then_inc(s3["idx_ready"], 1)
                            dve.wait_ge(st3[u], 16 * i + 16)
                            dve.wait_ge(s3["rstd"], new(i, u))
                            for t in range(TG):
                                last = v.tensor_scalar(x1d[u][:, t, :], uu[u][:, t, :], mv[u][:, t, 0:1], r[u][:, t:t + 1],
                                                       ALU.subtract, ALU.mult)
                            last.then_inc(s3["x1_ready"], 1)

                    v.memset(agg[1][:], 0.0).then_inc(s3["prime"], 1)
                    dve.wait_ge(s3["prime"], 2)
                    dve.wait_ge(primed_3, 1)
                    staggered(dve, ITERS, 11, 15, step)

        with ExitStack() as ctx:
            sem = sem_in(ctx)
            stages = ["T_s", "T_v", "Ts_sb", "Tv_sb", "xs_ps", "xv_ps", "hid_ps", "hid_sb", "w_s01", "w_s23", "w_vs",
                      "w_vv", "q_s01", "q_s23", "q_vs", "q_vv", "m_s01", "m_s23", "m_vs", "m_vv", "msg_ps0", "msg_ps1",
                      "msg_sb0", "msg_sb1", "dcol_sb", "sel_sb", "idx_ready", "agg_ps", "agg_sb", "N_s", "N_v", "Ns_sb",
                      "Nv_sb", "self_ps", "o_sb", "gates_sb", "gv_ready", "u_ready", "bn", "mv", "q", "rstd", "out_ready",
                      "prime"]
            s4 = {n: sem("e1_" + n) for n in stages}
            ix4, y4, em4, ld4, xd4 = ([sem(f"e1_{n}{u}") for u in range(2)] for n in ("ix", "y", "em", "ld", "xd"))
            xg4, sc4 = ([top_sem(f"e1_{n}{u}") for u in range(2)] for n in ("xg", "sc"))
            primed_4 = sem("primed_4")

            with nc.Block() as block:
                sb = sb_in(ctx)
                two = lambda name, shape, dt=F32: [sb(f"{name}{u}", shape, dt) for u in range(2)]
                sidx = two("sidx4", [P, TG], I32)
                xg = two("xg4", [P, TG, D])
                ybc = two("ybc4", [P, 4, GROUP])
                emb = two("emb", [8, GROUP])
                Ts, Tv, hid = two("Ts4", [64, GROUP]), two("Tv4", [96, GROUP]), two("hid", [64, GROUP])
                m_s01, m_s23, m_vs, m_vv = (two("n_" + n, [128 if n[0] == "s" else 96, GROUP]) for n in ("s01", "s23", "vs", "vv"))
                msg = two("msg", [P, TG, MSG])
                dcol_i, dcol = two("dcol_i4", [P, TG + 1], I32), two("dcol4", [P, TG + 1])
                dnext = two("dnext4", [P, TG], I32)
                dline = two("dline4", [P, GROUP], I32)
                tidx_f, tidx = two("tidx_f4", [P, TG]), two("tidx4", [P, TG], I32)
                sel, sel_c = two("sel4", [P, TG, P]), two("sel_c4", [P, TG, P])
                agg = two("agg4", [P, TG, MSG])
                x1d = two("x1d4", [P, TG, D])
                Ns, Nv = two("Ns", [64, GROUP]), two("Nv", [96, GROUP])
                o_sb = two("o_sb", [P, TG, MSG])
                gates, gv = two("gates4", [P, TG, 96]), two("gv4", [P, TG, CV3])
                uu, od = two("uu4", [P, TG, D]), two("od", [P, TG, D])
                st, mv = two("st4", [P, TG, 6]), two("mv4", [P, TG, 2])
                q, r = two("q4", [P, TG]), two("r4", [P, TG])
                flat, group = "p t d -> p (t d)", "a p t -> (a p) t"

                @block.sync
                def _(sp):
                    def load_idx(i, u):
                        sp.dma_start(sidx[u][:], src_idx[bass.ds(2 * i + u, 1)].rearrange(group)).then_inc(ix4[u], 16)

                    def step(i, u, k):
                        g1 = bass.ds(2 * i + u, 1)
                        cols = bass.ds(i * CHUNK + u * GROUP, GROUP)
                        if k == 0:
                            wait_old(sp, s4["hid_ps"], i, u)
                            sp.dma_start(emb[u][:], edge_rows[EMB:EMB + 8, cols]).then_inc(em4[u], 16)
                            wait_old(sp, s4["q_vv"], i, u)
                            for n, (row, rows, rep) in enumerate(((Y0, 2, 64), (YX + 1, 2, 64), (Y0, 1, 96), (YX, 3, 32))):
                                sp.dma_start(ybc[u][0:rows * rep, n, :],
                                             edge_rows[row:row + rows, cols].unsqueeze(0).broadcast_to([rep, rows, GROUP])
                                             ).then_inc(y4[u], 16)
                            wait_old(sp, s4["sel_sb"], i, u)
                            sp.dma_start(dcol_i[u][:], dst_cols[g1].rearrange(group)).then_inc(ld4[u], 16)
                            sp.dma_start(dnext[u][:], dst_next[g1].rearrange(group)).then_inc(ld4[u], 16)
                            sp.dma_start(dline[u][:], dst_line[bass.ds(i, 1), u * GROUP:(u + 1) * GROUP].broadcast_to([P, GROUP])
                                         ).then_inc(ld4[u], 16)
                        if k == 3:
                            wait_old(sp, s4["u_ready"], i, u)
                            sp.dma_start(x1d[u][:].rearrange(flat), x1_dst[g1].rearrange(group)).then_inc(xd4[u], 16)
                        if k == 2:
                            sp.wait_ge(xg4[u], 64 * i + 64)
                            load_idx(i + 1, u)

                    prime(sp, s4.values())
                    sp.sem_inc(primed_4, 1)
                    load_idx(0, 0)
                    load_idx(0, 1)
                    staggered(sp, ITERS, 11, 16, step)
                    for u in range(2):
                        sp.wait_ge(ix4[u], 16 * ITERS + 16)

                @block.gpsimd
                def _(pool):
                    def gather(i, u):
                        pool.wait_ge(ix4[u], 16 * i + 16)
                        pool.sem_inc(go, 1)
                        for t in range(TG):
                            pool.indirect_dma_start(out=xg[u][:, t, :], out_offset=None, in_=x1,
                                                    in_offset=bass.IndirectOffsetOnAxis(ap=sidx[u][:, t:t + 1], axis=0)
                                                    ).then_inc(xg4[u], 16)

                    def step(i, u, k):
                        if k == 2:
                            pool.wait_ge(s4["T_v"], new(i, u))
                            gather(i + 1, u)
                        if k == 13:
                            pool.wait_ge(s4["q"], new(i, u))
                            pool.tensor_tensor(r[u][:], q[u][:], half[:, 0:TG], ALU.pow).then_inc(s4["rstd"], 1)
                        if k == 15:
                            pool.wait_ge(s4["idx_ready"], new(i, u))
                            pool.wait_ge(s4["out_ready"], new(i, u))
                            pool.sem_inc(go, 1)
                            for t in range(TG):
                                pool.indirect_dma_start(out=out, in_=od[u][:, t, :], in_offset=None,
                                                        out_offset=bass.IndirectOffsetOnAxis(ap=tidx[u][:, t:t + 1], axis=0),
                                                        bounds_check=NP - 1, oob_is_err=False).then_inc(sc4[u], 16)

                    pool.wait_ge(primed_4, 1)
                    for u in range(2):
                        pool.dma_start(od[u][0:16, 0, :], x[0:16, :]).then_inc(sc4[u], 16)
                        gather(0, u)
                    staggered(pool, ITERS, 11, 16, step)
                    for u in range(2):
                        pool.wait_ge(sc4[u], 64 * ITERS + 16)
                        pool.wait_ge(xg4[u], 64 * ITERS + 64)

                @block.tensor
                def _(pe):
                    def job(i, u, bank, waits, w, rhs, done):
                        for name in waits:
                            pe.wait_ge(s4[name], new(i, u))
                        pe.matmul(B(u, bank)[0:w.shape[1], 0:GROUP], w, rhs, start=True, stop=True).then_inc(s4[done], 1)

                    def step(i, u, k):
                        if k == 1:
                            pe.wait_ge(xg4[u], 64 * i + 64)
                            wait_old(pe, s4["o_sb"], i, u)
                            for bank, c, n, done in ((0, 0, 64, "T_s"), (1, CS, 96, "T_v")):
                                pe.sem_inc(go, 1)
                                for t in range(TG):
                                    last = pe.transpose(B(u, bank)[0:n, t * P:(t + 1) * P], xg[u][:, t, c:c + n], id_sb[:])
                                last.then_inc(s4[done], 1)
                            pe.wait_ge(em4[u], 16 * i + 16)
                            job(i, u, 2, [], W("fc1"), emb[u][:], "hid_ps")
                        if k == 2:
                            job(i, u, 3, ["Ts_sb"], W("l1_xs"), Ts[u][:], "xs_ps")
                            job(i, u, 0, ["Tv_sb"], W("l1_xv"), Tv[u][:], "xv_ps")
                            job(i, u, 1, ["hid_sb"], W("fc2_s01"), hid[u][:], "w_s01")
                            job(i, u, 2, [], W("fc2_s23"), hid[u][:], "w_s23")
                        if k == 4:
                            job(i, u, 3, ["q_s23"], W("fc2_vs"), hid[u][:], "w_vs")
                            job(i, u, 0, ["q_vv"], W("fc2_vv"), hid[u][:], "w_vv")
                        if k == 5:
                            for name in ("m_s01", "m_s23", "m_vs", "m_vv"):
                                pe.wait_ge(s4[name], new(i, u))
                            for t in range(TG):
                                o = B(u, 1 + t // 2)[:, (t % 2) * MSG:(t % 2 + 1) * MSG]
                                ee = slice(t * P, (t + 1) * P)
                                pe.matmul(o[:, 0:128], m_s01[u][:, ee], W("l1_s01"), start=True, stop=False, skip_group_check=True)
                                pe.matmul(o[:, 128:192], m_s23[u][:, ee], W("l1_s23"), start=False, stop=False, skip_group_check=True)
                                pe.matmul(o[:, 96:192], m_vs[u][:, ee], W("l1_vs"), start=False, stop=False, skip_group_check=True)
                                last = pe.matmul(o[:, 0:96], m_vv[u][:, ee], W("l1_vv"), start=False, stop=True, skip_group_check=True)
                                if t == 1:
                                    last.then_inc(s4["msg_ps0"], 1)
                            last.then_inc(s4["msg_ps1"], 1)
                        if k == 6:
                            pe.wait_ge(xd4[u], 16 * i + 16)
                            for bank, c, n, done in ((3, 0, 64, "N_s"), (0, CS, 96, "N_v")):
                                pe.sem_inc(go, 1)
                                for t in range(TG):
                                    last = pe.transpose(B(u, bank)[0:n, t * P:(t + 1) * P], x1d[u][:, t, c:c + n], id_sb[:])
                                last.then_inc(s4[done], 1)
                        if 7 <= k < 7 + TG:
                            t = k - 7
                            o = B(u, 1 + t % 2)[:, 0:MSG]
                            n = 8 * i + 4 * u + t
                            prev = agg[u][:, t - 1, :] if t else agg[1 - u][:, TG - 1, :]
                            if t == 0:
                                pe.wait_ge(s4["msg_sb0"], new(i, u))
                                pe.wait_ge(s4["msg_sb1"], new(i, u))
                                pe.wait_ge(s4["sel_sb"], new(i, u))
                            if t >= 2:
                                pe.wait_ge(s4["agg_sb"], n)
                            pe.matmul(o, sel[u][:, t, :], msg[u][:, t, :], start=True, stop=False)
                            pe.wait_ge(s4["agg_sb"], n + 1)
                            pe.matmul(o, sel_c[u][:, t, :], prev, start=False, stop=True).then_inc(s4["agg_ps"], 1)
                        if k == 8:
                            pe.wait_ge(s4["Ns_sb"], new(i, u))
                            pe.wait_ge(s4["Nv_sb"], new(i, u))
                            for t in range(TG):
                                o = B(u, 3 if t < 2 else 0)[:, (t % 2) * MSG:(t % 2 + 1) * MSG]
                                ee = slice(t * P, (t + 1) * P)
                                pe.matmul(o[:, 0:96], Ns[u][:, ee], W("self_s"), start=True, stop=False, skip_group_check=True)
                                last = pe.matmul(o[:, 96:192], Nv[u][:, ee], W("self_v"), start=False, stop=True, skip_group_check=True)
                            last.then_inc(s4["self_ps"], 1)

                    pe.wait_ge(primed_4, 1)
                    staggered(pe, ITERS, 11, 16, step)

                @block.scalar
                def _(act):
                    def step(i, u, k):
                        if k == 1:
                            act.wait_ge(s4["T_s"], new(i, u))
                            wait_old(act, s4["xv_ps"], i, u)
                            nc.scalar.activation(Ts[u][:], B(u, 0)[0:64, :], ACT.Copy).then_inc(s4["Ts_sb"], 1)
                            act.wait_ge(s4["T_v"], new(i, u))
                            nc.scalar.activation(Tv[u][:], B(u, 1)[0:96, :], ACT.Copy).then_inc(s4["Tv_sb"], 1)
                            act.wait_ge(s4["hid_ps"], new(i, u))
                            wait_old(act, s4["w_vv"], i, u)
                            nc.scalar.activation(hid[u][:], B(u, 2)[0:64, :], ACT.Silu, bias=V("b_fc1", 64)).then_inc(s4["hid_sb"], 1)
                        if k == 5:
                            wait_old_sums(act, s4["agg_ps"], i, u)
                            act.wait_ge(s4["msg_ps0"], new(i, u))
                            nc.scalar.activation(msg[u][:, 0:2, :].rearrange("p t f -> p (t f)"), B(u, 1)[:, 0:2 * MSG], ACT.Copy).then_inc(s4["msg_sb0"], 1)
                            act.wait_ge(s4["msg_ps1"], new(i, u))
                            nc.scalar.activation(msg[u][:, 2:4, :].rearrange("p t f -> p (t f)"), B(u, 2)[:, 0:2 * MSG], ACT.Copy).then_inc(s4["msg_sb1"], 1)
                        if k == 6:
                            act.wait_ge(s4["N_s"], new(i, u))
                            wait_old(act, s4["self_ps"], i, u)
                            nc.scalar.activation(Ns[u][:], B(u, 3)[0:64, :], ACT.Copy).then_inc(s4["Ns_sb"], 1)
                            act.wait_ge(s4["N_v"], new(i, u))
                            nc.scalar.activation(Nv[u][:], B(u, 0)[0:96, :], ACT.Copy).then_inc(s4["Nv_sb"], 1)
                        if 7 <= k < 7 + TG:
                            t = k - 7
                            if t == 0:
                                wait_old(act, s4["o_sb"], i, u)
                            act.wait_ge(s4["agg_ps"], 8 * i + 4 * u + t + 2)
                            nc.scalar.activation(agg[u][:, t, :], B(u, 1 + t % 2)[:, 0:MSG], ACT.Copy).then_inc(s4["agg_sb"], 1)
                        if k == 11:
                            act.wait_ge(s4["o_sb"], new(i, u))
                            wait_old(act, s4["u_ready"], i, u)
                            nc.scalar.activation(gates[u][:], o_sb[u][:, :, 0:96], ACT.Silu).then_inc(s4["gates_sb"], 1)

                    act.wait_ge(primed_4, 1)
                    staggered(act, ITERS, 11, 16, step)

                @block.vector
                def _(dve):
                    v = nc.vector

                    def step(i, u, k):
                        if k == 2:
                            dve.wait_ge(ld4[u], 48 * i + 48)
                            wait_old_sums(dve, s4["agg_ps"], i, u)
                            wait_old(dve, s4["idx_ready"], i, u)
                            v.tensor_copy(dcol[u][:], dcol_i[u][:])
                            v.tensor_tensor(tidx_f[u][:], dcol_i[u][:, 1:], dnext[u][:], ALU.is_equal).then_inc(s4["dcol_sb"], 1)
                            dve.wait_ge(s4["dcol_sb"], new(i, u))
                            for t in range(TG):
                                line = dline[u][:, t * P:(t + 1) * P]
                                v.tensor_scalar(sel[u][:, t, :], line, dcol[u][:, t + 1:t + 2], None, ALU.is_equal)
                                last = v.tensor_scalar(sel_c[u][:, t, :], line, dcol[u][:, t:t + 1], V("last_row", P),
                                                       ALU.is_equal, ALU.mult)
                            last.then_inc(s4["sel_sb"], 1)
                        if k == 3:
                            dve.wait_ge(y4[u], 64 * i + 64)
                            dve.wait_ge(s4["xs_ps"], new(i, u))
                            wait_old(dve, s4["msg_ps1"], i, u)
                            v.tensor_tensor(m_s01[u][:], ybc[u][:, 0, :], B(u, 3)[:, :], ALU.mult).then_inc(s4["q_s01"], 1)
                            v.tensor_tensor(m_s23[u][:], ybc[u][:, 1, :], B(u, 3)[:, :], ALU.mult).then_inc(s4["q_s23"], 1)
                            dve.wait_ge(s4["xv_ps"], new(i, u))
                            v.tensor_tensor(m_vs[u][:], ybc[u][0:96, 2, :], B(u, 0)[0:96, :], ALU.mult).then_inc(s4["q_vs"], 1)
                            v.tensor_tensor(m_vv[u][:], ybc[u][0:96, 3, :], B(u, 0)[0:96, :], ALU.mult).then_inc(s4["q_vv"], 1)
                        if k == 4:
                            for bank, rows, wname, bias, m, q_ok, done in (
                                    (1, 128, "w_s01", "b_s01", m_s01, "q_s01", "m_s01"), (2, 128, "w_s23", "b_s23", m_s23, "q_s23", "m_s23"),
                                    (3, 96, "w_vs", "b_vs", m_vs, "q_vs", "m_vs"), (0, 96, "w_vv", "b_vv", m_vv, "q_vv", "m_vv")):
                                dve.wait_ge(s4[wname], new(i, u))
                                dve.wait_ge(s4[q_ok], new(i, u))
                                v.scalar_tensor_tensor(m[u][:], B(u, bank)[0:rows, :], V(bias, rows), m[u][:], ALU.add, ALU.mult
                                                       ).then_inc(s4[done], 1)
                        if k == 11:
                            dve.wait_ge(s4["self_ps"], new(i, u))
                            dve.wait_ge(s4["agg_sb"], 8 * i + 4 * u + 5)
                            wait_old(dve, s4["gates_sb"], i, u)
                            for n in range(2):
                                last = v.tensor_tensor(o_sb[u][:, 2 * n:2 * n + 2, :].rearrange("p t f -> p (t f)"),
                                                       agg[u][:, 2 * n:2 * n + 2, :].rearrange("p t f -> p (t f)"),
                                                       B(u, 3 if n == 0 else 0)[:, 0:2 * MSG], ALU.add)
                            last.then_inc(s4["o_sb"], 1)
                            dve.wait_ge(sc4[u], 64 * i + 16)
                            v.scalar_tensor_tensor(tidx[u][:], tidx_f[u][:], float(SKIP), dcol[u][:, 1:], ALU.mult, ALU.add
                                                   ).then_inc(s4["idx_ready"], 1)
                        if k == 13:
                            dve.wait_ge(s4["gates_sb"], new(i, u))
                            for n in range(2):
                                tt = slice(2 * n, 2 * n + 2)
                                last = v.tensor_tensor(gv[u][:, tt, :].rearrange("p t (k c) -> p t k c", c=3),
                                                       gates[u][:, tt, CS:96].unsqueeze(3).broadcast_to([P, 2, CV, 3]),
                                                       o_sb[u][:, tt, 96:192].rearrange("p t (c k) -> p t k c", c=3), ALU.mult)
                            last.then_inc(s4["gv_ready"], 1)
                            dve.wait_ge(xd4[u], 16 * i + 16)
                            v.scalar_tensor_tensor(uu[u][:, :, 0:CS], x1d[u][:, :, 0:CS], 2.0, gates[u][:, :, 0:CS], ALU.mult, ALU.add)
                            dve.wait_ge(s4["gv_ready"], new(i, u))
                            v.scalar_tensor_tensor(uu[u][:, :, CS:D], x1d[u][:, :, CS:D], 2.0, gv[u][:], ALU.mult, ALU.add
                                                   ).then_inc(s4["u_ready"], 1)
                            dve.wait_ge(s4["u_ready"], new(i, u))
                            for t in range(TG):
                                last = v.bn_stats(st[u][:, t, :], uu[u][:, t, :])
                            last.then_inc(s4["bn"], 1)
                            dve.wait_ge(s4["bn"], new(i, u))
                            dve.sem_inc(go, 1)
                            for t in range(TG):
                                last = v.bn_aggr(mv[u][:, t, :], st[u][:, t, :])
                            last.then_inc(s4["mv"], 1)
                            dve.wait_ge(s4["mv"], new(i, u))
                            v.tensor_scalar(q[u][:], mv[u][:, :, 1], EPS, None, ALU.add).then_inc(s4["q"], 1)
                        if k == 14:
                            dve.wait_ge(s4["rstd"], new(i, u))
                            dve.wait_ge(sc4[u], 64 * i + 16)
                            for t in range(TG):
                                last = v.tensor_scalar(od[u][:, t, :], uu[u][:, t, :], mv[u][:, t, 0:1], r[u][:, t:t + 1],
                                                       ALU.subtract, ALU.mult)
                            last.then_inc(s4["out_ready"], 1)

                    v.memset(agg[1][:], 0.0).then_inc(s4["prime"], 1)
                    dve.wait_ge(s4["prime"], 2)
                    dve.wait_ge(primed_4, 1)
                    staggered(dve, ITERS, 11, 16, step)


def pack_weights(np, w):
    a = np.zeros((P, WCOLS), np.float32)
    vec = np.zeros((P, len(VECS)), np.float32)

    def blk(name):
        c, r, n = COL[name]
        return a[:r, c:c + n]

    g0 = lambda n: np.asarray(w["L0_gnn_" + n])
    g1 = lambda n: np.asarray(w["L1_gnn_" + n])
    b = blk("msg_s")
    for j in range(2):
        b[:64, j::2] = g0("Ws_src")
        b[64:, j::2] = g0("Ws_dst")
    for c in range(3):
        blk("msg_v_src")[c::3, c::3] = g0("Wv_src")
        blk("msg_v_dst")[c::3, c::3] = g0("Wv_dst")
    wr = g0("W_rbf")
    ss, sv, vs, vv0, vv1 = wr[:, 0:64], wr[:, 64:128], wr[:, 128:160], wr[:, 160:192], wr[:, 192:224]
    blk("rbf_s")[1::5, 0::2] = ss
    blk("rbf_s")[0::5, 1::2] = sv
    for c in range(3):
        nxt, prv = (c + 1) % 3, (c + 2) % 3
        blk("rbf_vv0")[2 + c::5, c::3] = vv0
        blk("rbf_vs")[1::5, c::3] = vs
        blk("rbf_vv1_next")[2 + nxt::5, c::3] = vv1
        blk("rbf_vv1_prev")[2 + prv::5, c::3] = vv1
        blk("alpha_dotv")[c::3, :] = g0("W_alpha")[64:]
        blk("gate")[0::2, c::3] = g0("Wg")
        blk("val_v_sv")[1::2, c::3] = g0("Wv_val")[0:64]
        blk("val_v_vs")[c::3, c::3] = g0("Wv_val")[64:96]
        blk("val_v_next")[c::3, prv::3] = g0("Wv_val")[96:128]
        blk("val_v_prev")[c::3, nxt::3] = g0("Wv_val")[96:128]
        blk("out_dotv")[c::3, :] = g0("Ws_vlin")[64:]
        blk("out_vs")[c::3, c * 32:c * 32 + 32] = g0("Wv_vlin")[64:96]
        blk("out_next")[c::3, prv * 32:prv * 32 + 32] = g0("Wv_vlin")[96:128]
        blk("out_prev")[c::3, nxt * 32:nxt * 32 + 32] = g0("Wv_vlin")[96:128]
        blk("proj_v")[c * 32:c * 32 + 32, c::3] = g0("Wpv")
        blk("l1_xv")[c::3, c::3] = g1("W1_v")
        blk("fc2_vs")[:, c::3] = g1("fc_w2")[:, 128:160]
        blk("fc2_vv")[:, c::3] = g1("fc_w2")[:, 160:192]
        blk("l1_vs")[c::3, c * 32:c * 32 + 32] = g1("W2_v")[64:96]
        blk("l1_vv")[c::3, :] = g1("W2_s")[64:96]
        blk("self_v")[c::3, c * 32:c * 32 + 32] = g1("Wsc_v")
        for j in range(2):
            blk("val_dotv")[c::3, j::2] = g0("Ws_val")[64:]
        for name, v in (("gamma_v3", g0("gamma_v")), ("w2_vv0", g0("w2_vv0")), ("w2_vs", g0("w2_vs")),
                        ("w2_vv1", g0("w2_vv1")), ("b_vs", g1("fc_b2")[128:160]), ("b_vv", g1("fc_b2")[160:192])):
            vec[c:96:3, VCOL[name]] = v
    blk("alpha_s")[0::2, :] = g0("W_alpha")[:64]
    for j in range(2):
        blk("val_s")[0::2, j::2] = g0("Ws_val")[:64]
        blk("l1_xs")[:, j::2] = g1("W1_s")
        blk("fc2_s01")[:, j::2] = g1("fc_w2")[:, 64 * j:64 * j + 64]
        blk("fc2_s23")[:, j::2] = g1("fc_w2")[:, 64:128]
        blk("out_s23")[j::2, 32 * j:32 * j + 32] = g0("Wv_vlin")[0:64]
        blk("l1_s23")[j::2, 32 * j:32 * j + 32] = g1("W2_v")[0:64]
        vec[64 * j:64 * j + 64, VCOL["gamma_s2"]] = g0("gamma_s")
        vec[64 * j:64 * j + 64, VCOL["beta_s2"]] = g0("beta_s")
        vec[j::2, VCOL["w2_s01"]] = (g0("w2_ss"), g0("w2_sv"))[j]
        vec[j::2, VCOL["w2_s23"]] = g0("w2_sv")
        vec[j::2, VCOL["b_s01"]] = g1("fc_b2")[64 * j:64 * j + 64]
        vec[j::2, VCOL["b_s23"]] = g1("fc_b2")[64:128]
    for h in range(HEADS):
        blk("alpha_dot")[16 * h:16 * h + 16, h] = g0("alpha_dot")[0, h]
    blk("out_s01")[0::2, 0:64] = g0("Ws_vlin")[:64]
    blk("out_s01")[1::2, 64:96] = g0("Wv_vlin")[0:64]
    blk("proj_s")[:] = g0("Wps")
    blk("fc1")[:] = g1("fc_w1")
    blk("l1_s01")[0::2, 0:96] = g1("W2_s")[:64]
    blk("l1_s01")[1::2, 96:128] = g1("W2_v")[0:64]
    blk("self_s")[:] = g1("Wsc_s")
    vec[:64, VCOL["b_fc1"]] = g1("fc_b1")
    vec[P - 1, VCOL["last_row"]] = 1.0
    return a, vec


def kernel(**inputs):
    import numpy as np
    import concourse.bacc as bacc
    from concourse import mybir as mb
    from concourse.bass_utils import run_bass_kernel_spmd as run

    def padded(a, n, fill):
        a = np.asarray(a)
        return np.concatenate([a, np.full((n - a.shape[0],) + a.shape[1:], fill, a.dtype)])

    def tiles(a):
        return np.ascontiguousarray(a.reshape(GROUPS, TG, P).transpose(0, 2, 1))

    src = padded(inputs["src"], EP, 0)
    dst = padded(inputs["dst"], EP, NP - 1)
    before = tiles(np.concatenate([np.full(P, -1, np.int32), dst[:-P]]))
    after = np.concatenate([dst[1:], np.full(1, NP, np.int32)])
    dst_t = tiles(dst)
    dst_cols = np.concatenate([before[:, :, 0:1], dst_t], axis=2)
    rows = np.zeros((EROWS, EP + CHUNK), np.float32)
    y = np.asarray(inputs["edge_attr_4"]).T
    rows[ONE] = 1.0
    rows[Y0:Y0 + 4, :EDGES] = y
    rows[YX + 3:YX + 5, :EDGES] = y[1:3]
    rows[RBF:RBF + 16, :EDGES] = np.asarray(inputs["edge_attr_16"]).T
    rows[EMB:EMB + 8, :EDGES] = np.asarray(inputs["edge_attr_8"]).T
    weights, vectors = pack_weights(np, inputs)
    head_mask = np.zeros((1, SEG), np.float32)
    head_mask[0, ::ITERS] = -BIG
    arrays = {
        "x": padded(inputs["x"], NP, 0), "src_idx": padded(tiles(src), GROUPS + 2, 0), "dst_idx": padded(dst_t, GROUPS + 2, 0),
        "dst_cols": np.ascontiguousarray(dst_cols),
        "dst_next": tiles(after),
        "dst_line": dst.reshape(ITERS, CHUNK), "edge_rows": rows,
        "records": padded(np.concatenate([inputs[n] for n in ("edge_attr_4", "edge_attr_16", "edge_attr_8")], axis=1), EP, 0),
        "edge_ids": np.stack([src, dst], axis=1), "dst_grid": np.ascontiguousarray(dst.reshape(TILES, P).T),
        "next_grid": np.ascontiguousarray(after.reshape(TILES, P).T), "before_mask": np.tril(np.ones((P, P), np.float32), -1),
        "weights": weights, "vectors": vectors,
        "ident": np.eye(P, dtype=np.float32), "head_mask": head_mask,
    }
    nc = bacc.Bacc("TRN2", target_bir_lowering=False, num_devices=1)
    args, given, named = [], {}, {}
    for name, a in arrays.items():
        named[f"in_{name}"] = a
        ap = nc.dram_tensor(f"in_{name}", a.shape, mb.dt.from_np(a.dtype), kind="ExternalInput").ap()
        if name in ("src_idx", "dst_idx", "dst_cols", "dst_next", "dst_line", "edge_rows"):
            given[name] = ap
        else:
            args.append(ap)
    out = nc.dram_tensor("out_rows", (NP, D), F32, kind="ExternalOutput").ap()
    build(nc, args[0], given, *args[1:], out)
    r = run(nc, [named], core_ids=[0])
    return r.results[0]["out_rows"][:NODES]
```
